# Optimizing a Trainium2 kernel written in Bass

```python
import numpy as np
import jax
import jax.numpy as jnp

def _softmax(x, axis=-1):
    return jax.nn.softmax(x, axis=axis)

def _gelu(x):
    return jax.nn.gelu(x, approximate=True)

def _silu(x):
    return jax.nn.silu(x)

def _sigmoid(x):
    return jax.nn.sigmoid(x)

def _layernorm(x, axis=-1, eps=1e-05):
    m = jnp.mean(x, axis=axis, keepdims=True)
    v = jnp.var(x, axis=axis, keepdims=True)
    return (x - m) / jnp.sqrt(v + eps)

def _scatter_add(tgt, idx, src, axis=0):
    return tgt.at[idx].add(src)

def _segment_sum(src, seg, n):
    return jax.ops.segment_sum(src, seg, n)
kernel_name = 'mk_adj_ffn_d1_adj_r2_23b90b'

def setup_inputs(seed: int=0):
    np.random.seed(seed)
    _w = jnp.asarray

    def _rec_inputs():
        import jax
        import jax.numpy as jnp
        _gk = jax.random.key(seed)
        x = -0.000929 + 1 * jax.random.normal(jax.random.fold_in(_gk, 1), (3327, 128), jnp.float32)
        _a = jax.random.bernoulli(jax.random.fold_in(_gk, 2), 0.00120228, (3327, 3327))
        _a = jnp.logical_or(_a, jnp.eye(3327, dtype=bool))
        _af = _a.astype(jnp.float32)
        _af = _af * jax.random.uniform(jax.random.fold_in(_gk, 3), (3327, 3327), jnp.float32, 0.05, 1)
        adj = _af
        return (x, adj)
    x, adj = _rec_inputs()

    def _L0_gnn_setup():
        import jax, jax.numpy as jnp
        import numpy as np
        N, H, HEADS = (2048, 128, 3)
        ALPHA = 0.2
        NEG_INF = -9000000000000000.0

        def _sign_adj(key, n, density):
            k1, k2 = jax.random.split(key)
            mask = jax.random.uniform(k1, (n, n)) < density
            sign = jnp.where(jax.random.uniform(k2, (n, n)) < 0.5, -1.0, 1.0)
            adj = jnp.where(mask, sign, 0.0).astype(jnp.float32)
            idx = jnp.arange(n)
            return adj.at[idx, idx].set(1.0)

        def _gru_cell(x, hstate, Wih, Whh, bih, bhh):
            gi = x @ Wih.T + bih
            gh = hstate @ Whh.T + bhh
            ir, iz, inn = jnp.split(gi, 3, axis=1)
            hr, hz, hn = jnp.split(gh, 3, axis=1)
            r = jax.nn.sigmoid(ir + hr)
            z = jax.nn.sigmoid(iz + hz)
            n = jnp.tanh(inn + r * hn)
            return (1.0 - z) * n + z * hstate

        def _gat_head(h, node_adj, edge_adj, W, a):
            hW = h @ W
            hp = (node_adj > 0).astype(hW.dtype) @ hW
            hm = (node_adj < 0).astype(hW.dtype) @ hW
            e_plus = jax.nn.leaky_relu(jnp.concatenate([hp, hm], axis=1) @ a, ALPHA)[:, 0]
            e_minus = jax.nn.leaky_relu(jnp.concatenate([hm, hp], axis=1) @ a, ALPHA)[:, 0]
            att = jnp.where(edge_adj > 0, e_plus[None, :], NEG_INF)
            att = jnp.where(edge_adj < 0, e_minus[None, :], att)
            att = jax.nn.softmax(att, axis=1)
            return att * edge_adj @ hW
        key = jax.random.key(seed)
        ks = jax.random.split(key, 16)
        std = 0.01
        gain = 1.414
        return {'h': jax.random.normal(ks[0], (N, H), jnp.float32), 'node_adj': _sign_adj(ks[1], N, 0.005), 'edge_adj': _sign_adj(ks[2], N, 0.005), 'gat_W': jax.random.normal(ks[3], (HEADS, H, H), jnp.float32) * (gain / np.sqrt(H, dtype=np.float32)), 'gat_a': jax.random.normal(ks[4], (HEADS, 2 * H, 1), jnp.float32) * 0.1, 'edge_Wih': jax.random.normal(ks[5], (3 * H, H), jnp.float32) * std, 'edge_Whh': jax.random.normal(ks[6], (3 * H, H), jnp.float32) * std, 'edge_bih': jnp.zeros((3 * H,), jnp.float32), 'edge_bhh': jnp.zeros((3 * H,), jnp.float32), 'node_Wih': jax.random.normal(ks[7], (3 * H, H), jnp.float32) * std, 'node_Whh': jax.random.normal(ks[8], (3 * H, H), jnp.float32) * std, 'node_bih': jnp.zeros((3 * H,), jnp.float32), 'node_bhh': jnp.zeros((3 * H,), jnp.float32)}
    _L0_gnn_all = _L0_gnn_setup()
    _L0_gnn_in = {k: v for k, v in _L0_gnn_all.items() if k in ('gat_W', 'gat_a', 'edge_Wih', 'edge_Whh', 'edge_bih', 'edge_bhh', 'node_Wih', 'node_Whh', 'node_bih', 'node_bhh')}
    del _L0_gnn_all

    def _L0_ffn_setup():
        import jax, jax.numpy as jnp
        import numpy as np
        TOP_K = 2
        LN_EPS = 1e-05
        key = jax.random.key(seed)
        ks = jax.random.split(key, 8)
        B, S, D, E, H = (16, 512, 128, 8, 512)
        x = jax.random.normal(ks[0], (B, S, D), dtype=jnp.float32)
        Wr = jax.random.normal(ks[1], (D, E), dtype=jnp.float32) * 0.1
        br = jnp.zeros((E,), dtype=jnp.float32)
        ln_g = jnp.ones((E, D), dtype=jnp.float32)
        ln_b = jnp.zeros((E, D), dtype=jnp.float32)
        W1 = jax.random.normal(ks[2], (E, D, H), dtype=jnp.float32) * (1.0 / np.sqrt(D))
        b1 = jnp.zeros((E, H), dtype=jnp.float32)
        W2 = jax.random.normal(ks[3], (E, H, D), dtype=jnp.float32) * (1.0 / np.sqrt(H))
        b2 = jnp.zeros((E, D), dtype=jnp.float32)
        return {'x': x, 'Wr': Wr, 'br': br, 'ln_g': ln_g, 'ln_b': ln_b, 'W1': W1, 'b1': b1, 'W2': W2, 'b2': b2}
    _L0_ffn_all = _L0_ffn_setup()
    _L0_ffn_in = {k: v for k, v in _L0_ffn_all.items() if k in ('Wr', 'br', 'ln_g', 'ln_b', 'W1', 'b1', 'W2', 'b2')}
    del _L0_ffn_all
    return {'x': x, 'adj': adj, 'L0_gnn_gat_W': _L0_gnn_in['gat_W'], 'L0_gnn_gat_a': _L0_gnn_in['gat_a'], 'L0_gnn_edge_Wih': _L0_gnn_in['edge_Wih'], 'L0_gnn_edge_Whh': _L0_gnn_in['edge_Whh'], 'L0_gnn_edge_bih': _L0_gnn_in['edge_bih'], 'L0_gnn_edge_bhh': _L0_gnn_in['edge_bhh'], 'L0_gnn_node_Wih': _L0_gnn_in['node_Wih'], 'L0_gnn_node_Whh': _L0_gnn_in['node_Whh'], 'L0_gnn_node_bih': _L0_gnn_in['node_bih'], 'L0_gnn_node_bhh': _L0_gnn_in['node_bhh'], 'L0_ffn_Wr': _L0_ffn_in['Wr'], 'L0_ffn_br': _L0_ffn_in['br'], 'L0_ffn_ln_g': _L0_ffn_in['ln_g'], 'L0_ffn_ln_b': _L0_ffn_in['ln_b'], 'L0_ffn_W1': _L0_ffn_in['W1'], 'L0_ffn_b1': _L0_ffn_in['b1'], 'L0_ffn_W2': _L0_ffn_in['W2'], 'L0_ffn_b2': _L0_ffn_in['b2']}

def reference(x, adj, L0_gnn_gat_W, L0_gnn_gat_a, L0_gnn_edge_Wih, L0_gnn_edge_Whh, L0_gnn_edge_bih, L0_gnn_edge_bhh, L0_gnn_node_Wih, L0_gnn_node_Whh, L0_gnn_node_bih, L0_gnn_node_bhh, L0_ffn_Wr, L0_ffn_br, L0_ffn_ln_g, L0_ffn_ln_b, L0_ffn_W1, L0_ffn_b1, L0_ffn_W2, L0_ffn_b2):
    import jax
    import jax.numpy as jnp

    def _L0_gnn_ref(h, node_adj, edge_adj, gat_W, gat_a, edge_Wih, edge_Whh, edge_bih, edge_bhh, node_Wih, node_Whh, node_bih, node_bhh):
        import jax, jax.numpy as jnp
        import numpy as np
        N, H, HEADS = (2048, 128, 3)
        ALPHA = 0.2
        NEG_INF = -9000000000000000.0

        def _sign_adj(key, n, density):
            k1, k2 = jax.random.split(key)
            mask = jax.random.uniform(k1, (n, n)) < density
            sign = jnp.where(jax.random.uniform(k2, (n, n)) < 0.5, -1.0, 1.0)
            adj = jnp.where(mask, sign, 0.0).astype(jnp.float32)
            idx = jnp.arange(n)
            return adj.at[idx, idx].set(1.0)

        def _gru_cell(x, hstate, Wih, Whh, bih, bhh):
            gi = x @ Wih.T + bih
            gh = hstate @ Whh.T + bhh
            ir, iz, inn = jnp.split(gi, 3, axis=1)
            hr, hz, hn = jnp.split(gh, 3, axis=1)
            r = jax.nn.sigmoid(ir + hr)
            z = jax.nn.sigmoid(iz + hz)
            n = jnp.tanh(inn + r * hn)
            return (1.0 - z) * n + z * hstate

        def _gat_head(h, node_adj, edge_adj, W, a):
            hW = h @ W
            hp = (node_adj > 0).astype(hW.dtype) @ hW
            hm = (node_adj < 0).astype(hW.dtype) @ hW
            e_plus = jax.nn.leaky_relu(jnp.concatenate([hp, hm], axis=1) @ a, ALPHA)[:, 0]
            e_minus = jax.nn.leaky_relu(jnp.concatenate([hm, hp], axis=1) @ a, ALPHA)[:, 0]
            att = jnp.where(edge_adj > 0, e_plus[None, :], NEG_INF)
            att = jnp.where(edge_adj < 0, e_minus[None, :], att)
            att = jax.nn.softmax(att, axis=1)
            return att * edge_adj @ hW
        dn = jnp.diag(node_adj)
        de = jnp.diag(edge_adj)
        idx = jnp.arange(node_adj.shape[0])
        node_adj_norm = node_adj.at[idx, idx].add(-dn)
        edge_adj_norm = edge_adj.at[idx, idx].add(-de)
        node_support = node_adj_norm @ h
        edge_output = _gru_cell(node_support, h, edge_Wih, edge_Whh, edge_bih, edge_bhh)
        edge_support = _gat_head(h, node_adj_norm, edge_adj_norm, gat_W[0], gat_a[0])
        for i in range(1, HEADS):
            edge_support = edge_support + _gat_head(h, node_adj_norm, edge_adj_norm, gat_W[i], gat_a[i])
        edge_support = edge_support / HEADS
        node_output = _gru_cell(edge_support, h, node_Wih, node_Whh, node_bih, node_bhh)
        return de[:, None] * edge_output + dn[:, None] * node_output

    def _L0_ffn_ref(x, Wr, br, ln_g, ln_b, W1, b1, W2, b2):
        import jax, jax.numpy as jnp
        import numpy as np
        TOP_K = 2
        LN_EPS = 1e-05
        B, S, D = x.shape
        N = B * S
        xt = x.reshape(N, D)
        logits = xt @ Wr + br
        probs = jax.nn.softmax(logits, axis=-1)
        top_p, top_idx = jax.lax.top_k(probs, TOP_K)
        weights = top_p / top_p.sum(axis=-1, keepdims=True)
        mu = xt.mean(axis=-1, keepdims=True)
        var = ((xt - mu) ** 2).mean(axis=-1, keepdims=True)
        xn = (xt - mu) * jax.lax.rsqrt(var + LN_EPS)
        xe = xn[None, :, :] * ln_g[:, None, :] + ln_b[:, None, :]
        h = jax.nn.gelu(jnp.einsum('end,edh->enh', xe, W1) + b1[:, None, :], approximate=False)
        y = jnp.einsum('enh,ehd->end', h, W2) + b2[:, None, :]
        y_tok = jnp.transpose(y, (1, 0, 2))
        sel = jnp.take_along_axis(y_tok, top_idx[:, :, None], axis=1)
        out = (weights[:, :, None] * sel).sum(axis=1)
        return out.reshape(B, S, D)
    x = x + _L0_gnn_ref(_layernorm(x, axis=-1), adj, adj, L0_gnn_gat_W, L0_gnn_gat_a, L0_gnn_edge_Wih, L0_gnn_edge_Whh, L0_gnn_edge_bih, L0_gnn_edge_bhh, L0_gnn_node_Wih, L0_gnn_node_Whh, L0_gnn_node_bih, L0_gnn_node_bhh)
    x = x + _L0_ffn_ref(_layernorm(x, axis=-1)[None], L0_ffn_Wr, L0_ffn_br, L0_ffn_ln_g, L0_ffn_ln_b, L0_ffn_W1, L0_ffn_b1, L0_ffn_W2, L0_ffn_b2)[0]
    return x

_drawn_inputs = setup_inputs


def setup_inputs(seed=0):
    import zlib

    import numpy as np

    out = dict(_drawn_inputs(seed))
    spreads = {'L0_gnn_edge_bih': (0.0, 0.1),
     'L0_gnn_edge_bhh': (0.0, 0.282),
     'L0_gnn_node_bih': (0.0, 0.1),
     'L0_gnn_node_bhh': (0.0, 0.307),
     'L0_ffn_br': (0.0, 0.1),
     'L0_ffn_ln_g': (1.0, 0.2),
     'L0_ffn_ln_b': (0.0, 0.1),
     'L0_ffn_b1': (0.0, 0.1),
     'L0_ffn_b2': (0.0, 0.1)}
    factors = {'L0_gnn_gat_W': 2.87, 'L0_gnn_gat_a': 3.937, 'L0_gnn_node_Wih': 2.882}
    for name, (base, spread) in spreads.items():
        noise = np.random.default_rng([zlib.crc32(name.encode()), seed]).standard_normal(out[name].shape)
        drawn = base * np.exp(spread * noise) if base else spread * noise
        out[name] = jnp.asarray(drawn.astype(out[name].dtype))
    for name, factor in factors.items():
        out[name] = (out[name] * factor).astype(out[name].dtype)
    return out
```

```python
from contextlib import ExitStack

import concourse.bass as bass
from concourse import mybir

F32 = mybir.dt.float32
BF16 = mybir.dt.bfloat16
U32 = mybir.dt.uint32
I32 = mybir.dt.int32
ALU = mybir.AluOpType
ACT = mybir.ActivationFunctionType
AX = mybir.AxisListType

P = 128
NODES = 3327
TILES = (NODES + P - 1) // P
ROWS = TILES * P
PAD = ROWS - 1
D = 128
HEADS = 3
ALPHA = 0.2
NEG_INF = -9000000000000000.0
EPS = 1e-05
U = 2 * HEADS
PARTS = 3
TW = D + 2 * HEADS + 2
SEG = 4
QUAD = 32
SEG_FIRST = [0, 7, 14, 20, 26]
SEG_COLS = 7 * P
SEG_CAP = P + QUAD
CHUNKS = SEG_CAP * SEG // P
SLOTS = CHUNKS * P
ROUNDS = SEG_CAP // 8
UCOLS = PARTS * U + 1
BUFS = 4
LOOPED = TILES // BUFS * BUFS
ZC = HEADS * SLOTS
GB = 416
GBLOCKS = ROWS // GB
EXPERTS = 8
HID = 512
HC = HID // P
MB = 256
MBLOCKS = ROWS // MB
MT = MB // P


class Chain:

    def __init__(self, eng, sem):
        self.eng, self.sem, self.base, self.n, self.turn, self.per = eng, sem, 0, 0, None, 0

    def loop(self, turn, per):
        self.base, self.n, self.turn, self.per = self.base + self.n, 0, turn, per

    def done(self, turns):
        assert self.n == self.per, (self.n, self.per)
        self.base, self.n, self.turn = self.base + turns * self.per, 0, None

    def link(self, ins):
        self.n += 1
        ins.then_inc(self.sem, 1)
        count = self.base + self.n
        if self.turn is not None:
            count = self.turn * self.per + count
        self.eng.wait_ge(self.sem, count)


def gnn_moe(nc, x, adjT, diag, gatW, gatWT, gata, gruw, grub, Wr, br, lng, lnb, W1, b1, W2, b2, out, dbg=None):
    adj_chunks = adjT.rearrange("(c p) r -> c p r", p=P)
    adj_rows = adjT.rearrange("c (t r) -> (c t) r", r=P)
    table = nc.dram_tensor("neighbour_table", (ROWS, TW), F32, kind="Internal").ap()

    with ExitStack() as ctx:
        def sb(name, shape, dt=F32):
            return ctx.enter_context(nc.sbuf_tensor(name, shape, dt))

        def sem(name):
            return ctx.enter_context(nc.semaphore(name))

        xs = sb("xs", [P, TILES, D])
        hT = sb("hT", [P, ROWS])
        tab = sb("tab", [P, TILES, TW])
        h = tab[:, :, 0:D]
        dg = sb("dg", [P, TILES])
        ident = sb("ident", [P, P])
        identb = sb("identb", [P, P], BF16)
        notid = sb("notid", [P, P])
        ones = sb("ones", [P, P])
        gatW_s = sb("gatW_s", [P, HEADS, D])
        gatWT_s = sb("gatWT_s", [P, HEADS, D])
        gata_s = sb("gata_s", [P, HEADS, 2])
        gruw_s = sb("gruw_s", [P, 4, 3 * D])
        grub_s = sb("grub_s", [P, 4, 3])
        gbias = sb("gbias", [P, 2, 2])
        Wr_s = sb("Wr_s", [P, EXPERTS])
        br_s = sb("br_s", [P, EXPERTS])
        lng_s = sb("lng_s", [P, EXPERTS])
        lnb_s = sb("lnb_s", [P, EXPERTS])
        W1_s = sb("W1_s", [P, EXPERTS, HID])
        b1_s = sb("b1_s", [P, EXPERTS, HC])
        W2_s = sb("W2_s", [P, EXPERTS * HC, D])
        b2_s = sb("b2_s", [EXPERTS, D])
        region = sb("region", [P, 4 * ROWS])
        masks = region[:, 2 * ROWS:4 * ROWS].bitcast(BF16)
        pos = [masks[:, b * ROWS:(b + 1) * ROWS] for b in range(2)]
        sgn = [masks[:, (2 + b) * ROWS:(3 + b) * ROWS] for b in range(2)]
        num = region[:, :].rearrange("p (q r) -> p q r", q=4)
        WORK = 13312
        work = sb("work", [P, WORK])
        at = [region[:, b * ROWS:(b + 1) * ROWS] for b in range(2)] + [
            work[:, (1 + b) * ROWS:(2 + b) * ROWS] for b in range(2)]
        anyw = work[:, 0:TILES * (64 + 32 + 16) // 2].bitcast(BF16)
        gts = sb("gts", [P, BUFS, CHUNKS, TW])
        at_in = [sem(f"at_in{b}") for b in range(BUFS)]
        stat = sb("stat", [P, 6, TILES])
        V = sb("V", [P, U])
        u32_ = sb("u_f", [P, TILES, U])
        urest = sb("u_rest", [P, TILES, U])
        uparts = sb("u_parts", [P, TILES, UCOLS], BF16)
        anyc = sb("anyc", [P, TILES, TILES])
        cidx = sb("cidx", [P, TILES, CHUNKS])
        crel = sb("crel", [P, TILES, CHUNKS])
        idx_tab = sb("idx_tab", [P, TILES, CHUNKS], U32)
        idx_adj = sb("idx_adj", [P, TILES, CHUNKS], U32)
        coliota = sb("coliota", [P, P])
        flag = sb("flag", [1, 1], I32)
        zeros = sb("zeros", [P, 512], BF16)

        with ExitStack() as c1:
            def ps(name, shape, dt=F32):
                return c1.enter_context(nc.psum_tensor(name, shape, dt))

            def sem1(name):
                return c1.enter_context(nc.semaphore(name))

            psT = [ps(f"psT{k}", [P, 512]) for k in range(2)]
            psU = ps("psU", [P, TILES, U])
            psV = ps("psV", [P, U])
            x_in, w_in, gw_in = sem1("x_in"), sem1("w_in"), sem1("gw_in")
            consts, dve_c, centred, squared = sem1("consts"), sem1("dve_c1"), sem1("centred"), sem1("squared")
            vared, stdev, h_ready = sem1("vared"), sem1("stdev"), sem1("h_ready")
            group_T, hT_ready, V_ps, V_ready, u_ps = (sem1("group_T"), sem1("hT_ready"), sem1("V_ps"), sem1("V_ready"),
                                                      sem1("u_ps"))
            iotas = sem1("iotas1")
            groups = [(t, min(4, TILES - t)) for t in range(0, TILES, 4)]
            sq = work[:, 0:ROWS].rearrange("p (t d) -> p t d", t=TILES)
            with nc.Block() as block:
                @block.sync
                def _(sp):
                    sp.dma_start(xs[:], x.rearrange("(t p) d -> p t d", p=P)).then_inc(x_in, 16)
                    sp.dma_start(gatWT_s[:], gatWT).then_inc(gw_in, 16)
                    sp.dma_start(gata_s[:], gata).then_inc(gw_in, 16)
                    for dst, src in ((dg, diag), (gatW_s, gatW), (gruw_s, gruw), (grub_s, grub), (Wr_s, Wr),
                                     (lng_s, lng), (lnb_s, lnb), (W1_s, W1), (b1_s, b1), (W2_s, W2), (b2_s, b2)):
                        sp.dma_start(dst[:], src).then_inc(w_in, 16)
                    sp.dma_start(br_s[:], br.partition_broadcast(P)).then_inc(w_in, 16)
                    for b in range(BUFS):
                        sp.dma_start(at[b], adj_chunks[b, :, :]).then_inc(at_in[b], 16)
                    sp.wait_ge(w_in, 16 * 12)

                @block.gpsimd
                def _(pool):
                    pool.memset(ident[:], 0.0).then_inc(iotas, 1)
                    pool.memset(identb[:], 0.0).then_inc(iotas, 1)
                    pool.memset(notid[:], 1.0).then_inc(iotas, 1)
                    pool.wait_ge(iotas, 3)
                    for tile, fill in ((ident, 1.0), (identb, 1.0), (notid, 0.0)):
                        pool.affine_select(out=tile[:], in_=tile[:], compare_op=ALU.not_equal, fill=fill, base=0,
                                           pattern=[[-1, P]], channel_multiplier=1).then_inc(consts, 1)
                    pool.memset(ones[:], 1.0).then_inc(consts, 1)
                    pool.memset(zeros[:], 0.0).then_inc(consts, 1)
                    pool.memset(tab[:, :, D:TW], 0.0).then_inc(consts, 1)
                    pool.memset(uparts[:, :, PARTS * U:UCOLS], 1.0).then_inc(consts, 1)
                    pool.iota(coliota[:], pattern=[[1, P]], base=0, channel_multiplier=0,
                              allow_small_or_imprecise_dtypes=True).then_inc(consts, 1)

                @block.vector
                def _(dve):
                    ch = Chain(dve, dve_c)
                    dve.wait_ge(x_in, 16)
                    ch.link(dve.tensor_reduce(out=stat[:, 0, :], in_=xs[:], axis=AX.X, op=ALU.add))
                    ch.link(dve.tensor_scalar(stat[:, 1, :], stat[:, 0, :], 1.0 / D, None, ALU.mult))
                    dve.tensor_tensor(out=h, in0=xs[:], in1=stat[:, 1, :].unsqueeze(2).to_broadcast([P, TILES, D]),
                                      op=ALU.subtract).then_inc(centred, 1)
                    dve.wait_ge(squared, 1)
                    ch.link(dve.tensor_reduce(out=stat[:, 2, :], in_=sq, axis=AX.X, op=ALU.add))
                    dve.tensor_scalar(stat[:, 3, :], stat[:, 2, :], 1.0 / D, EPS, ALU.mult, ALU.add).then_inc(vared, 1)
                    dve.wait_ge(stdev, 1)
                    ch.link(dve.reciprocal(stat[:, 5, :], stat[:, 4, :]))
                    dve.tensor_tensor(out=h, in0=h, in1=stat[:, 5, :].unsqueeze(2).to_broadcast([P, TILES, D]),
                                      op=ALU.mult).then_inc(h_ready, 1)
                    dve.wait_ge(V_ps, 1)
                    dve.tensor_copy(V[:], psV[:]).then_inc(V_ready, 1)
                    dve.wait_ge(u_ps, 1)
                    ch.link(dve.tensor_copy(u32_[:], psU[:]))
                    src = u32_
                    for k in range(PARTS):
                        part = uparts[:, :, k * U:(k + 1) * U]
                        ch.link(dve.tensor_copy(part, src[:]))
                        if k < PARTS - 1:
                            ch.link(dve.tensor_tensor(out=urest[:], in0=src[:], in1=part, op=ALU.subtract))
                            src = urest

                @block.scalar
                def _(act):
                    act.wait_ge(centred, 1)
                    act.activation(sq, h, ACT.Square).then_inc(squared, 1)
                    act.wait_ge(vared, 1)
                    act.activation(stat[:, 4, :], stat[:, 3, :], ACT.Sqrt).then_inc(stdev, 1)
                    for g, (t0, n) in enumerate(groups):
                        act.wait_ge(group_T, g + 1)
                        act.copy(hT[:, t0 * P:(t0 + n) * P], psT[g % 2][:, 0:n * P]).then_inc(hT_ready, 1)

                @block.tensor
                def _(pe):
                    pe.wait_ge(consts, 8)
                    pe.wait_ge(gw_in, 32)
                    for i in range(HEADS):
                        last = pe.matmul(psV[:, 2 * i:2 * i + 2], gatWT_s[:, i, :], gata_s[:, i, :], start=True,
                                         stop=True)
                    last.then_inc(V_ps, 1)
                    pe.wait_ge(h_ready, 1)
                    for g, (t0, n) in enumerate(groups):
                        if g >= 2:
                            pe.wait_ge(hT_ready, g - 1)
                        for t in range(n):
                            last = pe.transpose(psT[g % 2][:, t * P:(t + 1) * P], tab[:, t0 + t, 0:D], ident[:])
                        last.then_inc(group_T, 1)
                    pe.wait_ge(V_ready, 1)
                    pe.wait_ge(hT_ready, len(groups))
                    for t in range(TILES):
                        last = pe.matmul(psU[:, t, :], hT[:, t * P:(t + 1) * P], V[:], start=True, stop=True)
                    last.then_inc(u_ps, 1)

        with ExitStack() as c2:
            def ps(name, shape, dt=F32):
                return c2.enter_context(nc.psum_tensor(name, shape, dt))

            def sem2(name):
                return c2.enter_context(nc.semaphore(name))

            psP = ps("psP", [P, TILES, UCOLS])
            psS = ps("psS", [P, TILES, UCOLS])
            undiag, pos_ready, sgn_ready, any_done, pe_used, tree = (
                sem2("undiag"), sem2("pos_ready"), sem2("sgn_ready"), sem2("any_done"), sem2("pe_used"), sem2("tree"))
            TREE = 3
            with nc.Block() as block:
                def over_chunks(eng, step):
                    with eng.Fori(0, LOOPED // BUFS) as i:
                        for b in range(BUFS):
                            step(i * BUFS + b, b)
                    for c in range(LOOPED, TILES):
                        step(c, c - LOOPED)

                @block.sync
                def _(sp):
                    def load(c, b):
                        sp.wait_ge(pos_ready, c + 1)
                        sp.wait_ge(sgn_ready, c + 1)
                        src = adj_chunks[c + BUFS:c + BUFS + 1, :, :] if isinstance(c, int) else \
                            adj_chunks[bass.ds(c + BUFS, 1), :, :]
                        sp.dma_start(at[b], src.rearrange("o p r -> p (o r)")).then_inc(at_in[b], 16)

                    with sp.Fori(0, LOOPED // BUFS - 1) as i:
                        for b in range(BUFS):
                            load(i * BUFS + b, b)
                    for c in range(LOOPED - BUFS, TILES - BUFS):
                        load(c, c % BUFS)

                @block.gpsimd
                def _(pool):
                    def step(c, b):
                        turn = c // BUFS if isinstance(c, int) else None
                        if turn is None:
                            pool.wait_ge(at_in[b], (c - b) * (16 // BUFS) + 16)
                        else:
                            pool.wait_ge(at_in[b], 16 * turn + 16)
                        dblock = at[b][:, bass.ds(c * P, P)]
                        pool.tensor_tensor(out=dblock, in0=dblock, in1=notid[:], op=ALU.mult).then_inc(undiag, 1)

                    over_chunks(pool, step)

                @block.vector
                def _(dve):
                    def step(c, b):
                        dve.wait_ge(undiag, c + 1)
                        dve.wait_ge(pe_used, c + 1)
                        dve.tensor_scalar(pos[b % 2], at[b], 0.0, None, ALU.is_gt).then_inc(pos_ready, 1)
                        dve.wait_ge(pos_ready, c + 1)
                        src, w, o = pos[b % 2].rearrange("p (t r) -> p t r", r=P), P, 0
                        for k in range(TREE):
                            w //= 2
                            dst = anyw[:, o:o + TILES * w].rearrange("p (t r) -> p t r", r=w)
                            o += TILES * w
                            dve.tensor_tensor(out=dst, in0=src[:, :, 0:w], in1=src[:, :, w:2 * w],
                                              op=ALU.max).then_inc(tree, 1)
                            dve.wait_ge(tree, c * TREE + k + 1)
                            src = dst
                        dve.tensor_reduce(out=anyc[:, bass.ds(c, 1), :].rearrange("p o t -> p (o t)"), in_=src,
                                          axis=AX.X, op=ALU.max).then_inc(any_done, 1)

                    over_chunks(dve, step)

                @block.scalar
                def _(act):
                    def step(c, b):
                        act.wait_ge(undiag, c + 1)
                        act.wait_ge(pe_used, c + 1)
                        act.activation(sgn[b % 2], at[b], ACT.Sign).then_inc(sgn_ready, 1)

                    over_chunks(act, step)

                @block.tensor
                def _(pe):
                    for bank in (psP, psS):
                        pe.matmul(bank[:].rearrange("p t u -> p (t u)"), zeros[:, 0:P], zeros[:, 0:TILES * UCOLS],
                                  start=True, stop=False, skip_group_check=True)
                    pe.sem_inc(pe_used, 2)

                    def step(c, b):
                        parts = uparts[:, bass.ds(c, 1), :].rearrange("p o u -> p (o u)")
                        for bank, mask, ready in ((psP, pos, pos_ready), (psS, sgn, sgn_ready)):
                            pe.wait_ge(ready, c + 1)
                            for t in range(TILES):
                                last = pe.matmul(bank[:, t, :], mask[b % 2][:, t * P:(t + 1) * P], parts,
                                                 start=False, stop=False, skip_group_check=True)
                        last.then_inc(pe_used, 1)

                    over_chunks(pe, step)

            psK = ps("psK", [P, 2 * 512])
            psI = ps("psI", [P, SEG_CAP])
            psF = ps("psF", [1, 1])
            pneg = work[:, 0:3 * TILES * U].rearrange("p (k t u) -> p k t u", k=3, t=TILES)
            counts = work[:, 470:470 + TILES]
            counts2 = work[:, 496:496 + 1]
            anyb = work[:, 512:512 + TILES * QUAD // 2].bitcast(BF16).rearrange("p (c q) -> p c q", q=QUAD)
            keys = work[:, 1024:1024 + SEG_COLS]
            keyiota = work[:, 2048:2048 + SEG_COLS]
            top = work[:, 3072:3072 + SEG_CAP]
            lists = work[:, 3328:3328 + SEG_CAP]
            padz = work[:, 3584:3584 + SEG_CAP]
            left = work[:, 3840:3848]
            segb = work[:, 3848:3850]
            leftf = work[:, 3850:3851]
            tileiota = work[:, 3900:3900 + TILES * CHUNKS].rearrange("p (t k) -> p t k", k=CHUNKS)
            scaled = work[:, 4100:4100 + TILES * CHUNKS].rearrange("p (t k) -> p t k", k=CHUNKS)
            made, dve_c, any_t, keys_ps, lists_ready, lists_ps, e_ready, stored, over, over_ps = (
                sem2("made"), sem2("dve_c3"), sem2("any_t"), sem2("keys_ps"), sem2("lists_ready"), sem2("lists_ps"),
                sem2("e_ready"), sem2("stored"), sem2("over"), sem2("over_ps"))
            with nc.Block() as block:
                @block.sync
                def _(sp):
                    sp.wait_ge(e_ready, 1)
                    sp.dma_start(table.rearrange("(t p) w -> p t w", p=P), tab[:]).then_inc(stored, 16)
                    sp.wait_ge(stored, 16)

                @block.gpsimd
                def _(pool):
                    pool.iota(keyiota, pattern=[[1, SEG_COLS]], base=1, channel_multiplier=0,
                              allow_small_or_imprecise_dtypes=True).then_inc(made, 1)
                    pool.iota(tileiota, pattern=[[1, TILES], [0, CHUNKS]], base=0, channel_multiplier=0,
                              allow_small_or_imprecise_dtypes=True).then_inc(made, 1)

                @block.vector
                def _(dve):
                    ch = Chain(dve, dve_c)
                    dve.memset(anyb, 0.0)
                    for s in range(SEG):
                        q = slice(s * QUAD, (s + 1) * QUAD)
                        dve.memset(segb[q, 0:1], float(SEG_FIRST[s] * P - 1))
                        dve.memset(segb[q, 1:2], float(PAD + 1 - SEG_FIRST[s] * P))
                    ch.link(dve.memset(keys[64:P, 6 * P:7 * P], 0.0))
                    dve.tensor_scalar(anyb[:, :, 0:TILES], anyc[:], 0.0, None, ALU.is_gt).then_inc(any_t, 1)
                    by_part = "p t (k u) -> p t u k"
                    for k, bank in enumerate((psP, psS)):
                        ch.link(dve.tensor_reduce(out=pneg[:, k], in_=bank[:, :, 0:PARTS * U].rearrange(
                            by_part, k=PARTS), axis=AX.X, op=ALU.add))
                    ch.link(dve.tensor_copy(counts.unsqueeze(2), psP[:, :, PARTS * U:UCOLS]))
                    ch.link(dve.tensor_tensor(out=counts.unsqueeze(2), in0=counts.unsqueeze(2),
                                              in1=psS[:, :, PARTS * U:UCOLS], op=ALU.subtract))
                    ch.link(dve.tensor_reduce(out=counts2, in_=counts, axis=AX.X, op=ALU.max))
                    ch.link(dve.tensor_tensor(out=pneg[:, 2], in0=pneg[:, 0], in1=pneg[:, 1], op=ALU.subtract))
                    for dst, a, b in ((0, 0, 2), (HEADS, 2, 0)):
                        e = tab[:, :, D + dst:D + dst + HEADS]
                        ch.link(dve.tensor_tensor(out=e, in0=pneg[:, a, :, 0:U:2], in1=pneg[:, b, :, 1:U:2],
                                                  op=ALU.add))
                    e = tab[:, :, D:D + 2 * HEADS]
                    dve.scalar_tensor_tensor(out=e, in0=e, scalar=ALPHA, in1=e, op0=ALU.mult,
                                             op1=ALU.max).then_inc(e_ready, 1)
                    dve.wait_ge(keys_ps, 1)
                    dve.wait_ge(made, 2)
                    dve.tensor_tensor(out=keys[0:64, :], in0=psK[0:64, 0:SEG_COLS], in1=keyiota[0:64, :], op=ALU.mult)
                    ch.link(dve.tensor_tensor(out=keys[64:P, 0:6 * P], in0=psK[64:P, 0:6 * P],
                                              in1=keyiota[64:P, 0:6 * P], op=ALU.mult))
                    for k in range(ROUNDS):
                        eight = top[:, 8 * k:8 * k + 8]
                        ch.link(dve.max(out=eight, in_=keys))
                        ch.link(dve.match_replace(out=keys, in_to_replace=eight, in_values=keys, imm_value=0.0))
                    ch.link(dve.max(out=left, in_=keys))
                    ch.link(dve.tensor_tensor(out=leftf, in0=left[:, 0:1], in1=counts2, op=ALU.max))
                    dve.tensor_scalar(leftf, leftf, 0.0, None, ALU.is_gt).then_inc(over, 1)
                    ch.link(dve.tensor_scalar(padz, top, 0.0, segb[:, 1:2], ALU.is_equal, ALU.mult))
                    dve.scalar_tensor_tensor(out=lists, in0=top, scalar=segb[:, 0:1], in1=padz, op0=ALU.add,
                                             op1=ALU.add).then_inc(lists_ready, 1)
                    dve.wait_ge(over_ps, 1)
                    dve.tensor_copy(flag[:], psF[:])
                    dve.wait_ge(lists_ps, 1)
                    ch.link(dve.tensor_copy(cidx[:], psI[:].rearrange("p (k r) -> p r k", r=QUAD)[:, 0:TILES, :]))
                    dve.tensor_copy(idx_tab[:], cidx[:])
                    dve.scalar_tensor_tensor(out=crel[:], in0=tileiota, scalar=-float(P), in1=cidx[:], op0=ALU.mult,
                                             op1=ALU.add)
                    ch.link(dve.tensor_scalar(scaled, cidx[:], float(TILES), None, ALU.mult))
                    dve.tensor_tensor(out=idx_adj[:], in0=scaled, in1=tileiota, op=ALU.add)

                @block.tensor
                def _(pe):
                    pe.wait_ge(any_t, 1)
                    for s in range(SEG):
                        for c in range(SEG_FIRST[s], SEG_FIRST[s + 1]):
                            j = (c - SEG_FIRST[s]) * P
                            last = pe.matmul(psK[s * QUAD:(s + 1) * QUAD, j:j + P], anyb[:, c, :], identb[:], start=True,
                                             stop=True)
                    last.then_inc(keys_ps, 1)
                    pe.wait_ge(over, 1)
                    pe.matmul(psF[:], leftf, ones[:, 0:1], start=True, stop=True).then_inc(over_ps, 1)
                    pe.wait_ge(lists_ready, 1)
                    pe.transpose(psI[:, 0:P], lists[:, 0:P], ident[:])
                    for s in range(SEG):
                        q = slice(s * QUAD, (s + 1) * QUAD)
                        last = pe.matmul(psI[q, P:SEG_CAP], lists[q, P:SEG_CAP], ident[q, q], start=True, stop=True)
                    last.then_inc(lists_ps, 1)

        with ExitStack() as c4:
            def ps(name, shape, dt=F32):
                return c4.enter_context(nc.psum_tensor(name, shape, dt))

            def sem4(name):
                return c4.enter_context(nc.semaphore(name))

            zT = ps("zT", [P, 4 * 512])
            eT = [ps(f"eT{k}", [P, 512]) for k in range(2)]
            psN = [ps(f"psN{k}", [P, 512]) for k in range(2)]
            o = 0

            def carve(*shape):
                nonlocal o
                n = 1
                for s in shape:
                    n *= s
                v = work[:, o:o + n]
                o += n
                return v

            ga = [carve(SLOTS).rearrange("p (k r) -> p k r", k=CHUNKS) for _ in range(BUFS)]
            z = carve(ZC).rearrange("p (i s) -> p i s", i=HEADS)
            E = carve(ZC).rearrange("p (i s) -> p i s", i=HEADS)
            offs = carve(SLOTS)
            rs = carve(6 * HEADS).rearrange("p (s i) -> p s i", i=HEADS)
            fast_o = o
            da, dz, dE, dB = carve(P), carve(HEADS * P), carve(HEADS * P), carve(4 * P)
            dt_ = carve(TW)
            doffs, dmsk, dsc = carve(P), carve(P), carve(6 * HEADS).rearrange("p (s i) -> p s i", i=HEADS)
            diota = carve(TILES)
            assert o <= WORK, o
            o = fast_o
            B = [carve(CHUNKS * 4 * P).rearrange("p (k q r) -> p k q r", k=CHUNKS, q=4) for _ in range(2)]
            assert o <= WORK, o
            gt = [gts[:, b] for b in range(BUFS)]
            rglob = work[:, 0:ROWS]
            stage = sb("stage", [P, BUFS, 2, CHUNKS], U32)
            negm = [rs[:, b, :] for b in range(2)]
            den = [rs[:, 2 + b, :] for b in range(2)]
            rden = rs[:, 4, :]
            (staged, idx_seen, z_ready, zT_ready, max_ready, exp_done, e_ready, eT_ready, mul_done, num_ready, evac,
             dve_c) = (sem4(n) for n in (
                 "staged", "idx_seen", "z_ready", "zT_ready", "max_ready", "exp_done", "e_ready4", "eT_ready",
                 "mul_done", "num_ready", "evac", "dve_c4"))
            rd_ready = sem4("rd_ready")
            gathered = [sem4(f"gathered{b}") for b in range(BUFS)]
            PER_GATHER = 16 * 2 * CHUNKS

            def over_tiles(eng, step):
                with eng.Fori(0, LOOPED // BUFS) as i:
                    for b in range(BUFS):
                        step(i * BUFS + b, b)
                for t in range(LOOPED, TILES):
                    step(t, t % BUFS)

            def sparse_pool(pool):
                def step(t, b):
                    pool.wait_ge(num_ready, t + 1)
                    for w, lst in enumerate((idx_tab, idx_adj)):
                        pool.tensor_copy(stage[:, b, w, :], lst[:, bass.ds(t, 1), :].rearrange(
                            "p o k -> p (o k)")).then_inc(staged, 1)
                    pool.wait_ge(staged, 2 * t + 2)
                    pool.sem_inc(idx_seen, 1)
                    for k in range(CHUNKS):
                        pool.indirect_dma_start(
                            out=ga[b][:, k, :], out_offset=None, in_=adj_rows,
                            in_offset=bass.IndirectOffsetOnAxis(ap=stage[:, b, 1, k:k + 1], axis=0),
                        ).then_inc(gathered[b], 16)
                        pool.indirect_dma_start(
                            out=gt[b][:, k, :], out_offset=None, in_=table,
                            in_offset=bass.IndirectOffsetOnAxis(ap=stage[:, b, 0, k:k + 1], axis=0),
                        ).then_inc(gathered[b], 16)

                over_tiles(pool, step)

            def sparse_vector(dve):
                def link(ins, t, n):
                    ins.then_inc(dve_c, 1)
                    dve.wait_ge(dve_c, t * 2 + n)

                def fill(t, b, turn):
                    dve.wait_ge(gathered[b], turn * PER_GATHER + PER_GATHER)
                    dve.wait_ge(num_ready, t + BUFS - 1)
                    for k in range(CHUNKS):
                        last = dve.scalar_tensor_tensor(
                            out=B[b % 2][:, k, HEADS, :], in0=coliota[:],
                            scalar=crel[:, bass.ds(t, 1), k:k + 1].rearrange("p o k -> p (o k)"),
                            in1=ga[b][:, k, :], op0=ALU.not_equal, op1=ALU.mult)
                    link(last, t, 1)
                    link(dve.tensor_scalar(offs.rearrange("p (k r) -> p k r", k=CHUNKS), B[b % 2][:, :, HEADS, :],
                                           0.0, NEG_INF, ALU.is_equal, ALU.mult), t, 2)
                    for j in range(HEADS):
                        for k in range(CHUNKS):
                            cols = slice(k * P, (k + 1) * P)
                            last = dve.tensor_scalar(z[:, j, cols], offs[:, cols],
                                                     gt[b][:, k, D + j:D + j + 1], None, ALU.add)
                    last.then_inc(z_ready, 1)

                def highest(t, b):
                    dve.wait_ge(zT_ready, t + 1)
                    dve.tensor_reduce(out=negm[b % 2], in_=zT[:, 0:ZC].rearrange("p (i s) -> p i s", i=HEADS),
                                      axis=AX.X, op=ALU.max, negate=True).then_inc(max_ready, 1)

                def finish(t, b):
                    dve.wait_ge(exp_done, t + 2)
                    dve.reciprocal(rden, den[b % 2]).then_inc(rd_ready, 1)
                    dve.wait_ge(rd_ready, t + 1)
                    for j in range(HEADS):
                        last = dve.tensor_scalar(E[:, j, :], E[:, j, :], rden[:, j:j + 1], None, ALU.mult)
                    last.then_inc(e_ready, 1)
                    for k in range(CHUNKS):
                        dve.wait_ge(eT_ready, t * CHUNKS + k + 2)
                        dve.tensor_tensor(
                            out=B[b % 2][:, k, 0:HEADS, :],
                            in0=eT[k % 2][:, 0:HEADS * P].rearrange("p (i r) -> p i r", i=HEADS),
                            in1=B[b % 2][:, k, HEADS:HEADS + 1, :].to_broadcast([P, HEADS, P]),
                            op=ALU.mult).then_inc(mul_done, 1)

                dve.sem_inc(mul_done, 2)
                fill(0, 0, 0)
                with dve.Fori(0, LOOPED // BUFS) as i:
                    for b in range(BUFS):
                        t = i * BUFS + b
                        highest(t, b)
                        fill(t + 1, (b + 1) % BUFS, i + (b + 1) // BUFS)
                        finish(t, b)
                for t in range(LOOPED, TILES):
                    highest(t, t % BUFS)
                    if t + 1 < TILES:
                        fill(t + 1, (t + 1) % BUFS, (t + 1) // BUFS)
                    finish(t, t % BUFS)

            def sparse_scalar(act):
                act.sem_inc(exp_done, 1)
                act.sem_inc(evac, 2)

                def step(t, b):
                    act.wait_ge(max_ready, t + 1)
                    act.wait_ge(eT_ready, t * CHUNKS + 1)
                    for j in range(HEADS):
                        last = act.activation(E[:, j, :], zT[:, j * SLOTS:(j + 1) * SLOTS], ACT.Exp,
                                              bias=negm[b % 2][:, j:j + 1], accum_out=den[b % 2][:, j:j + 1])
                    last.then_inc(exp_done, 1)
                    act.wait_ge(num_ready, t + BUFS + 1)
                    act.copy(num[:, :, bass.ds(t * P, P)], psN[b % 2][:].rearrange("p (q r) -> p q r", q=4)
                             ).then_inc(evac, 1)

                over_tiles(act, step)

            def sparse_tensor(pe):
                pe.sem_inc(num_ready, BUFS)
                pe.sem_inc(eT_ready, 1)

                def forth(t, b):
                    pe.wait_ge(z_ready, t + 1)
                    pe.wait_ge(exp_done, t + 1)
                    for j in range(HEADS):
                        for k in range(CHUNKS):
                            c0 = (j * CHUNKS + k) * P
                            last = pe.transpose(zT[:, c0:c0 + P], z[:, j, k * P:(k + 1) * P], ident[:])
                    last.then_inc(zT_ready, 1)

                def back(t, b):
                    pe.wait_ge(e_ready, t + 1)
                    pe.wait_ge(evac, t + 1)
                    for k in range(CHUNKS + 1):
                        if k < CHUNKS:
                            pe.wait_ge(mul_done, t * CHUNKS + k + 1)
                            for j in range(HEADS):
                                last = pe.transpose(eT[k % 2][:, j * P:(j + 1) * P], E[:, j, k * P:(k + 1) * P],
                                                    ident[:])
                            last.then_inc(eT_ready, 1)
                        if k > 0:
                            pe.wait_ge(mul_done, t * CHUNKS + k + 2)
                            last = pe.matmul(psN[b % 2][:], gt[b][:, k - 1, 0:D],
                                             B[b % 2][:, k - 1, :, :].rearrange("p q r -> p (q r)"),
                                             start=(k == 1), stop=(k == CHUNKS))
                    last.then_inc(num_ready, 1)

                forth(0, 0)
                with pe.Fori(0, LOOPED // BUFS) as i:
                    for b in range(BUFS):
                        forth(i * BUFS + b + 1, (b + 1) % BUFS)
                        back(i * BUFS + b, b)
                for t in range(LOOPED, TILES):
                    if t + 1 < TILES:
                        forth(t + 1, (t + 1) % BUFS)
                    back(t, t % BUFS)

            HIGHEST, SUM, PRODUCT = range(3)
            PASSES = (HIGHEST, SUM, PRODUCT)
            LINKS = (6, 6, 7)
            dn = ("d_in", "d_z", "d_zT", "d_exp", "d_e", "d_eT", "d_mul", "d_num", "d_link")
            ds_ = {p: {n: sem4(f"{n}{p}") for n in dn} for p in PASSES}
            d_start, d_rden, d_tile, d_open, d_iota, d_evac, d_free = (sem4(n) for n in (
                "d_start", "d_rden", "d_tile", "d_open", "d_iota", "d_evac", "d_free"))
            d_pass = [sem4(f"d_pass{p}") for p in PASSES]

            def dense_sync(sp):
                with sp.Fori(0, TILES) as t:
                    for p in PASSES:
                        s = ds_[p]
                        with sp.Fori(0, TILES) as c:
                            sp.wait_ge(d_free, (t * len(PASSES) + p) * TILES + c + 1)
                            sp.dma_start(da, adj_chunks[bass.ds(c, 1), :, bass.ds(t * P, P)].rearrange(
                                "o p r -> p (o r)")).then_inc(s["d_in"], 16)
                            sp.dma_start(dt_, table.rearrange("(c p) w -> c p w", p=P)[bass.ds(c, 1), :, :].rearrange(
                                "o p w -> p (o w)")).then_inc(s["d_in"], 16)

            def dense_pool(pool):
                pool.iota(rglob, pattern=[[1, ROWS]], base=0, channel_multiplier=0,
                          allow_small_or_imprecise_dtypes=True).then_inc(d_iota, 1)
                pool.iota(diota, pattern=[[P, TILES]], base=0, channel_multiplier=1,
                          allow_small_or_imprecise_dtypes=True).then_inc(d_iota, 1)

            def dense_vector(dve):
                negc, negall, denc, denall, rdall = (dsc[:, k, :] for k in range(5))
                az = dB[:, HEADS * P:4 * P]
                dve.sem_inc(d_free, 1)
                dve.wait_ge(d_iota, 2)
                with dve.Fori(0, TILES) as t:
                    dve.wait_ge(d_evac, t + 1)
                    dve.memset(negall, 3.0e38)
                    dve.memset(denall, 0.0).then_inc(d_start, 1)
                    dve.wait_ge(d_start, t + 1)
                    dve.sem_inc(d_open, 1)
                    for p in PASSES:
                        s = ds_[p]
                        with dve.Fori(0, TILES) as c:
                            n = t * TILES + c
                            count = [0]

                            def link(ins):
                                count[0] += 1
                                ins.then_inc(s["d_link"], 1)
                                dve.wait_ge(s["d_link"], n * LINKS[p] + count[0])

                            dve.wait_ge(s["d_in"], n * 32 + 32)
                            link(dve.scalar_tensor_tensor(out=az, in0=rglob[:, bass.ds(t * P, P)],
                                                          scalar=diota[:, bass.ds(c, 1)], in1=da,
                                                          op0=ALU.not_equal, op1=ALU.mult))
                            link(dve.tensor_scalar(doffs, az, 0.0, NEG_INF, ALU.is_equal, ALU.mult))
                            for sign, e0 in ((ALU.is_lt, HEADS), (ALU.is_gt, 0)):
                                link(dve.tensor_scalar(dmsk, az, 0.0, None, sign))
                                for j in range(HEADS):
                                    src = doffs if e0 else dz[:, j * P:(j + 1) * P]
                                    last = dve.scalar_tensor_tensor(
                                        out=dz[:, j * P:(j + 1) * P], in0=dmsk, scalar=dt_[:, D + e0 + j:D + e0 + j + 1],
                                        in1=src, op0=ALU.mult, op1=ALU.add)
                                if e0:
                                    link(last)
                                else:
                                    last.then_inc(s["d_z"], 1)
                            dve.wait_ge(s["d_zT"], n + 1)
                            if p == HIGHEST:
                                link(dve.tensor_reduce(out=negc, in_=zT[:, 0:HEADS * P].rearrange(
                                    "p (i s) -> p i s", i=HEADS), axis=AX.X, op=ALU.max, negate=True))
                                dve.tensor_tensor(out=negall, in0=negall, in1=negc, op=ALU.min).then_inc(d_free, 1)
                            elif p == SUM:
                                dve.wait_ge(s["d_exp"], n + 1)
                                link(dve.tensor_copy(rdall, denall))
                                dve.tensor_tensor(out=denall, in0=rdall, in1=denc, op=ALU.add).then_inc(d_free, 1)
                            else:
                                dve.wait_ge(s["d_exp"], n + 1)
                                for j in range(HEADS):
                                    last = dve.tensor_scalar(dE[:, j * P:(j + 1) * P], dE[:, j * P:(j + 1) * P],
                                                             rdall[:, j:j + 1], None, ALU.mult)
                                link(last)
                                dve.sem_inc(s["d_e"], 1)
                                dve.wait_ge(s["d_eT"], n + 1)
                                link(dve.tensor_tensor(
                                    out=dB[:, 0:HEADS * P].rearrange("p (i r) -> p i r", i=HEADS),
                                    in0=eT[0][:, 0:HEADS * P].rearrange("p (i r) -> p i r", i=HEADS),
                                    in1=az.unsqueeze(1).to_broadcast([P, HEADS, P]), op=ALU.mult))
                                dve.sem_inc(s["d_mul"], 1)
                                dve.wait_ge(s["d_num"], n + 1)
                                dve.sem_inc(d_free, 1)
                            assert count[0] == LINKS[p], count
                        dve.wait_ge(d_free, (t * len(PASSES) + p) * TILES + TILES + 1)
                        if p == SUM:
                            dve.reciprocal(rdall, denall).then_inc(d_rden, 1)
                            dve.wait_ge(d_rden, t + 1)
                        dve.sem_inc(d_pass[p], 1)
                    dve.sem_inc(d_tile, 1)

            def dense_scalar(act):
                act.sem_inc(d_evac, 1)
                with act.Fori(0, TILES) as t:
                    act.wait_ge(d_pass[HIGHEST], t + 1)
                    for p in (SUM, PRODUCT):
                        s = ds_[p]
                        with act.Fori(0, TILES) as c:
                            n = t * TILES + c
                            act.wait_ge(s["d_zT"], n + 1)
                            for j in range(HEADS):
                                last = act.activation(dE[:, j * P:(j + 1) * P], zT[:, j * P:(j + 1) * P], ACT.Exp,
                                                      bias=dsc[:, 1, j:j + 1], accum_out=dsc[:, 2, j:j + 1])
                            last.then_inc(s["d_exp"], 1)
                    act.wait_ge(d_tile, t + 1)
                    act.copy(num[:, :, bass.ds(t * P, P)], psN[0][:].rearrange("p (q r) -> p q r", q=4)
                             ).then_inc(d_evac, 1)

            def dense_tensor(pe):
                with pe.Fori(0, TILES) as t:
                    pe.wait_ge(d_evac, t + 1)
                    pe.matmul(psN[0][:], zeros[:, 0:P], zeros[:], start=True, stop=False, skip_group_check=True)
                    for p in PASSES:
                        s = ds_[p]
                        with pe.Fori(0, TILES) as c:
                            n = t * TILES + c
                            pe.wait_ge(s["d_z"], n + 1)
                            for j in range(HEADS):
                                last = pe.transpose(zT[:, j * P:(j + 1) * P], dz[:, j * P:(j + 1) * P], ident[:])
                            last.then_inc(s["d_zT"], 1)
                            if p == PRODUCT:
                                pe.wait_ge(s["d_e"], n + 1)
                                for j in range(HEADS):
                                    last = pe.transpose(eT[0][:, j * P:(j + 1) * P], dE[:, j * P:(j + 1) * P], ident[:])
                                last.then_inc(s["d_eT"], 1)
                                pe.wait_ge(s["d_mul"], n + 1)
                                pe.matmul(psN[0][:], dt_[:, 0:D], dB, start=False, stop=False,
                                          skip_group_check=True).then_inc(s["d_num"], 1)

            with nc.Block() as block:
                def either(eng, dense, sparse):
                    crowded = eng.value_load(flag[0:1, 0:1], min_val=0, max_val=P)
                    with eng.If(crowded > 0):
                        if dense:
                            dense(eng)
                        else:
                            eng.nop()
                    with eng.Else():
                        if sparse:
                            sparse(eng)
                        else:
                            eng.nop()

                @block.sync
                def _(sp):
                    either(sp, dense_sync, None)

                @block.gpsimd
                def _(pool):
                    either(pool, dense_pool, sparse_pool)

                @block.vector
                def _(dve):
                    either(dve, dense_vector, sparse_vector)

                @block.scalar
                def _(act):
                    either(act, dense_scalar, sparse_scalar)

                @block.tensor
                def _(pe):
                    either(pe, dense_tensor, sparse_tensor)

        with ExitStack() as c5:
            def ps(name, shape, dt=F32):
                return c5.enter_context(nc.psum_tensor(name, shape, dt))

            def sem5(name):
                return c5.enter_context(nc.semaphore(name))

            gates = [[ps(f"gate{c}{g}", [P, 512]) for g in range(4)] for c in range(2)]
            buf = [work[:, k * GB:(k + 1) * GB] for k in range(12)]
            es = buf[0]
            rg, zg, ng, tg = buf[1:3], buf[3:5], buf[5:7], buf[7:9]
            sumT = num[:, HEADS, :]
            es_ps, es_ready, gate_ps, rz_ready, t_ready, n_ready, rn_used = (
                sem5("es_ps"), sem5("es_ready"), sem5("gate_ps"), sem5("rz_ready"), sem5("t_ready"), sem5("n_ready"),
                sem5("rn_used"))
            cell_done, dve_c, bias_c = sem5("cell_done"), sem5("dve_c5"), sem5("bias_c")
            with nc.Block() as block:
                @block.tensor
                def _(pe):
                    with pe.Fori(0, GBLOCKS) as i:
                        cols = bass.ds(i * GB, GB)
                        pe.wait_ge(cell_done, 2 * i + 1)
                        for j in range(HEADS):
                            last = pe.matmul(gates[1][0][:, 0:GB], gatW_s[:, j, :], num[:, j, cols], start=(j == 0),
                                             stop=(j == HEADS - 1))
                        last.then_inc(es_ps, 1)
                        for c in range(2):
                            if c:
                                pe.wait_ge(es_ready, i + 1)
                            inp = es if c else num[:, HEADS, cols]
                            wi, wh = gruw_s[:, 2 * c, :], gruw_s[:, 2 * c + 1, :]
                            for g in range(2):
                                pe.matmul(gates[c][g][:, 0:GB], wi[:, g * D:(g + 1) * D], inp, start=True, stop=False)
                                pe.matmul(gates[c][g][:, 0:GB], wh[:, g * D:(g + 1) * D], hT[:, cols], start=False,
                                          stop=True)
                            pe.matmul(gates[c][2][:, 0:GB], wi[:, 2 * D:3 * D], inp, start=True, stop=True)
                            pe.matmul(gates[c][3][:, 0:GB], wh[:, 2 * D:3 * D], hT[:, cols], start=True,
                                      stop=True).then_inc(gate_ps, 1)

                @block.scalar
                def _(act):
                    act.wait_ge(bias_c, 1)
                    with act.Fori(0, GBLOCKS) as i:
                        act.wait_ge(es_ps, i + 1)
                        act.mul(es, gates[1][0][:, 0:GB], 1.0 / HEADS).then_inc(es_ready, 1)
                        for c in range(2):
                            act.wait_ge(gate_ps, 2 * i + c + 1)
                            act.wait_ge(cell_done, 2 * i + 1)
                            act.activation(rg[c], gates[c][0][:, 0:GB], ACT.Sigmoid, bias=gbias[:, c, 0:1])
                            act.activation(zg[c], gates[c][1][:, 0:GB], ACT.Sigmoid,
                                           bias=gbias[:, c, 1:2]).then_inc(rz_ready, 1)
                            act.wait_ge(t_ready, 2 * i + c + 1)
                            act.activation(ng[c], tg[c], ACT.Tanh, bias=grub_s[:, 2 * c, 2:3]).then_inc(n_ready, 1)

                @block.vector
                def _(dve):
                    dve.tensor_tensor(out=gbias[:], in0=grub_s[:, 0:4:2, 0:2], in1=grub_s[:, 1:4:2, 0:2],
                                      op=ALU.add).then_inc(bias_c, 1)
                    dve.sem_inc(cell_done, 1)
                    ch = Chain(dve, dve_c)
                    with dve.Fori(0, GBLOCKS) as i:
                        ch.loop(i, 2 * 3 + 2)
                        cols = bass.ds(i * GB, GB)
                        for c in range(2):
                            dve.wait_ge(rz_ready, 2 * i + c + 1)
                            ch.link(dve.scalar_tensor_tensor(out=tg[c], in0=gates[c][3][:, 0:GB],
                                                             scalar=grub_s[:, 2 * c + 1, 2:3], in1=rg[c], op0=ALU.add,
                                                             op1=ALU.mult))
                            dve.tensor_tensor(out=tg[c], in0=gates[c][2][:, 0:GB], in1=tg[c],
                                              op=ALU.add).then_inc(t_ready, 1)
                            dve.wait_ge(n_ready, 2 * i + c + 1)
                            ch.link(dve.tensor_tensor(out=rg[c], in0=hT[:, cols], in1=ng[c], op=ALU.subtract))
                            ch.link(dve.tensor_tensor(out=rg[c], in0=rg[c], in1=zg[c], op=ALU.mult))
                            if c == 0:
                                ch.link(dve.tensor_tensor(out=buf[9], in0=rg[c], in1=ng[c], op=ALU.add))
                                dve.sem_inc(cell_done, 1)
                            else:
                                ch.link(dve.tensor_tensor(out=rg[c], in0=rg[c], in1=ng[c], op=ALU.add))
                                dve.tensor_tensor(out=sumT[:, cols], in0=rg[c], in1=buf[9],
                                                  op=ALU.add).then_inc(cell_done, 1)
                        ch.done(GBLOCKS)

        xt = region[:, 0:ROWS].rearrange("p (t d) -> p t d", t=TILES)
        xn = region[:, ROWS:2 * ROWS].rearrange("p (t d) -> p t d", t=TILES)
        xtT = region[:, 2 * ROWS:3 * ROWS]
        xnT = hT
        sq = work[:, 0:ROWS].rearrange("p (t d) -> p t d", t=TILES)
        small = work[:, ROWS:]
        logits = small[:, 0:TILES * EXPERTS].rearrange("p (t e) -> p t e", e=EXPERTS)
        best = small[:, 256:256 + TILES * 8].rearrange("p (t e) -> p t e", e=8)
        besti = small[:, 512:512 + TILES * 8].bitcast(U32).rearrange("p (t e) -> p t e", e=8)
        bestf = small[:, 768:768 + TILES * 2].rearrange("p (t e) -> p t e", e=2)
        w12 = small[:, 832:832 + 4 * TILES].rearrange("p (k t) -> p k t", k=4)
        eiota = small[:, 960:960 + TILES * EXPERTS].rearrange("p (t e) -> p t e", e=EXPERTS)
        gtf = gts[:].rearrange("p b k w -> p (b k w)")
        wt = gtf[:, 0:TILES * EXPERTS]
        wtv = wt.rearrange("p (t e) -> p t e", e=EXPERTS)
        wtmp = small[:, 1216:1216 + TILES * EXPERTS].rearrange("p (t e) -> p t e", e=EXPERTS)
        wT8 = small[0:EXPERTS, 1472:1472 + ROWS]
        b1g = gtf[:, 256:256 + EXPERTS * HC]
        with ExitStack() as c6:
            def ps(name, shape, dt=F32):
                return c6.enter_context(nc.psum_tensor(name, shape, dt))

            def sem6(name):
                return c6.enter_context(nc.semaphore(name))

            psT = [ps(f"psR{k}", [P, 512]) for k in range(2)]
            psL = ps("psL", [P, TILES, EXPERTS])
            psB = ps("psB", [P, EXPERTS * HC])
            psW = [ps(f"psW{k}", [P, 512]) for k in range(2)]
            psZ = [ps(f"psZ{k}", [P, 512]) for k in range(2)]
            groups = [(t, min(4, TILES - t)) for t in range(0, TILES, 4)]
            NG = len(groups)
            (sum_T, x_done, dve_c, centred, squared, vared, stdev, xt_ready, xn_ready, tr, tr_copied, log_ps, expd,
             dif, wt_ready, wT_ps, wT_ready, bz_ps, b1_ps, eio, scaled_w) = (sem6(n) for n in (
                 "sum_T", "x_done", "dve_c6", "centred6", "squared6", "vared6", "stdev6", "xt_ready", "xn_ready", "tr6",
                 "tr_copied", "log_ps", "expd", "dif", "wt_ready", "wT_ps", "wT_ready", "bz_ps", "b1_ps", "eio",
                 "scaled_w"))
            with nc.Block() as block:
                @block.gpsimd
                def _(pool):
                    pool.iota(eiota, pattern=[[0, TILES], [1, EXPERTS]], base=0, channel_multiplier=0,
                              allow_small_or_imprecise_dtypes=True).then_inc(eio, 1)
                    pool.wait_ge(b1_ps, 1)
                    for e in range(EXPERTS):
                        pool.tensor_scalar(W1_s[:, e, :], W1_s[:, e, :], lng_s[:, e:e + 1], None,
                                           ALU.mult).then_inc(scaled_w, 1)

                @block.tensor
                def _(pe):
                    for e in range(EXPERTS):
                        for c in range(HC):
                            last = pe.matmul(psB[:, e * HC + c:e * HC + c + 1], W1_s[:, e, c * P:(c + 1) * P],
                                             lnb_s[:, e:e + 1], start=True, stop=True)
                    last.then_inc(b1_ps, 1)
                    for g, (t0, n) in enumerate(groups):
                        if g >= 2:
                            pe.wait_ge(x_done, g - 1)
                        for t in range(n):
                            last = pe.transpose(psT[g % 2][:, t * P:(t + 1) * P],
                                                sumT[:, (t0 + t) * P:(t0 + t + 1) * P], ident[:])
                        last.then_inc(sum_T, 1)
                    for w, (ready, src) in enumerate(((xt_ready, xt), (xn_ready, xn))):
                        pe.wait_ge(ready, 1)
                        for g, (t0, n) in enumerate(groups):
                            if g >= 2 or w:
                                pe.wait_ge(tr_copied, w * NG + g - 1)
                            for t in range(n):
                                last = pe.transpose(psT[g % 2][:, t * P:(t + 1) * P], src[:, t0 + t, :], ident[:])
                            last.then_inc(tr, 1)
                        if w == 0:
                            pe.wait_ge(tr_copied, NG)
                            for t in range(TILES):
                                last = pe.matmul(psL[:, t, :], xtT[:, t * P:(t + 1) * P], Wr_s[:], start=True,
                                                 stop=True)
                            last.then_inc(log_ps, 1)
                    pe.wait_ge(wt_ready, 1)
                    for g, (t0, n) in enumerate(groups):
                        if g >= 2:
                            pe.wait_ge(wT_ready, g - 1)
                        for t in range(n):
                            last = pe.transpose(psW[g % 2][0:EXPERTS, t * P:(t + 1) * P], wtv[:, t0 + t, :], ident[:])
                        last.then_inc(wT_ps, 1)
                    for g, (t0, n) in enumerate(groups):
                        pe.wait_ge(wT_ready, g + 1)
                        if g >= 2:
                            pe.wait_ge(x_done, NG + g - 1)
                        for t in range(n):
                            last = pe.matmul(psZ[g % 2][:, t * P:(t + 1) * P], wT8[:, (t0 + t) * P:(t0 + t + 1) * P],
                                             b2_s[:], start=True, stop=True)
                        last.then_inc(bz_ps, 1)

                @block.scalar
                def _(act):
                    for k in range(2):
                        act.wait_ge(centred, k + 1)
                        act.activation(sq, (xt, xn)[k], ACT.Square).then_inc(squared, 1)
                        act.wait_ge(vared, k + 1)
                        act.activation(stat[:, 4, :], stat[:, 3, :], ACT.Sqrt).then_inc(stdev, 1)
                    for w, dst in enumerate((xtT, xnT)):
                        for g, (t0, n) in enumerate(groups):
                            act.wait_ge(tr, w * NG + g + 1)
                            act.copy(dst[:, t0 * P:(t0 + n) * P], psT[g % 2][:, 0:n * P]).then_inc(tr_copied, 1)
                    act.wait_ge(dif, 1)
                    act.activation(w12[:, 1, :], w12[:, 0, :], ACT.Exp).then_inc(expd, 1)
                    for g, (t0, n) in enumerate(groups):
                        act.wait_ge(wT_ps, g + 1)
                        act.copy(wT8[:, t0 * P:(t0 + n) * P], psW[g % 2][0:EXPERTS, 0:n * P]).then_inc(wT_ready, 1)

                @block.vector
                def _(dve):
                    ch = Chain(dve, dve_c)
                    for g, (t0, n) in enumerate(groups):
                        dve.wait_ge(sum_T, g + 1)
                        for t in range(n):
                            last = dve.scalar_tensor_tensor(out=xs[:, t0 + t, :], in0=psT[g % 2][:, t * P:(t + 1) * P],
                                                            scalar=dg[:, t0 + t:t0 + t + 1], in1=xs[:, t0 + t, :],
                                                            op0=ALU.mult, op1=ALU.add)
                        last.then_inc(x_done, 1)
                    dve.wait_ge(x_done, NG)
                    for k, (src, dst) in enumerate(((xs, xt), (xt, xn))):
                        ch.link(dve.tensor_reduce(out=stat[:, 0, :], in_=src[:, :, :], axis=AX.X, op=ALU.add))
                        ch.link(dve.tensor_scalar(stat[:, 1, :], stat[:, 0, :], 1.0 / D, None, ALU.mult))
                        dve.tensor_tensor(out=dst, in0=src[:, :, :], op=ALU.subtract,
                                          in1=stat[:, 1, :].unsqueeze(2).to_broadcast([P, TILES, D])
                                          ).then_inc(centred, 1)
                        dve.wait_ge(squared, k + 1)
                        ch.link(dve.tensor_reduce(out=stat[:, 2, :], in_=sq, axis=AX.X, op=ALU.add))
                        dve.tensor_scalar(stat[:, 3, :], stat[:, 2, :], 1.0 / D, EPS, ALU.mult,
                                          ALU.add).then_inc(vared, 1)
                        dve.wait_ge(stdev, k + 1)
                        ch.link(dve.reciprocal(stat[:, 5, :], stat[:, 4, :]))
                        ch.link(dve.tensor_tensor(out=dst, in0=dst, op=ALU.mult,
                                                  in1=stat[:, 5, :].unsqueeze(2).to_broadcast([P, TILES, D])))
                        dve.sem_inc((xt_ready, xn_ready)[k], 1)
                    dve.wait_ge(b1_ps, 1)
                    dve.tensor_tensor(out=b1g, in0=psB[:], in1=b1_s[:].rearrange("p e c -> p (e c)"), op=ALU.add)
                    dve.wait_ge(log_ps, 1)
                    ch.link(dve.tensor_tensor(out=logits, in0=psL[:], in1=br_s[:].unsqueeze(1).to_broadcast(
                        [P, TILES, EXPERTS]), op=ALU.add))
                    for t in range(TILES):
                        last = dve.max(out=best[:, t, :], in_=logits[:, t, :])
                    ch.link(last)
                    for t in range(TILES):
                        last = dve.max_index(out=besti[:, t, :], in_max=best[:, t, :], in_values=logits[:, t, :])
                    ch.link(last)
                    ch.link(dve.tensor_copy(bestf, besti[:, :, 0:2]))
                    dve.tensor_tensor(out=w12[:, 0, :].unsqueeze(2), in0=best[:, :, 1:2], in1=best[:, :, 0:1],
                                      op=ALU.subtract).then_inc(dif, 1)
                    dve.wait_ge(expd, 1)
                    ch.link(dve.tensor_scalar(w12[:, 2, :], w12[:, 1, :], 1.0, None, ALU.add))
                    ch.link(dve.reciprocal(w12[:, 2, :], w12[:, 2, :]))
                    ch.link(dve.tensor_tensor(out=w12[:, 3, :], in0=w12[:, 1, :], in1=w12[:, 2, :], op=ALU.mult))
                    dve.wait_ge(eio, 1)
                    for k, dst in enumerate((wtv, wtmp)):
                        ch.link(dve.tensor_tensor(out=dst, in0=eiota, in1=bestf[:, :, k:k + 1].to_broadcast(
                            [P, TILES, EXPERTS]), op=ALU.is_equal))
                        ch.link(dve.tensor_tensor(out=dst, in0=dst, in1=w12[:, 2 + k, :].unsqueeze(2).to_broadcast(
                            [P, TILES, EXPERTS]), op=ALU.mult))
                    dve.tensor_tensor(out=wtv, in0=wtv, in1=wtmp, op=ALU.add).then_inc(wt_ready, 1)
                    for g, (t0, n) in enumerate(groups):
                        dve.wait_ge(bz_ps, g + 1)
                        dve.tensor_tensor(out=xs[:, t0:t0 + n, :], in0=psZ[g % 2][:, 0:n * P].rearrange(
                            "p (t d) -> p t d", t=n), in1=xs[:, t0:t0 + n, :], op=ALU.add).then_inc(x_done, 1)

        with ExitStack() as c7:
            def ps(name, shape, dt=F32):
                return c7.enter_context(nc.psum_tensor(name, shape, dt))

            def sem7(name):
                return c7.enter_context(nc.semaphore(name))

            psH = [ps(f"psH{k}", [P, 512]) for k in range(4)]
            psY = [ps(f"psY{k}", [P, MT, D]) for k in range(2)]
            act_h = [work[:, k * HC * MB:(k + 1) * HC * MB].rearrange("p (c n) -> p c n", c=HC) for k in range(2)]
            h_ps, h_ready, y_ps, y_used, stored = (sem7("h_ps"), sem7("h_ready7"), sem7("y_ps"), sem7("y_used"),
                                                   sem7("stored7"))
            HALF = HC // 2
            with nc.Block() as block:
                @block.tensor
                def _(pe):
                    def up(i, e):
                        pe.wait_ge(h_ready, EXPERTS * i + e + 1)
                        for c in range(HC):
                            last = pe.matmul(psH[2 * (e % 2) + c // 2][:, (c % 2) * MB:(c % 2 + 1) * MB],
                                             W1_s[:, e, c * P:(c + 1) * P], xnT[:, bass.ds(i * MB, MB)],
                                             start=True, stop=True)
                            if c % HALF == HALF - 1:
                                last.then_inc(h_ps, 1)

                    def down(i, e):
                        pe.wait_ge(h_ready, EXPERTS * i + e + 3)
                        pe.wait_ge(y_used, EXPERTS * i + e + 1)
                        for t in range(MT):
                            for c in range(HC):
                                last = pe.matmul(psY[e % 2][:, t, :], act_h[e % 2][:, c, t * P:(t + 1) * P],
                                                 W2_s[:, e * HC + c, :], start=(c == 0), stop=(c == HC - 1))
                        last.then_inc(y_ps, 1)

                    pe.sem_inc(y_ps, 2)
                    with pe.Fori(0, MBLOCKS) as i:
                        up(i, 0)
                        for e in range(EXPERTS):
                            if e + 1 < EXPERTS:
                                up(i, e + 1)
                            down(i, e)

                @block.scalar
                def _(act):
                    act.sem_inc(h_ready, 2)
                    with act.Fori(0, MBLOCKS) as i:
                        for e in range(EXPERTS):
                            act.wait_ge(y_ps, EXPERTS * i + e + 1)
                            for c in range(HC):
                                if c % HALF == 0:
                                    act.wait_ge(h_ps, 2 * EXPERTS * i + 2 * e + c // HALF + 1)
                                last = act.activation(act_h[e % 2][:, c, :],
                                                      psH[2 * (e % 2) + c // 2][:, (c % 2) * MB:(c % 2 + 1) * MB],
                                                      ACT.Gelu, bias=b1g[:, e * HC + c:e * HC + c + 1])
                            last.then_inc(h_ready, 1)

                @block.vector
                def _(dve):
                    dve.sem_inc(y_used, 2)
                    with dve.Fori(0, MBLOCKS) as i:
                        for e in range(EXPERTS):
                            dve.wait_ge(y_ps, EXPERTS * i + e + 3)
                            dve.wait_ge(y_used, EXPERTS * i + e + 2)
                            for t in range(MT):
                                row = xs[:, bass.ds(MT * i + t, 1), :].rearrange("p o d -> p (o d)")
                                last = dve.scalar_tensor_tensor(
                                    out=row, in0=psY[e % 2][:, t, :],
                                    scalar=wt[:, bass.ds((MT * i + t) * EXPERTS + e, 1)], in1=row, op0=ALU.mult,
                                    op1=ALU.add)
                            last.then_inc(y_used, 1)

                @block.sync
                def _(sp):
                    sp.wait_ge(y_used, EXPERTS * MBLOCKS + 2)
                    full = TILES - 1
                    sp.dma_start(out[0:full * P, :].rearrange("(t p) d -> p t d", p=P), xs[:, 0:full, :]
                                 ).then_inc(stored, 16)
                    sp.dma_start(out[full * P:NODES, :], xs[0:NODES - full * P, full, :]).then_inc(stored, 16)
                    sp.wait_ge(stored, 32)


def kernel(**inputs):
    import numpy as np
    import concourse.bacc as _bacc
    from concourse import mybir as _mybir
    from concourse.bass_utils import run_bass_kernel_spmd as _run

    src = {k: np.asarray(v) for k, v in inputs.items()}
    adj = src["adj"]
    adjT = np.zeros((ROWS, ROWS), adj.dtype)
    adjT[:NODES, :NODES] = adj.T
    x = np.zeros((ROWS, D), src["x"].dtype)
    x[:NODES] = src["x"]
    dg = np.zeros(ROWS, adj.dtype)
    dg[:NODES] = np.diagonal(adj)
    g = {k[len("L0_gnn_"):]: v for k, v in src.items() if k.startswith("L0_gnn_")}
    f = {k[len("L0_ffn_"):]: v for k, v in src.items() if k.startswith("L0_ffn_")}
    gru = [g[n] for n in ("edge_Wih", "edge_Whh", "node_Wih", "node_Whh")]
    bias = [g[n] for n in ("edge_bih", "edge_bhh", "node_bih", "node_bhh")]
    laid = {
        "x": x, "adjT": adjT, "diag": dg.reshape(TILES, P).T,
        "gatW": g["gat_W"].transpose(1, 0, 2), "gatWT": g["gat_W"].transpose(2, 0, 1),
        "gata": g["gat_a"].reshape(HEADS, 2, D).transpose(2, 0, 1),
        "gruw": np.stack([w.T for w in gru], axis=1),
        "grub": np.stack([b.reshape(3, D).T for b in bias], axis=1),
        "Wr": f["Wr"], "br": f["br"], "lng": f["ln_g"].T, "lnb": f["ln_b"].T,
        "W1": f["W1"].transpose(1, 0, 2), "b1": f["b1"].reshape(EXPERTS, HC, P).transpose(2, 0, 1),
        "W2": f["W2"].reshape(EXPERTS * HC, P, D).transpose(1, 0, 2), "b2": f["b2"],
    }
    nc = _bacc.Bacc("TRN2", target_bir_lowering=False, num_devices=1)
    arrays, args = {}, []
    for name, a in laid.items():
        a = np.ascontiguousarray(a)
        arrays[f"in_{name}"] = a
        args.append(nc.dram_tensor(f"in_{name}", a.shape, _mybir.dt.from_np(a.dtype), kind="ExternalInput").ap())
    args.append(nc.dram_tensor("out_0", (NODES, D), _mybir.dt.float32, kind="ExternalOutput").ap())
    gnn_moe(nc, *args)
    r = _run(nc, [arrays], core_ids=[0])
    return r.results[0]["out_0"]
```

```python
from contextlib import ExitStack

import concourse.bass as bass
import numpy as np
from concourse import mybir

F32 = mybir.dt.float32
BF16 = mybir.dt.bfloat16
U32 = mybir.dt.uint32
I32 = mybir.dt.int32
ALU = mybir.AluOpType
ACT = mybir.ActivationFunctionType
AX = mybir.AxisListType

P = 128
NODES = 3327
TILES = (NODES + P - 1) // P
ROWS = TILES * P
PAD = ROWS - 1
D = 128
HEADS = 3
ALPHA = 0.2
NEG_INF = -9000000000000000.0
EPS = 1e-05
U = 2 * HEADS
PARTS = 3
TW = D + 2 * HEADS + 2
SEG = 4
QUAD = 32
SEG_FIRST = [0, 7, 14, 20, 26]
SEG_COLS = 7 * P
SEG_CAP = P + QUAD
CHUNKS = SEG_CAP * SEG // P
SLOTS = CHUNKS * P
ROUNDS = SEG_CAP // 8
UCOLS = PARTS * U + 1
BUFS = 4
DEPTH = 6
ZBUFS = 3
LOOPED = TILES // BUFS * BUFS
ZC = HEADS * SLOTS
HR = HEADS * P
GB = 416
GBLOCKS = ROWS // GB
EXPERTS = 8
HID = 512
HC = HID // P
TOP = 2
BLOCKS_E = TILES + 1
SPARE = EXPERTS
STEPS = -(-(TOP * TILES + EXPERTS - 1) // 6) * 6
XW = D + 2
XBUFS = 6
WBUFS = 3
SCAN = 16


class Chain:

    def __init__(self, eng, sem):
        self.eng, self.sem, self.base, self.n, self.turn, self.per = eng, sem, 0, 0, None, 0

    def loop(self, turn, per):
        self.base, self.n, self.turn, self.per = self.base + self.n, 0, turn, per

    def done(self, turns):
        assert self.n == self.per, (self.n, self.per)
        self.base, self.n, self.turn = self.base + turns * self.per, 0, None

    def link(self, ins):
        self.n += 1
        ins.then_inc(self.sem, 1)
        count = self.base + self.n
        if self.turn is not None:
            count = self.turn * self.per + count
        self.eng.wait_ge(self.sem, count)


def gnn_moe(nc, x, adjT, diag, gatW, gatWT, gata, gruw, grub, Wr, br, lng, lnb, W1, b1, W2, b2, out, dbg=None):
    adj_chunks = adjT.rearrange("(c p) r -> c p r", p=P)
    adj_rows = adjT.rearrange("c (t r) -> (c t) r", r=P)
    table = nc.dram_tensor("neighbour_table", (ROWS, TW), F32, kind="Internal").ap()
    BLOCKS = EXPERTS * BLOCKS_E + SPARE
    slots = nc.dram_tensor("slots", (BLOCKS * P, XW), F32, kind="Internal").ap()
    slot_blocks = slots.rearrange("(b p) w -> b p w", p=P)
    expert_out = nc.dram_tensor("expert_out", (TOP * ROWS + 2 * SPARE * P, D), F32, kind="Internal").ap()

    with ExitStack() as ctx:
        def sb(name, shape, dt=F32):
            return ctx.enter_context(nc.sbuf_tensor(name, shape, dt))

        def sem(name):
            return ctx.enter_context(nc.semaphore(name))

        xs = sb("xs", [P, TILES, D])
        hT = sb("hT", [P, ROWS])
        tab = sb("tab", [P, TILES, TW])
        h = tab[:, :, 0:D]
        dg = sb("dg", [P, TILES])
        ident = sb("ident", [P, P])
        identb = sb("identb", [P, P], BF16)
        notid = sb("notid", [P, P])
        ones = sb("ones", [P, P])
        gatW_s = sb("gatW_s", [P, HEADS, D])
        gatWT_s = sb("gatWT_s", [P, HEADS, D])
        gata_s = sb("gata_s", [P, HEADS, 2])
        gruw_s = sb("gruw_s", [P, 4, 3 * D])
        grub_s = sb("grub_s", [P, 4, 3])
        gbias = sb("gbias", [P, 2, 2])
        Wr_s = sb("Wr_s", [P, EXPERTS])
        br_s = sb("br_s", [P, EXPERTS])
        lng_s = sb("lng_s", [P, EXPERTS])
        lnb_s = sb("lnb_s", [P, EXPERTS])
        W1_s = sb("W1_s", [P, EXPERTS, HID])
        b1_s = sb("b1_s", [P, EXPERTS, HC])
        W2_s = sb("W2_s", [P, EXPERTS * HC, D])
        b2_s = sb("b2_s", [EXPERTS, D])
        region = sb("region", [P, 4 * ROWS])
        masks = region[:, 2 * ROWS:4 * ROWS].bitcast(BF16)
        pos = [masks[:, b * ROWS:(b + 1) * ROWS] for b in range(2)]
        sgn = [masks[:, (2 + b) * ROWS:(3 + b) * ROWS] for b in range(2)]
        num = region[:, :].rearrange("p (q r) -> p q r", q=4)
        WORK = 13312
        work = sb("work", [P, WORK])
        at = [region[:, b * ROWS:(b + 1) * ROWS] for b in range(2)] + [
            work[:, (1 + b) * ROWS:(2 + b) * ROWS] for b in range(2)]
        anyw = work[:, 0:TILES * (64 + 32 + 16) // 2].bitcast(BF16)
        gts = sb("gts", [P, 1, CHUNKS, TW])
        at_in = [sem(f"at_in{b}") for b in range(BUFS)]
        stat = sb("stat", [P, 6, TILES])
        V = sb("V", [P, U])
        u32_ = sb("u_f", [P, TILES, U])
        urest = sb("u_rest", [P, TILES, U])
        uparts = sb("u_parts", [P, TILES, UCOLS], BF16)
        anyc = sb("anyc", [P, TILES, TILES])
        cidx = sb("cidx", [P, TILES, CHUNKS])
        crel = sb("crel", [P, TILES, CHUNKS])
        idx_tab = sb("idx_tab", [P, TILES, CHUNKS], U32)
        idx_adj = sb("idx_adj", [P, TILES, CHUNKS], U32)
        coliota = sb("coliota", [P, P])
        flag = sb("flag", [1, 1], I32)
        y_out = [sem(f"y_out{b}") for b in range(XBUFS)]
        plan = sb("plan", [1, 2, STEPS], I32)
        zeros = sb("zeros", [P, 512], BF16)

        done_with = []

        with ExitStack() as c1:
            def ps(name, shape, dt=F32):
                return c1.enter_context(nc.psum_tensor(name, shape, dt))

            def sem1(name):
                done_with.append(c1.enter_context(nc.semaphore(name)))
                return done_with[-1]

            psT = [ps(f"psT{k}", [P, 512]) for k in range(2)]
            psU = ps("psU", [P, TILES, U])
            psV = ps("psV", [P, U])
            x_in, w_in, gw_in = sem1("x_in"), sem1("w_in"), sem1("gw_in")
            consts, dve_c, centred, squared = sem1("consts"), sem1("dve_c1"), sem1("centred"), sem1("squared")
            vared, stdev, h_ready = sem1("vared"), sem1("stdev"), sem1("h_ready")
            group_T, hT_ready, V_ps, V_ready, u_ps = (sem1("group_T"), sem1("hT_ready"), sem1("V_ps"), sem1("V_ready"),
                                                      sem1("u_ps"))
            iotas = sem1("iotas1")
            groups = [(t, min(4, TILES - t)) for t in range(0, TILES, 4)]
            sq = work[:, 0:ROWS].rearrange("p (t d) -> p t d", t=TILES)
            with nc.Block() as block:
                @block.sync
                def _(sp):
                    sp.dma_start(xs[:], x.rearrange("(t p) d -> p t d", p=P)).then_inc(x_in, 16)
                    sp.dma_start(gatWT_s[:], gatWT).then_inc(gw_in, 16)
                    sp.dma_start(gata_s[:], gata).then_inc(gw_in, 16)
                    for dst, src in ((dg, diag), (gatW_s, gatW), (gruw_s, gruw), (grub_s, grub), (Wr_s, Wr),
                                     (lng_s, lng), (lnb_s, lnb), (W1_s, W1), (b1_s, b1), (W2_s, W2), (b2_s, b2)):
                        sp.dma_start(dst[:], src).then_inc(w_in, 16)
                    sp.dma_start(br_s[:], br.partition_broadcast(P)).then_inc(w_in, 16)
                    for b in range(BUFS):
                        sp.dma_start(at[b], adj_chunks[b, :, :]).then_inc(at_in[b], 16)
                    sp.wait_ge(w_in, 16 * 12)

                @block.gpsimd
                def _(pool):
                    pool.memset(ident[:], 0.0).then_inc(iotas, 1)
                    pool.memset(identb[:], 0.0).then_inc(iotas, 1)
                    pool.memset(notid[:], 1.0).then_inc(iotas, 1)
                    pool.wait_ge(iotas, 3)
                    for tile, fill in ((ident, 1.0), (identb, 1.0), (notid, 0.0)):
                        pool.affine_select(out=tile[:], in_=tile[:], compare_op=ALU.not_equal, fill=fill, base=0,
                                           pattern=[[-1, P]], channel_multiplier=1).then_inc(consts, 1)
                    pool.memset(ones[:], 1.0).then_inc(consts, 1)
                    pool.memset(zeros[:], 0.0).then_inc(consts, 1)
                    pool.memset(tab[:, :, D:TW], 0.0).then_inc(consts, 1)
                    pool.memset(uparts[:, :, PARTS * U:UCOLS], 1.0).then_inc(consts, 1)
                    pool.iota(coliota[:], pattern=[[1, P]], base=0, channel_multiplier=0,
                              allow_small_or_imprecise_dtypes=True).then_inc(consts, 1)

                @block.vector
                def _(dve):
                    ch = Chain(dve, dve_c)
                    dve.wait_ge(x_in, 16)
                    ch.link(dve.tensor_reduce(out=stat[:, 0, :], in_=xs[:], axis=AX.X, op=ALU.add))
                    ch.link(dve.tensor_scalar(stat[:, 1, :], stat[:, 0, :], 1.0 / D, None, ALU.mult))
                    dve.tensor_tensor(out=h, in0=xs[:], in1=stat[:, 1, :].unsqueeze(2).to_broadcast([P, TILES, D]),
                                      op=ALU.subtract).then_inc(centred, 1)
                    dve.wait_ge(squared, 1)
                    ch.link(dve.tensor_reduce(out=stat[:, 2, :], in_=sq, axis=AX.X, op=ALU.add))
                    dve.tensor_scalar(stat[:, 3, :], stat[:, 2, :], 1.0 / D, EPS, ALU.mult, ALU.add).then_inc(vared, 1)
                    dve.wait_ge(stdev, 1)
                    ch.link(dve.reciprocal(stat[:, 5, :], stat[:, 4, :]))
                    dve.tensor_tensor(out=h, in0=h, in1=stat[:, 5, :].unsqueeze(2).to_broadcast([P, TILES, D]),
                                      op=ALU.mult).then_inc(h_ready, 1)
                    dve.wait_ge(V_ps, 1)
                    dve.tensor_copy(V[:], psV[:]).then_inc(V_ready, 1)
                    dve.wait_ge(u_ps, 1)
                    ch.link(dve.tensor_copy(u32_[:], psU[:]))
                    src = u32_
                    for k in range(PARTS):
                        part = uparts[:, :, k * U:(k + 1) * U]
                        ch.link(dve.tensor_copy(part, src[:]))
                        if k < PARTS - 1:
                            ch.link(dve.tensor_tensor(out=urest[:], in0=src[:], in1=part, op=ALU.subtract))
                            src = urest

                @block.scalar
                def _(act):
                    act.wait_ge(centred, 1)
                    act.activation(sq, h, ACT.Square).then_inc(squared, 1)
                    act.wait_ge(vared, 1)
                    act.activation(stat[:, 4, :], stat[:, 3, :], ACT.Sqrt).then_inc(stdev, 1)
                    for g, (t0, n) in enumerate(groups):
                        act.wait_ge(group_T, g + 1)
                        act.copy(hT[:, t0 * P:(t0 + n) * P], psT[g % 2][:, 0:n * P]).then_inc(hT_ready, 1)

                @block.tensor
                def _(pe):
                    pe.wait_ge(consts, 8)
                    pe.wait_ge(gw_in, 32)
                    for i in range(HEADS):
                        last = pe.matmul(psV[:, 2 * i:2 * i + 2], gatWT_s[:, i, :], gata_s[:, i, :], start=True,
                                         stop=True)
                    last.then_inc(V_ps, 1)
                    pe.wait_ge(h_ready, 1)
                    for g, (t0, n) in enumerate(groups):
                        if g >= 2:
                            pe.wait_ge(hT_ready, g - 1)
                        for t in range(n):
                            last = pe.transpose(psT[g % 2][:, t * P:(t + 1) * P], tab[:, t0 + t, 0:D], ident[:])
                        last.then_inc(group_T, 1)
                    pe.wait_ge(V_ready, 1)
                    pe.wait_ge(hT_ready, len(groups))
                    for t in range(TILES):
                        last = pe.matmul(psU[:, t, :], hT[:, t * P:(t + 1) * P], V[:], start=True, stop=True)
                    last.then_inc(u_ps, 1)

        with ExitStack() as c2:
            def ps(name, shape, dt=F32):
                return c2.enter_context(nc.psum_tensor(name, shape, dt))

            def sem2(name):
                return c2.enter_context(nc.semaphore(name))

            psP = ps("psP", [P, TILES, UCOLS])
            psS = ps("psS", [P, TILES, UCOLS])
            undiag, pos_ready, sgn_ready, any_done, pe_used, tree = (
                sem2("undiag"), sem2("pos_ready"), sem2("sgn_ready"), sem2("any_done"), sem2("pe_used"), sem2("tree"))
            TREE = 3
            with nc.Block() as block:
                def over_chunks(eng, step):
                    with eng.Fori(0, LOOPED // BUFS) as i:
                        for b in range(BUFS):
                            step(i * BUFS + b, b)
                    for c in range(LOOPED, TILES):
                        step(c, c - LOOPED)

                @block.sync
                def _(sp):
                    def load(c, b):
                        sp.wait_ge(pos_ready, c + 1)
                        sp.wait_ge(sgn_ready, c + 1)
                        src = adj_chunks[c + BUFS:c + BUFS + 1, :, :] if isinstance(c, int) else \
                            adj_chunks[bass.ds(c + BUFS, 1), :, :]
                        sp.dma_start(at[b], src.rearrange("o p r -> p (o r)")).then_inc(at_in[b], 16)

                    with sp.Fori(0, LOOPED // BUFS - 1) as i:
                        for b in range(BUFS):
                            load(i * BUFS + b, b)
                    for c in range(LOOPED - BUFS, TILES - BUFS):
                        load(c, c % BUFS)

                @block.gpsimd
                def _(pool):
                    def step(c, b):
                        turn = c // BUFS if isinstance(c, int) else None
                        if turn is None:
                            pool.wait_ge(at_in[b], (c - b) * (16 // BUFS) + 16)
                        else:
                            pool.wait_ge(at_in[b], 16 * turn + 16)
                        dblock = at[b][:, bass.ds(c * P, P)]
                        pool.tensor_tensor(out=dblock, in0=dblock, in1=notid[:], op=ALU.mult).then_inc(undiag, 1)

                    over_chunks(pool, step)

                @block.vector
                def _(dve):
                    def step(c, b):
                        dve.wait_ge(undiag, c + 1)
                        dve.wait_ge(pe_used, c + 1)
                        dve.tensor_scalar(pos[b % 2], at[b], 0.0, None, ALU.is_gt).then_inc(pos_ready, 1)
                        dve.wait_ge(pos_ready, c + 1)
                        src, w, o = pos[b % 2].rearrange("p (t r) -> p t r", r=P), P, 0
                        for k in range(TREE):
                            w //= 2
                            dst = anyw[:, o:o + TILES * w].rearrange("p (t r) -> p t r", r=w)
                            o += TILES * w
                            dve.tensor_tensor(out=dst, in0=src[:, :, 0:w], in1=src[:, :, w:2 * w],
                                              op=ALU.max).then_inc(tree, 1)
                            dve.wait_ge(tree, c * TREE + k + 1)
                            src = dst
                        dve.tensor_reduce(out=anyc[:, bass.ds(c, 1), :].rearrange("p o t -> p (o t)"), in_=src,
                                          axis=AX.X, op=ALU.max).then_inc(any_done, 1)

                    over_chunks(dve, step)

                @block.scalar
                def _(act):
                    def step(c, b):
                        act.wait_ge(undiag, c + 1)
                        act.wait_ge(pe_used, c + 1)
                        act.activation(sgn[b % 2], at[b], ACT.Sign).then_inc(sgn_ready, 1)

                    over_chunks(act, step)

                @block.tensor
                def _(pe):
                    for bank in (psP, psS):
                        pe.matmul(bank[:].rearrange("p t u -> p (t u)"), zeros[:, 0:P], zeros[:, 0:TILES * UCOLS],
                                  start=True, stop=False, skip_group_check=True)
                    pe.sem_inc(pe_used, 2)

                    def step(c, b):
                        parts = uparts[:, bass.ds(c, 1), :].rearrange("p o u -> p (o u)")
                        for bank, mask, ready in ((psP, pos, pos_ready), (psS, sgn, sgn_ready)):
                            pe.wait_ge(ready, c + 1)
                            for t in range(TILES):
                                last = pe.matmul(bank[:, t, :], mask[b % 2][:, t * P:(t + 1) * P], parts,
                                                 start=False, stop=False, skip_group_check=True)
                        last.then_inc(pe_used, 1)

                    over_chunks(pe, step)

            psK = ps("psK", [P, 2 * 512])
            psI = ps("psI", [P, SEG_CAP])
            psF = ps("psF", [1, 1])
            pneg = work[:, 0:3 * TILES * U].rearrange("p (k t u) -> p k t u", k=3, t=TILES)
            counts = work[:, 470:470 + TILES]
            counts2 = work[:, 496:496 + 1]
            anyb = work[:, 512:512 + TILES * QUAD // 2].bitcast(BF16).rearrange("p (c q) -> p c q", q=QUAD)
            keys = work[:, 1024:1024 + SEG_COLS]
            keyiota = work[:, 2048:2048 + SEG_COLS]
            top = work[:, 3072:3072 + SEG_CAP]
            lists = work[:, 3328:3328 + SEG_CAP]
            padz = work[:, 3584:3584 + SEG_CAP]
            left = work[:, 3840:3848]
            segb = work[:, 3848:3850]
            leftf = work[:, 3850:3851]
            tileiota = work[:, 3900:3900 + TILES * CHUNKS].rearrange("p (t k) -> p t k", k=CHUNKS)
            scaled = work[:, 4100:4100 + TILES * CHUNKS].rearrange("p (t k) -> p t k", k=CHUNKS)
            made, dve_c, any_t, keys_ps, lists_ready, lists_ps, e_ready, stored, over, over_ps = (
                sem2("made"), sem2("dve_c3"), sem2("any_t"), sem2("keys_ps"), sem2("lists_ready"), sem2("lists_ps"),
                sem2("e_ready"), sem2("stored"), sem2("over"), sem2("over_ps"))
            with nc.Block() as block:
                @block.sync
                def _(sp):
                    sp.wait_ge(e_ready, 1)
                    sp.dma_start(table.rearrange("(t p) w -> p t w", p=P), tab[:]).then_inc(stored, 16)
                    sp.wait_ge(stored, 16)

                @block.gpsimd
                def _(pool):
                    pool.iota(keyiota, pattern=[[1, SEG_COLS]], base=1, channel_multiplier=0,
                              allow_small_or_imprecise_dtypes=True).then_inc(made, 1)
                    pool.iota(tileiota, pattern=[[1, TILES], [0, CHUNKS]], base=0, channel_multiplier=0,
                              allow_small_or_imprecise_dtypes=True).then_inc(made, 1)

                @block.vector
                def _(dve):
                    ch = Chain(dve, dve_c)
                    dve.memset(anyb, 0.0)
                    for s in range(SEG):
                        q = slice(s * QUAD, (s + 1) * QUAD)
                        dve.memset(segb[q, 0:1], float(SEG_FIRST[s] * P - 1))
                        dve.memset(segb[q, 1:2], float(PAD + 1 - SEG_FIRST[s] * P))
                    ch.link(dve.memset(keys[64:P, 6 * P:7 * P], 0.0))
                    dve.tensor_scalar(anyb[:, :, 0:TILES], anyc[:], 0.0, None, ALU.is_gt).then_inc(any_t, 1)
                    by_part = "p t (k u) -> p t u k"
                    for k, bank in enumerate((psP, psS)):
                        ch.link(dve.tensor_reduce(out=pneg[:, k], in_=bank[:, :, 0:PARTS * U].rearrange(
                            by_part, k=PARTS), axis=AX.X, op=ALU.add))
                    ch.link(dve.tensor_copy(counts.unsqueeze(2), psP[:, :, PARTS * U:UCOLS]))
                    ch.link(dve.tensor_tensor(out=counts.unsqueeze(2), in0=counts.unsqueeze(2),
                                              in1=psS[:, :, PARTS * U:UCOLS], op=ALU.subtract))
                    ch.link(dve.tensor_reduce(out=counts2, in_=counts, axis=AX.X, op=ALU.max))
                    ch.link(dve.tensor_tensor(out=pneg[:, 2], in0=pneg[:, 0], in1=pneg[:, 1], op=ALU.subtract))
                    for dst, a, b in ((0, 0, 2), (HEADS, 2, 0)):
                        e = tab[:, :, D + dst:D + dst + HEADS]
                        ch.link(dve.tensor_tensor(out=e, in0=pneg[:, a, :, 0:U:2], in1=pneg[:, b, :, 1:U:2],
                                                  op=ALU.add))
                    e = tab[:, :, D:D + 2 * HEADS]
                    dve.scalar_tensor_tensor(out=e, in0=e, scalar=ALPHA, in1=e, op0=ALU.mult,
                                             op1=ALU.max).then_inc(e_ready, 1)
                    dve.wait_ge(keys_ps, 1)
                    dve.wait_ge(made, 2)
                    dve.tensor_tensor(out=keys[0:64, :], in0=psK[0:64, 0:SEG_COLS], in1=keyiota[0:64, :], op=ALU.mult)
                    ch.link(dve.tensor_tensor(out=keys[64:P, 0:6 * P], in0=psK[64:P, 0:6 * P],
                                              in1=keyiota[64:P, 0:6 * P], op=ALU.mult))
                    for k in range(ROUNDS):
                        eight = top[:, 8 * k:8 * k + 8]
                        ch.link(dve.max(out=eight, in_=keys))
                        ch.link(dve.match_replace(out=keys, in_to_replace=eight, in_values=keys, imm_value=0.0))
                    ch.link(dve.max(out=left, in_=keys))
                    ch.link(dve.tensor_tensor(out=leftf, in0=left[:, 0:1], in1=counts2, op=ALU.max))
                    dve.tensor_scalar(leftf, leftf, 0.0, None, ALU.is_gt).then_inc(over, 1)
                    ch.link(dve.tensor_scalar(padz, top, 0.0, segb[:, 1:2], ALU.is_equal, ALU.mult))
                    dve.scalar_tensor_tensor(out=lists, in0=top, scalar=segb[:, 0:1], in1=padz, op0=ALU.add,
                                             op1=ALU.add).then_inc(lists_ready, 1)
                    dve.wait_ge(over_ps, 1)
                    dve.tensor_copy(flag[:], psF[:])
                    dve.wait_ge(lists_ps, 1)
                    ch.link(dve.tensor_copy(cidx[:], psI[:].rearrange("p (k r) -> p r k", r=QUAD)[:, 0:TILES, :]))
                    dve.tensor_copy(idx_tab[:], cidx[:])
                    dve.scalar_tensor_tensor(out=crel[:], in0=tileiota, scalar=-float(P), in1=cidx[:], op0=ALU.mult,
                                             op1=ALU.add)
                    ch.link(dve.tensor_scalar(scaled, cidx[:], float(TILES), None, ALU.mult))
                    dve.tensor_tensor(out=idx_adj[:], in0=scaled, in1=tileiota, op=ALU.add)

                @block.tensor
                def _(pe):
                    pe.wait_ge(any_t, 1)
                    for s in range(SEG):
                        for c in range(SEG_FIRST[s], SEG_FIRST[s + 1]):
                            j = (c - SEG_FIRST[s]) * P
                            last = pe.matmul(psK[s * QUAD:(s + 1) * QUAD, j:j + P], anyb[:, c, :], identb[:], start=True,
                                             stop=True)
                    last.then_inc(keys_ps, 1)
                    pe.wait_ge(over, 1)
                    pe.matmul(psF[:], leftf, ones[:, 0:1], start=True, stop=True).then_inc(over_ps, 1)
                    pe.wait_ge(lists_ready, 1)
                    pe.transpose(psI[:, 0:P], lists[:, 0:P], ident[:])
                    for s in range(SEG):
                        q = slice(s * QUAD, (s + 1) * QUAD)
                        last = pe.matmul(psI[q, P:SEG_CAP], lists[q, P:SEG_CAP], ident[q, q], start=True, stop=True)
                    last.then_inc(lists_ps, 1)

        with ExitStack() as c4:
            def ps(name, shape, dt=F32):
                return c4.enter_context(nc.psum_tensor(name, shape, dt))

            def sem4(name):
                return c4.enter_context(nc.semaphore(name))

            o = 0

            def carve(*shape):
                nonlocal o
                n = 1
                for s in shape:
                    n *= s
                v = work[:, o:o + n]
                o += n
                return v

            ga = [carve(SLOTS).rearrange("p (k r) -> p k r", k=CHUNKS) for _ in range(DEPTH)]
            z = [carve(ZC).rearrange("p (k i r) -> p k i r", k=CHUNKS, i=HEADS) for _ in range(ZBUFS)]
            offs = carve(SLOTS)
            tree = carve(HR * 2)
            mdiag = carve(HR)
            rdiag = carve(HR)
            rdenb = carve(HR)
            rden = carve(HEADS)
            negm = carve(HEADS)
            assert o <= WORK, o
            tabf = tab[:].rearrange("p t w -> p (t w)")
            gt = [tabf[:, b * CHUNKS * TW:(b + 1) * CHUNKS * TW].rearrange("p (k w) -> p k w", k=CHUNKS)
                  for b in range(DEPTH - 1)] + [gts[:, 0]]
            stage = sb("stage", [P, DEPTH, 2, CHUNKS], U32)
            zT = ps("zT", [P, 512])
            mB = ps("mB", [P, 512])
            psD = ps("psD", [P, 512])
            rB = ps("rB", [P, 512])
            psN = [ps(f"psN{k}", [P, 512]) for k in range(2)]
            psM = [ps(f"psM{k}", [P, 512]) for k in range(2)]
            (staged, idx_seen, az_ready, offs_ready, z_ready, tree_c, top_ready, topT_ready, negm_ready, diag_ready,
             mB_ready, s_ready, exp_ready, den_ready, mul_ready, num_ready, rden_ready, rdiag_ready, rB_ready,
             rdenb_ready, evac_heads, evac_sum) = (
                 sem4(n) for n in (
                     "staged", "idx_seen", "az_ready", "offs_ready", "z_ready", "tree_c", "top_ready",
                     "topT_ready", "negm_ready", "diag_ready", "mB_ready", "s_ready", "exp_ready", "den_ready",
                     "mul_ready", "num_ready", "rden_ready", "rdiag_ready", "rB_ready",
                     "rdenb_ready", "evac_heads", "evac_sum"))
            gathered = [sem4(f"gathered{b}") for b in range(DEPTH)]
            PER_GATHER = 16 * 2 * CHUNKS

            class Tile:

                def __init__(self, t, buf, turn):
                    self.t, self.b, self.turn, self.n = t, buf % DEPTH, turn + buf // DEPTH, buf

                def exists(self):
                    return not isinstance(self.t, int) or 0 <= self.t < TILES

                def plus(self, d):
                    return Tile(self.t + d, self.n + d, self.turn - self.n // DEPTH)

            HEAD_TILES = 2
            TURNS = (TILES - HEAD_TILES - 1) // DEPTH

            def pipeline(eng, step, drain):
                for t in range(HEAD_TILES):
                    step(Tile(t, t, 0))
                with eng.Fori(0, TURNS) as i:
                    for b in range(HEAD_TILES, HEAD_TILES + DEPTH):
                        step(Tile(i * DEPTH + b, b, i))
                for t in range(HEAD_TILES + TURNS * DEPTH, TILES + drain):
                    step(Tile(t, t, 0))

            def sparse_pool(pool):
                def step(x):
                    t, b = x.t, x.b
                    pool.wait_ge(num_ready, t + 1)
                    for w, lst in enumerate((idx_tab, idx_adj)):
                        pool.tensor_copy(stage[:, b, w, :], lst[:, bass.ds(t, 1), :].rearrange(
                            "p o k -> p (o k)")).then_inc(staged, 1)
                    pool.wait_ge(staged, 2 * t + 2)
                    pool.sem_inc(idx_seen, 1)
                    for k in range(CHUNKS):
                        pool.indirect_dma_start(
                            out=ga[b][:, k, :], out_offset=None, in_=adj_rows,
                            in_offset=bass.IndirectOffsetOnAxis(ap=stage[:, b, 1, k:k + 1], axis=0),
                        ).then_inc(gathered[b], 16)
                        pool.indirect_dma_start(
                            out=gt[b][:, k, :], out_offset=None, in_=table,
                            in_offset=bass.IndirectOffsetOnAxis(ap=stage[:, b, 0, k:k + 1], axis=0),
                        ).then_inc(gathered[b], 16)

                pipeline(pool, step, 0)

            def sparse_vector(dve):
                def fill(x):
                    dve.wait_ge(gathered[x.b], x.turn * PER_GATHER + PER_GATHER)
                    for k in range(CHUNKS):
                        last = dve.scalar_tensor_tensor(
                            out=ga[x.b][:, k, :], in0=coliota[:],
                            scalar=crel[:, bass.ds(x.t, 1), k:k + 1].rearrange("p o k -> p (o k)"),
                            in1=ga[x.b][:, k, :], op0=ALU.not_equal, op1=ALU.mult)
                    last.then_inc(az_ready, 1)
                    dve.wait_ge(az_ready, x.t + 1)
                    dve.tensor_scalar(offs, ga[x.b].rearrange("p k r -> p (k r)"), 0.0, NEG_INF, ALU.is_equal,
                                      ALU.mult).then_inc(offs_ready, 1)

                def top(x):
                    dve.wait_ge(z_ready, x.t + 1)
                    zz = z[x.b % ZBUFS].rearrange("p k i r -> p (k i r)")
                    pairs = zz[:, 0:4 * HR].rearrange("p (two n) -> p two n", two=2)
                    dve.tensor_tensor(out=tree, in0=pairs[:, 0], in1=pairs[:, 1], op=ALU.max).then_inc(tree_c, 1)
                    dve.wait_ge(tree_c, 2 * x.t + 1)
                    dve.tensor_tensor(out=tree[:, 0:HR], in0=tree[:, 0:HR], in1=tree[:, HR:2 * HR],
                                      op=ALU.max).then_inc(tree_c, 1)
                    dve.wait_ge(tree_c, 2 * x.t + 2)
                    dve.tensor_tensor(out=tree[:, 0:HR], in0=tree[:, 0:HR], in1=zz[:, 4 * HR:5 * HR],
                                      op=ALU.max).then_inc(top_ready, 1)

                def highest(x):
                    dve.wait_ge(topT_ready, x.t + 1)
                    dve.tensor_reduce(out=negm, in_=zT[:, 0:HR].rearrange("p (i s) -> p i s", i=HEADS), axis=AX.X,
                                      op=ALU.max, negate=True).then_inc(negm_ready, 1)
                    dve.wait_ge(negm_ready, x.t + 1)
                    for j in range(HEADS):
                        last = dve.tensor_scalar(mdiag[:, j * P:(j + 1) * P], ident[:], negm[:, j:j + 1], None,
                                                 ALU.mult)
                    last.then_inc(diag_ready, 1)

                def below(x):
                    dve.wait_ge(mB_ready, x.t + 1)
                    flat = z[x.b % ZBUFS].rearrange("p k i r -> p k (i r)")
                    dve.tensor_tensor(out=flat, in0=flat, in1=mB[:, 0:HR].unsqueeze(1).to_broadcast(
                        [P, CHUNKS, HR]), op=ALU.add).then_inc(s_ready, 1)

                def times_adj(x):
                    dve.wait_ge(den_ready, x.t + 1)
                    dve.tensor_tensor(out=z[x.b % ZBUFS], in0=z[x.b % ZBUFS],
                                      in1=ga[x.b].unsqueeze(2).to_broadcast([P, CHUNKS, HEADS, P]),
                                      op=ALU.mult).then_inc(mul_ready, 1)

                def inverse(x):
                    dve.wait_ge(den_ready, x.t + 1)
                    dve.reciprocal(rden, psD[:, 0:HEADS]).then_inc(rden_ready, 1)
                    dve.wait_ge(rden_ready, x.t + 2)
                    dve.wait_ge(rB_ready, x.t + 1)
                    for j in range(HEADS):
                        last = dve.tensor_scalar(rdiag[:, j * P:(j + 1) * P], ident[:], rden[:, j:j + 1], None,
                                                 ALU.mult)
                    last.then_inc(rdiag_ready, 1)

                def normalize(x):
                    dve.wait_ge(rdenb_ready, x.t + 2)
                    dve.wait_ge(num_ready, x.t + DEPTH + 1)
                    dve.tensor_tensor(out=num[:, 0:HEADS, bass.ds(x.t * P, P)],
                                      in0=psN[x.b % 2][:, 0:HR].rearrange("p (i r) -> p i r", i=HEADS),
                                      in1=rdenb.rearrange("p (i r) -> p i r", i=HEADS),
                                      op=ALU.mult).then_inc(evac_heads, 1)

                dve.sem_inc(rden_ready, 1)
                dve.sem_inc(evac_heads, 2)
                fill(Tile(0, 0, 0))

                def step(x):
                    for f, d in ((top, 0), (fill, 1), (highest, 0), (inverse, -1), (normalize, -2), (times_adj, -1),
                                 (below, 0)):
                        if x.plus(d).exists():
                            f(x.plus(d))

                pipeline(dve, step, 2)

            def sparse_scalar(act):
                def fill(x):
                    act.wait_ge(offs_ready, x.t + 1)
                    for k in range(CHUNKS):
                        for j in range(HEADS):
                            last = act.activation(z[x.b % ZBUFS][:, k, j, :], offs[:, k * P:(k + 1) * P], ACT.Identity,
                                                  bias=gt[x.b][:, k, D + j:D + j + 1])
                    last.then_inc(z_ready, 1)

                def exponential(x):
                    act.wait_ge(s_ready, x.t + 1)
                    act.activation(z[x.b % ZBUFS], z[x.b % ZBUFS], ACT.Exp).then_inc(exp_ready, 1)

                def support(x):
                    act.wait_ge(num_ready, x.t + DEPTH + 1)
                    act.copy(num[:, HEADS, bass.ds(x.t * P, P)], psM[x.b % 2][:, 0:P]).then_inc(evac_sum, 1)

                def inverse(x):
                    act.wait_ge(rB_ready, x.t + 2)
                    act.wait_ge(evac_heads, x.t + 2)
                    act.copy(rdenb, rB[:, 0:HR]).then_inc(rdenb_ready, 1)

                act.sem_inc(evac_sum, 2)
                act.sem_inc(rdenb_ready, 1)
                fill(Tile(0, 0, 0))

                def step(x):
                    for f, d in ((support, -2), (fill, 1), (inverse, -1), (exponential, 0)):
                        if x.plus(d).exists():
                            f(x.plus(d))

                pipeline(act, step, 2)

            def sparse_tensor(pe):
                pe.sem_inc(num_ready, DEPTH)

                pe.sem_inc(rB_ready, 1)

                def sums(x):
                    pe.wait_ge(exp_ready, x.t + 1)
                    pe.wait_ge(rden_ready, x.t + 1)
                    for j in range(HEADS):
                        for k in range(CHUNKS):
                            last = pe.matmul(psD[:, j:j + 1], z[x.b % ZBUFS][:, k, j, :], ones[:, 0:1], start=(k == 0),
                                             stop=(k == CHUNKS - 1))
                    last.then_inc(den_ready, 1)

                def spread_inverse(x):
                    pe.wait_ge(rdiag_ready, x.t + 1)
                    pe.wait_ge(rdenb_ready, x.t + 1)
                    pe.matmul(rB[:, 0:HR], ones[:], rdiag, start=True, stop=True).then_inc(rB_ready, 1)

                def transposed(x):
                    pe.wait_ge(top_ready, x.t + 1)
                    for j in range(HEADS):
                        last = pe.transpose(zT[:, j * P:(j + 1) * P], tree[:, j * P:(j + 1) * P], ident[:])
                    last.then_inc(topT_ready, 1)

                def spread(x):
                    pe.wait_ge(diag_ready, x.t + 1)
                    pe.matmul(mB[:, 0:HR], ones[:], mdiag, start=True, stop=True).then_inc(mB_ready, 1)

                def products(x):
                    pe.wait_ge(mul_ready, x.t + 1)
                    pe.wait_ge(evac_heads, x.t + 1)
                    pe.wait_ge(evac_sum, x.t + 1)
                    for k in range(CHUNKS):
                        hk = gt[x.b][:, k, 0:D]
                        pe.matmul(psN[x.b % 2][:, 0:HR], hk, z[x.b % ZBUFS][:, k].rearrange("p i r -> p (i r)"),
                                  start=(k == 0), stop=(k == CHUNKS - 1))
                        last = pe.matmul(psM[x.b % 2][:, 0:P], hk, ga[x.b][:, k, :],
                                         start=(k == 0), stop=(k == CHUNKS - 1))
                    last.then_inc(num_ready, 1)

                def step(x):
                    for f, d in ((transposed, 0), (sums, -1), (spread, 0), (spread_inverse, -1), (products, -1)):
                        if x.plus(d).exists():
                            f(x.plus(d))

                pipeline(pe, step, 1)

            o = 0
            rglob = carve(ROWS)
            da, dz, dE, dB = carve(P), carve(HR), carve(HR), carve(4 * P)
            dt_ = carve(TW)
            doffs, dmsk, dsc = carve(P), carve(P), carve(6 * HEADS).rearrange("p (s i) -> p s i", i=HEADS)
            diota = carve(TILES)
            eT = [mB]

            HIGHEST, SUM, PRODUCT = range(3)
            PASSES = (HIGHEST, SUM, PRODUCT)
            LINKS = (6, 6, 7)
            dn = ("d_in", "d_z", "d_zT", "d_exp", "d_e", "d_eT", "d_mul", "d_num", "d_link")
            ds_ = {p: {n: sem4(f"{n}{p}") for n in dn} for p in PASSES}
            d_start, d_rden, d_tile, d_open, d_iota, d_evac, d_free = (sem4(n) for n in (
                "d_start", "d_rden", "d_tile", "d_open", "d_iota", "d_evac", "d_free"))
            d_pass = [sem4(f"d_pass{p}") for p in PASSES]

            def dense_sync(sp):
                with sp.Fori(0, TILES) as t:
                    for p in PASSES:
                        s = ds_[p]
                        with sp.Fori(0, TILES) as c:
                            sp.wait_ge(d_free, (t * len(PASSES) + p) * TILES + c + 1)
                            sp.dma_start(da, adj_chunks[bass.ds(c, 1), :, bass.ds(t * P, P)].rearrange(
                                "o p r -> p (o r)")).then_inc(s["d_in"], 16)
                            sp.dma_start(dt_, table.rearrange("(c p) w -> c p w", p=P)[bass.ds(c, 1), :, :].rearrange(
                                "o p w -> p (o w)")).then_inc(s["d_in"], 16)

            def dense_pool(pool):
                pool.iota(rglob, pattern=[[1, ROWS]], base=0, channel_multiplier=0,
                          allow_small_or_imprecise_dtypes=True).then_inc(d_iota, 1)
                pool.iota(diota, pattern=[[P, TILES]], base=0, channel_multiplier=1,
                          allow_small_or_imprecise_dtypes=True).then_inc(d_iota, 1)

            def dense_vector(dve):
                negc, negall, denc, denall, rdall = (dsc[:, k, :] for k in range(5))
                az = dB[:, HEADS * P:4 * P]
                dve.sem_inc(d_free, 1)
                dve.wait_ge(d_iota, 2)
                with dve.Fori(0, TILES) as t:
                    dve.wait_ge(d_evac, t + 1)
                    dve.memset(negall, 3.0e38)
                    dve.memset(denall, 0.0).then_inc(d_start, 1)
                    dve.wait_ge(d_start, t + 1)
                    dve.sem_inc(d_open, 1)
                    for p in PASSES:
                        s = ds_[p]
                        with dve.Fori(0, TILES) as c:
                            n = t * TILES + c
                            count = [0]

                            def link(ins):
                                count[0] += 1
                                ins.then_inc(s["d_link"], 1)
                                dve.wait_ge(s["d_link"], n * LINKS[p] + count[0])

                            dve.wait_ge(s["d_in"], n * 32 + 32)
                            link(dve.scalar_tensor_tensor(out=az, in0=rglob[:, bass.ds(t * P, P)],
                                                          scalar=diota[:, bass.ds(c, 1)], in1=da,
                                                          op0=ALU.not_equal, op1=ALU.mult))
                            link(dve.tensor_scalar(doffs, az, 0.0, NEG_INF, ALU.is_equal, ALU.mult))
                            for sign, e0 in ((ALU.is_lt, HEADS), (ALU.is_gt, 0)):
                                link(dve.tensor_scalar(dmsk, az, 0.0, None, sign))
                                for j in range(HEADS):
                                    src = doffs if e0 else dz[:, j * P:(j + 1) * P]
                                    last = dve.scalar_tensor_tensor(
                                        out=dz[:, j * P:(j + 1) * P], in0=dmsk, scalar=dt_[:, D + e0 + j:D + e0 + j + 1],
                                        in1=src, op0=ALU.mult, op1=ALU.add)
                                if e0:
                                    link(last)
                                else:
                                    last.then_inc(s["d_z"], 1)
                            dve.wait_ge(s["d_zT"], n + 1)
                            if p == HIGHEST:
                                link(dve.tensor_reduce(out=negc, in_=zT[:, 0:HEADS * P].rearrange(
                                    "p (i s) -> p i s", i=HEADS), axis=AX.X, op=ALU.max, negate=True))
                                dve.tensor_tensor(out=negall, in0=negall, in1=negc, op=ALU.min).then_inc(d_free, 1)
                            elif p == SUM:
                                dve.wait_ge(s["d_exp"], n + 1)
                                link(dve.tensor_copy(rdall, denall))
                                dve.tensor_tensor(out=denall, in0=rdall, in1=denc, op=ALU.add).then_inc(d_free, 1)
                            else:
                                dve.wait_ge(s["d_exp"], n + 1)
                                for j in range(HEADS):
                                    last = dve.tensor_scalar(dE[:, j * P:(j + 1) * P], dE[:, j * P:(j + 1) * P],
                                                             rdall[:, j:j + 1], None, ALU.mult)
                                link(last)
                                dve.sem_inc(s["d_e"], 1)
                                dve.wait_ge(s["d_eT"], n + 1)
                                link(dve.tensor_tensor(
                                    out=dB[:, 0:HEADS * P].rearrange("p (i r) -> p i r", i=HEADS),
                                    in0=eT[0][:, 0:HEADS * P].rearrange("p (i r) -> p i r", i=HEADS),
                                    in1=az.unsqueeze(1).to_broadcast([P, HEADS, P]), op=ALU.mult))
                                dve.sem_inc(s["d_mul"], 1)
                                dve.wait_ge(s["d_num"], n + 1)
                                dve.sem_inc(d_free, 1)
                            assert count[0] == LINKS[p], count
                        dve.wait_ge(d_free, (t * len(PASSES) + p) * TILES + TILES + 1)
                        if p == SUM:
                            dve.reciprocal(rdall, denall).then_inc(d_rden, 1)
                            dve.wait_ge(d_rden, t + 1)
                        dve.sem_inc(d_pass[p], 1)
                    dve.sem_inc(d_tile, 1)

            def dense_scalar(act):
                act.sem_inc(d_evac, 1)
                with act.Fori(0, TILES) as t:
                    act.wait_ge(d_pass[HIGHEST], t + 1)
                    for p in (SUM, PRODUCT):
                        s = ds_[p]
                        with act.Fori(0, TILES) as c:
                            n = t * TILES + c
                            act.wait_ge(s["d_zT"], n + 1)
                            for j in range(HEADS):
                                last = act.activation(dE[:, j * P:(j + 1) * P], zT[:, j * P:(j + 1) * P], ACT.Exp,
                                                      bias=dsc[:, 1, j:j + 1], accum_out=dsc[:, 2, j:j + 1])
                            last.then_inc(s["d_exp"], 1)
                    act.wait_ge(d_tile, t + 1)
                    act.copy(num[:, :, bass.ds(t * P, P)], psN[0][:].rearrange("p (q r) -> p q r", q=4)
                             ).then_inc(d_evac, 1)

            def dense_tensor(pe):
                with pe.Fori(0, TILES) as t:
                    pe.wait_ge(d_evac, t + 1)
                    pe.matmul(psN[0][:], zeros[:, 0:P], zeros[:], start=True, stop=False, skip_group_check=True)
                    for p in PASSES:
                        s = ds_[p]
                        with pe.Fori(0, TILES) as c:
                            n = t * TILES + c
                            pe.wait_ge(s["d_z"], n + 1)
                            for j in range(HEADS):
                                last = pe.transpose(zT[:, j * P:(j + 1) * P], dz[:, j * P:(j + 1) * P], ident[:])
                            last.then_inc(s["d_zT"], 1)
                            if p == PRODUCT:
                                pe.wait_ge(s["d_e"], n + 1)
                                for j in range(HEADS):
                                    last = pe.transpose(eT[0][:, j * P:(j + 1) * P], dE[:, j * P:(j + 1) * P], ident[:])
                                last.then_inc(s["d_eT"], 1)
                                pe.wait_ge(s["d_mul"], n + 1)
                                pe.matmul(psN[0][:], dt_[:, 0:D], dB, start=False, stop=False,
                                          skip_group_check=True).then_inc(s["d_num"], 1)

            with nc.Block() as block:
                def either(eng, dense, sparse):
                    crowded = eng.value_load(flag[0:1, 0:1], min_val=0, max_val=P)
                    with eng.If(crowded > 0):
                        if dense:
                            dense(eng)
                        else:
                            eng.nop()
                    with eng.Else():
                        if sparse:
                            sparse(eng)
                        else:
                            eng.nop()

                @block.sync
                def _(sp):
                    either(sp, dense_sync, None)

                @block.gpsimd
                def _(pool):
                    either(pool, dense_pool, sparse_pool)

                @block.vector
                def _(dve):
                    either(dve, dense_vector, sparse_vector)

                @block.scalar
                def _(act):
                    either(act, dense_scalar, sparse_scalar)

                @block.tensor
                def _(pe):
                    either(pe, dense_tensor, sparse_tensor)

        with ExitStack() as c5:
            def ps(name, shape, dt=F32):
                return c5.enter_context(nc.psum_tensor(name, shape, dt))

            def sem5(name):
                return c5.enter_context(nc.semaphore(name))

            gates = [[ps(f"gate{c}{g}", [P, 512]) for g in range(4)] for c in range(2)]
            buf = [work[:, k * GB:(k + 1) * GB] for k in range(12)]
            es = buf[0]
            rg, zg, ng, tg = buf[1:3], buf[3:5], buf[5:7], buf[7:9]
            sumT = num[:, HEADS, :]
            es_ps, es_ready, gate_ps, rz_ready, t_ready, n_ready, rn_used = (
                sem5("es_ps"), sem5("es_ready"), sem5("gate_ps"), sem5("rz_ready"), sem5("t_ready"), sem5("n_ready"),
                sem5("rn_used"))
            cell_done, dve_c, bias_c = sem5("cell_done"), sem5("dve_c5"), sem5("bias_c")
            with nc.Block() as block:
                @block.gpsimd
                def _(pool):
                    for used in done_with:
                        pool.sem_clear(used)

                @block.tensor
                def _(pe):
                    with pe.Fori(0, GBLOCKS) as i:
                        cols = bass.ds(i * GB, GB)
                        pe.wait_ge(cell_done, 2 * i + 1)
                        for j in range(HEADS):
                            last = pe.matmul(gates[1][0][:, 0:GB], gatW_s[:, j, :], num[:, j, cols], start=(j == 0),
                                             stop=(j == HEADS - 1))
                        last.then_inc(es_ps, 1)
                        for c in range(2):
                            if c:
                                pe.wait_ge(es_ready, i + 1)
                            inp = es if c else num[:, HEADS, cols]
                            wi, wh = gruw_s[:, 2 * c, :], gruw_s[:, 2 * c + 1, :]
                            for g in range(2):
                                pe.matmul(gates[c][g][:, 0:GB], wi[:, g * D:(g + 1) * D], inp, start=True, stop=False)
                                pe.matmul(gates[c][g][:, 0:GB], wh[:, g * D:(g + 1) * D], hT[:, cols], start=False,
                                          stop=True)
                            pe.matmul(gates[c][2][:, 0:GB], wi[:, 2 * D:3 * D], inp, start=True, stop=True)
                            pe.matmul(gates[c][3][:, 0:GB], wh[:, 2 * D:3 * D], hT[:, cols], start=True,
                                      stop=True).then_inc(gate_ps, 1)

                @block.scalar
                def _(act):
                    act.wait_ge(bias_c, 1)
                    with act.Fori(0, GBLOCKS) as i:
                        act.wait_ge(es_ps, i + 1)
                        act.mul(es, gates[1][0][:, 0:GB], 1.0 / HEADS).then_inc(es_ready, 1)
                        for c in range(2):
                            act.wait_ge(gate_ps, 2 * i + c + 1)
                            act.wait_ge(cell_done, 2 * i + 1)
                            act.activation(rg[c], gates[c][0][:, 0:GB], ACT.Sigmoid, bias=gbias[:, c, 0:1])
                            act.activation(zg[c], gates[c][1][:, 0:GB], ACT.Sigmoid,
                                           bias=gbias[:, c, 1:2]).then_inc(rz_ready, 1)
                            act.wait_ge(t_ready, 2 * i + c + 1)
                            act.activation(ng[c], tg[c], ACT.Tanh, bias=grub_s[:, 2 * c, 2:3]).then_inc(n_ready, 1)

                @block.vector
                def _(dve):
                    dve.tensor_tensor(out=gbias[:], in0=grub_s[:, 0:4:2, 0:2], in1=grub_s[:, 1:4:2, 0:2],
                                      op=ALU.add).then_inc(bias_c, 1)
                    dve.sem_inc(cell_done, 1)
                    ch = Chain(dve, dve_c)
                    with dve.Fori(0, GBLOCKS) as i:
                        ch.loop(i, 2 * 3 + 2)
                        cols = bass.ds(i * GB, GB)
                        for c in range(2):
                            dve.wait_ge(rz_ready, 2 * i + c + 1)
                            ch.link(dve.scalar_tensor_tensor(out=tg[c], in0=gates[c][3][:, 0:GB],
                                                             scalar=grub_s[:, 2 * c + 1, 2:3], in1=rg[c], op0=ALU.add,
                                                             op1=ALU.mult))
                            dve.tensor_tensor(out=tg[c], in0=gates[c][2][:, 0:GB], in1=tg[c],
                                              op=ALU.add).then_inc(t_ready, 1)
                            dve.wait_ge(n_ready, 2 * i + c + 1)
                            ch.link(dve.tensor_tensor(out=rg[c], in0=hT[:, cols], in1=ng[c], op=ALU.subtract))
                            ch.link(dve.tensor_tensor(out=rg[c], in0=rg[c], in1=zg[c], op=ALU.mult))
                            if c == 0:
                                ch.link(dve.tensor_tensor(out=buf[9], in0=rg[c], in1=ng[c], op=ALU.add))
                                dve.sem_inc(cell_done, 1)
                            else:
                                ch.link(dve.tensor_tensor(out=rg[c], in0=rg[c], in1=ng[c], op=ALU.add))
                                dve.tensor_tensor(out=sumT[:, cols], in0=rg[c], in1=buf[9],
                                                  op=ALU.add).then_inc(cell_done, 1)
                        ch.done(GBLOCKS)

        xt = region[:, 0:ROWS].rearrange("p (t d) -> p t d", t=TILES)
        sent = [tab[:, :, 0:XW], region[:, ROWS:ROWS + TILES * XW].rearrange("p (t w) -> p t w", w=XW)]
        xn = sent[0][:, :, 0:D]
        filling = hT[:, 0:2 * SPARE * XW].rearrange("p (j w) -> p j w", w=XW)
        xtT = region[:, 3 * ROWS:4 * ROWS]
        sq = work[:, 0:ROWS].rearrange("p (t d) -> p t d", t=TILES)
        small = work[:, ROWS:]
        logits = small[:, 0:TILES * EXPERTS].rearrange("p (t e) -> p t e", e=EXPERTS)
        best = small[:, 256:256 + TILES * 8].rearrange("p (t e) -> p t e", e=8)
        besti = small[:, 512:512 + TILES * 8].bitcast(U32).rearrange("p (t e) -> p t e", e=8)
        bestf = small[:, 768:768 + TILES * 2].rearrange("p (t e) -> p t e", e=2)
        w12 = small[:, 832:832 + 4 * TILES].rearrange("p (k t) -> p k t", k=4)
        eiota = small[:, 960:960 + TILES * EXPERTS].rearrange("p (t e) -> p t e", e=EXPERTS)
        gtf = gts[:].rearrange("p b k w -> p (b k w)")
        wt = gtf[:, 0:TILES * EXPERTS]
        wtv = wt.rearrange("p (t e) -> p t e", e=EXPERTS)
        wtmp = small[:, 1216:1216 + TILES * EXPERTS].rearrange("p (t e) -> p t e", e=EXPERTS)
        wT8 = small[0:EXPERTS, 1472:1472 + ROWS]
        so = 1472 + ROWS

        def small_part(*shape):
            nonlocal so
            n = int(np.prod(shape))
            v = small[:, so:so + n]
            so += n
            assert ROWS + so <= WORK
            names = "abcd"[:len(shape)]
            return v.rearrange(f"p ({' '.join(names)}) -> p {' '.join(names)}",
                               **dict(zip(names, shape))) if len(shape) > 1 else v

        chosen = small_part(TOP, TILES, EXPERTS)
        chosen2 = small_part(TOP, TILES, EXPERTS)
        either_chosen = small_part(TILES, EXPERTS)
        earlier = small_part(P)
        scan = [small_part(SCAN + TILES, EXPERTS) for _ in range(2)]
        place = small_part(TILES, EXPERTS)
        slot_f = small_part(TOP, TILES)
        slot_i = small_part(TOP * TILES).bitcast(U32)
        first_slot = small_part(EXPERTS)
        fill_first = small_part(EXPERTS)
        fill_f = small_part(EXPERTS)
        fill_i = small_part(EXPERTS).bitcast(U32)
        block_first = small_part(EXPERTS, BLOCKS_E)
        block_used = small_part(EXPERTS, BLOCKS_E)
        ends = [small_part(4 + EXPERTS) for _ in range(2)]
        unused = small_part(EXPERTS)
        step_no = small_part(STEPS, EXPERTS)
        past = small_part(STEPS, EXPERTS)
        past_unused = small_part(STEPS, EXPERTS)
        step_f = small_part(2, STEPS)
        plan_end = so
        b1g = gtf[:, 256:256 + EXPERTS * HC]
        with ExitStack() as c6:
            def ps(name, shape, dt=F32):
                return c6.enter_context(nc.psum_tensor(name, shape, dt))

            def sem6(name):
                return c6.enter_context(nc.semaphore(name))

            psT = [ps(f"psR{k}", [P, 512]) for k in range(2)]
            psL = ps("psL", [P, TILES, EXPERTS])
            psQ = ps("psQ", [P, 512])
            psB = psQ[:, 0:EXPERTS * HC]
            TE = TILES * EXPERTS
            psC = psQ[:, 32:32 + 2 * TE].rearrange("p (k t e) -> p k t e", k=2, e=EXPERTS)
            psW = [ps(f"psW{k}", [P, 512]) for k in range(2)]
            psZ = [ps(f"psZ{k}", [P, 512]) for k in range(2)]
            groups = [(t, min(4, TILES - t)) for t in range(0, TILES, 4)]
            NG = len(groups)
            (sum_T, x_done, dve_c, centred, squared, vared, stdev, xt_ready, xn_ready, tr, tr_copied, log_ps, expd,
             dif, wt_ready, wT_ps, wT_ready, bz_ps, b1_ps, eio, scaled_w, xn_copied, chosen_ready, place_ps,
             slots_ready, fill_ready, ready_seen, sent_done, spare_ready,
             spare_sent) = (sem6(n) for n in (
                 "sum_T", "x_done", "dve_c6", "centred6", "squared6", "vared6", "stdev6", "xt_ready", "xn_ready", "tr6",
                 "tr_copied", "log_ps", "expd", "dif", "wt_ready", "wT_ps", "wT_ready", "bz_ps", "b1_ps", "eio",
                 "scaled_w", "xn_copied", "chosen_ready", "place_ps", "slots_ready", "fill_ready", "ready_seen",
                 "sent_done", "spare_ready", "spare_sent"))
            with nc.Block() as block:
                @block.sync
                def _(sp):
                    sp.wait_ge(spare_ready, 3)
                    sp.dma_start(slot_blocks[EXPERTS * BLOCKS_E:BLOCKS, :, :].rearrange("b p w -> p b w"),
                                 filling[:, SPARE:2 * SPARE, :]).then_inc(spare_sent, 16)
                    sp.wait_ge(spare_sent, 16)

                @block.gpsimd
                def _(pool):
                    def iota(out, pattern, base, channel, sem):
                        pool.iota(out, pattern=pattern, base=base, channel_multiplier=channel,
                                  allow_small_or_imprecise_dtypes=True).then_inc(sem, 1)

                    iota(eiota, [[0, TILES], [1, EXPERTS]], 0, 0, eio)
                    iota(first_slot, [[BLOCKS_E * P, EXPERTS]], 0, 0, eio)
                    iota(fill_first, [[BLOCKS_E * P, EXPERTS]], 0, 1, eio)
                    iota(block_first, [[0, EXPERTS], [P, BLOCKS_E]], 0, 0, eio)
                    iota(step_no, [[1, STEPS], [0, EXPERTS]], 0, 0, eio)
                    for v in scan:
                        pool.memset(v[:, 0:SCAN, :], 0.0).then_inc(eio, 1)
                    for v in ends:
                        pool.memset(v[:, 0:4], 0.0).then_inc(eio, 1)
                    pool.wait_ge(eio, 9)
                    pool.tensor_scalar(earlier, coliota[:], fill_first[:, 0:1], None, ALU.is_gt).then_inc(eio, 1)
                    pool.memset(filling[:, :, 0:D], 0.0).then_inc(spare_ready, 1)
                    pool.memset(filling[:, :, D + 1:XW], 0.0).then_inc(spare_ready, 1)
                    iota(filling[:, :, D:D + 1].bitcast(I32), [[P, 2 * SPARE], [0, 1]], TOP * ROWS, 1, spare_ready)
                    for k in range(TOP):
                        iota(sent[k][:, :, D:D + 1].bitcast(I32), [[P, TILES], [0, 1]], k * ROWS, 1, eio)
                    pool.wait_ge(b1_ps, 1)
                    for e in range(EXPERTS):
                        pool.tensor_scalar(W1_s[:, e, :], W1_s[:, e, :], lng_s[:, e:e + 1], None,
                                           ALU.mult).then_inc(scaled_w, 1)
                    pool.wait_ge(xn_copied, 1)
                    pool.wait_ge(slots_ready, 3)
                    pool.sem_inc(ready_seen, 1)
                    for t in range(TILES):
                        for k in range(TOP):
                            pool.indirect_dma_start(
                                out=slots, out_offset=bass.IndirectOffsetOnAxis(
                                    ap=slot_i[:, k * TILES + t:k * TILES + t + 1], axis=0),
                                in_=sent[k][:, t, :], in_offset=None).then_inc(sent_done, 16)
                    pool.wait_ge(fill_ready, 1)
                    pool.sem_inc(ready_seen, 1)
                    for e in range(EXPERTS):
                        pool.indirect_dma_start(
                            out=slots, out_offset=bass.IndirectOffsetOnAxis(ap=fill_i[:, e:e + 1], axis=0),
                            in_=filling[:, e, :], in_offset=None).then_inc(sent_done, 16)
                    pool.wait_ge(sent_done, 16 * (TOP * TILES + EXPERTS))

                @block.tensor
                def _(pe):
                    for e in range(EXPERTS):
                        for c in range(HC):
                            last = pe.matmul(psB[:, e * HC + c:e * HC + c + 1], W1_s[:, e, c * P:(c + 1) * P],
                                             lnb_s[:, e:e + 1], start=True, stop=True)
                    last.then_inc(b1_ps, 1)
                    for g, (t0, n) in enumerate(groups):
                        if g >= 2:
                            pe.wait_ge(x_done, g - 1)
                        for t in range(n):
                            last = pe.transpose(psT[g % 2][:, t * P:(t + 1) * P],
                                                sumT[:, (t0 + t) * P:(t0 + t + 1) * P], ident[:])
                        last.then_inc(sum_T, 1)
                    pe.wait_ge(xt_ready, 1)
                    for g, (t0, n) in enumerate(groups):
                        if g >= 2:
                            pe.wait_ge(tr_copied, g - 1)
                        for t in range(n):
                            last = pe.transpose(psT[g % 2][:, t * P:(t + 1) * P], xt[:, t0 + t, :], ident[:])
                        last.then_inc(tr, 1)
                    for g, (t0, n) in enumerate(groups):
                        pe.wait_ge(tr_copied, g + 1)
                        for t in range(t0, t0 + n):
                            last = pe.matmul(psL[:, t, :], xtT[:, t * P:(t + 1) * P], Wr_s[:], start=True,
                                             stop=True)
                    last.then_inc(log_ps, 1)
                    pe.wait_ge(chosen_ready, 1)
                    for k, m in enumerate((earlier, ones[:])):
                        last = pe.matmul(psQ[:, 32 + k * TE:32 + (k + 1) * TE], m,
                                         either_chosen.rearrange("p t e -> p (t e)"), start=True, stop=True)
                    last.then_inc(place_ps, 1)
                    pe.wait_ge(wt_ready, 1)
                    for g, (t0, n) in enumerate(groups):
                        if g >= 2:
                            pe.wait_ge(wT_ready, g - 1)
                        for t in range(n):
                            last = pe.transpose(psW[g % 2][0:EXPERTS, t * P:(t + 1) * P], wtv[:, t0 + t, :], ident[:])
                        last.then_inc(wT_ps, 1)
                    for g, (t0, n) in enumerate(groups):
                        pe.wait_ge(wT_ready, g + 1)
                        if g >= 2:
                            pe.wait_ge(x_done, NG + g - 1)
                        for t in range(n):
                            last = pe.matmul(psZ[g % 2][:, t * P:(t + 1) * P], wT8[:, (t0 + t) * P:(t0 + t + 1) * P],
                                             b2_s[:], start=True, stop=True)
                        last.then_inc(bz_ps, 1)

                @block.scalar
                def _(act):
                    for k in range(2):
                        act.wait_ge(centred, k + 1)
                        act.activation(sq, (xt, xn)[k], ACT.Square).then_inc(squared, 1)
                        act.wait_ge(vared, k + 1)
                        act.activation(stat[:, 4, :], stat[:, 3, :], ACT.Sqrt).then_inc(stdev, 1)
                    for g, (t0, n) in enumerate(groups):
                        act.wait_ge(tr, g + 1)
                        act.copy(xtT[:, t0 * P:(t0 + n) * P], psT[g % 2][:, 0:n * P]).then_inc(tr_copied, 1)
                    act.wait_ge(xn_ready, 1)
                    act.copy(sent[1][:, :, 0:D], xn).then_inc(xn_copied, 1)
                    act.wait_ge(dif, 1)
                    act.activation(w12[:, 1, :], w12[:, 0, :], ACT.Exp).then_inc(expd, 1)
                    for g, (t0, n) in enumerate(groups):
                        act.wait_ge(wT_ps, g + 1)
                        act.copy(wT8[:, t0 * P:(t0 + n) * P], psW[g % 2][0:EXPERTS, 0:n * P]).then_inc(wT_ready, 1)

                @block.vector
                def _(dve):
                    ch = Chain(dve, dve_c)
                    for g, (t0, n) in enumerate(groups):
                        dve.wait_ge(sum_T, g + 1)
                        for t in range(n):
                            last = dve.scalar_tensor_tensor(out=xs[:, t0 + t, :], in0=psT[g % 2][:, t * P:(t + 1) * P],
                                                            scalar=dg[:, t0 + t:t0 + t + 1], in1=xs[:, t0 + t, :],
                                                            op0=ALU.mult, op1=ALU.add)
                        last.then_inc(x_done, 1)
                    dve.wait_ge(x_done, NG)
                    for k, (src, dst) in enumerate(((xs, xt), (xt, xn))):
                        ch.link(dve.tensor_reduce(out=stat[:, 0, :], in_=src[:, :, :], axis=AX.X, op=ALU.add))
                        ch.link(dve.tensor_scalar(stat[:, 1, :], stat[:, 0, :], 1.0 / D, None, ALU.mult))
                        dve.tensor_tensor(out=dst, in0=src[:, :, :], op=ALU.subtract,
                                          in1=stat[:, 1, :].unsqueeze(2).to_broadcast([P, TILES, D])
                                          ).then_inc(centred, 1)
                        dve.wait_ge(squared, k + 1)
                        ch.link(dve.tensor_reduce(out=stat[:, 2, :], in_=sq, axis=AX.X, op=ALU.add))
                        dve.tensor_scalar(stat[:, 3, :], stat[:, 2, :], 1.0 / D, EPS, ALU.mult,
                                          ALU.add).then_inc(vared, 1)
                        dve.wait_ge(stdev, k + 1)
                        ch.link(dve.reciprocal(stat[:, 5, :], stat[:, 4, :]))
                        ch.link(dve.tensor_tensor(out=dst, in0=dst, op=ALU.mult,
                                                  in1=stat[:, 5, :].unsqueeze(2).to_broadcast([P, TILES, D])))
                        dve.sem_inc((xt_ready, xn_ready)[k], 1)
                    dve.wait_ge(b1_ps, 1)
                    dve.tensor_tensor(out=b1g, in0=psB, in1=b1_s[:].rearrange("p e c -> p (e c)"), op=ALU.add)
                    dve.wait_ge(log_ps, 1)
                    ch.link(dve.tensor_tensor(out=logits, in0=psL[:], in1=br_s[:].unsqueeze(1).to_broadcast(
                        [P, TILES, EXPERTS]), op=ALU.add))
                    for t in range(TILES):
                        last = dve.max(out=best[:, t, :], in_=logits[:, t, :])
                    ch.link(last)
                    for t in range(TILES):
                        last = dve.max_index(out=besti[:, t, :], in_max=best[:, t, :], in_values=logits[:, t, :])
                    ch.link(last)
                    ch.link(dve.tensor_copy(bestf, besti[:, :, 0:2]))
                    dve.tensor_tensor(out=w12[:, 0, :].unsqueeze(2), in0=best[:, :, 1:2], in1=best[:, :, 0:1],
                                      op=ALU.subtract).then_inc(dif, 1)
                    dve.wait_ge(expd, 1)
                    ch.link(dve.tensor_scalar(w12[:, 2, :], w12[:, 1, :], 1.0, None, ALU.add))
                    ch.link(dve.reciprocal(w12[:, 2, :], w12[:, 2, :]))
                    ch.link(dve.tensor_tensor(out=w12[:, 3, :], in0=w12[:, 1, :], in1=w12[:, 2, :], op=ALU.mult))
                    dve.wait_ge(eio, 12)
                    for k in range(TOP):
                        last = dve.tensor_tensor(out=chosen[:, k, :, :], in0=eiota,
                                                 in1=bestf[:, :, k:k + 1].to_broadcast([P, TILES, EXPERTS]),
                                                 op=ALU.is_equal)
                    ch.link(last)
                    dve.tensor_tensor(out=either_chosen, in0=chosen[:, 0, :, :], in1=chosen[:, 1, :, :],
                                      op=ALU.add).then_inc(chosen_ready, 1)
                    for k in range(TOP):
                        dve.tensor_copy(sent[k][:, :, D + 1:XW], w12[:, 2 + k, :].unsqueeze(2)).then_inc(
                            slots_ready, 1)
                    ch.link(dve.tensor_tensor(out=chosen2, in0=chosen, in1=w12[:, 2:4, :].unsqueeze(3).to_broadcast(
                        [P, TOP, TILES, EXPERTS]), op=ALU.mult))
                    dve.tensor_tensor(out=wtv, in0=chosen2[:, 0, :, :], in1=chosen2[:, 1, :, :],
                                      op=ALU.add).then_inc(wt_ready, 1)
                    dve.wait_ge(place_ps, 1)
                    dve.wait_ge(wt_ready, 1)
                    ch.link(dve.tensor_copy(scan[0][:, SCAN:, :], psC[:, 1, :, :]))
                    src, dst = scan
                    for d in (1, 2, 4, 8, 16):
                        ch.link(dve.tensor_tensor(out=dst[:, SCAN:, :], in0=src[:, SCAN:, :],
                                                  in1=src[:, SCAN - d:SCAN - d + TILES, :], op=ALU.add))
                        src, dst = dst, src
                    total = src[:, SCAN + TILES - 1, :]
                    ch.link(dve.tensor_tensor(out=place, in0=psC[:, 0, :, :], in1=src[:, SCAN - 1:SCAN - 1 + TILES, :],
                                              op=ALU.add))
                    ch.link(dve.tensor_tensor(out=place, in0=place, in1=first_slot.unsqueeze(1).to_broadcast(
                        [P, TILES, EXPERTS]), op=ALU.add))
                    ch.link(dve.tensor_tensor(out=chosen2, in0=chosen, in1=place.unsqueeze(1).to_broadcast(
                        [P, TOP, TILES, EXPERTS]), op=ALU.mult))
                    ch.link(dve.tensor_reduce(out=slot_f, in_=chosen2, axis=AX.X, op=ALU.add))
                    dve.tensor_copy(slot_i, slot_f.rearrange("p k t -> p (k t)")).then_inc(slots_ready, 1)
                    ch.link(dve.tensor_tensor(out=fill_f, in0=fill_first, in1=total, op=ALU.add))
                    dve.tensor_copy(fill_i, fill_f).then_inc(fill_ready, 1)
                    ch.link(dve.tensor_tensor(out=block_used, in0=block_first, in1=total.unsqueeze(2).to_broadcast(
                        [P, EXPERTS, BLOCKS_E]), op=ALU.is_lt))
                    ch.link(dve.tensor_reduce(out=ends[0][:, 4:], in_=block_used, axis=AX.X, op=ALU.add))
                    ch.link(dve.tensor_scalar(unused, ends[0][:, 4:], -1.0, float(BLOCKS_E), ALU.mult, ALU.add))
                    src, dst = ends
                    for d in (1, 2, 4):
                        ch.link(dve.tensor_tensor(out=dst[:, 4:], in0=src[:, 4:], in1=src[:, 4 - d:4 - d + EXPERTS],
                                                  op=ALU.add))
                        src, dst = dst, src
                    ch.link(dve.tensor_tensor(out=past, in0=step_no, in1=src[:, 4:].unsqueeze(1).to_broadcast(
                        [P, STEPS, EXPERTS]), op=ALU.is_ge))
                    ch.link(dve.tensor_tensor(out=past_unused, in0=past, in1=unused.unsqueeze(1).to_broadcast(
                        [P, STEPS, EXPERTS]), op=ALU.mult))
                    ch.link(dve.tensor_reduce(out=step_f[:, 0, :], in_=past, axis=AX.X, op=ALU.add))
                    ch.link(dve.tensor_reduce(out=step_f[:, 1, :], in_=past_unused, axis=AX.X, op=ALU.add))
                    dve.tensor_scalar(plan[0:1, 0, :], step_f[0:1, 0, :], float(EXPERTS - 1), None, ALU.min)
                    dve.tensor_tensor(out=plan[0:1, 1, :], in0=step_f[0:1, 1, :], in1=step_no[0:1, :, 0], op=ALU.add)
                    for g, (t0, n) in enumerate(groups):
                        dve.wait_ge(bz_ps, g + 1)
                        dve.tensor_tensor(out=xs[:, t0:t0 + n, :], in0=psZ[g % 2][:, 0:n * P].rearrange(
                            "p (t d) -> p t d", t=n), in1=xs[:, t0:t0 + n, :], op=ALU.add).then_inc(x_done, 1)

        with ExitStack() as c7:
            def ps(name, shape, dt=F32):
                return c7.enter_context(nc.psum_tensor(name, shape, dt))

            def sem7(name):
                return c7.enter_context(nc.semaphore(name))

            o = 0

            def part(n):
                nonlocal o
                o += n
                assert o <= WORK
                return work[:, o - n:o]

            psX = [ps(f"psX{k}", [P, 512]) for k in range(2)]
            psH = [ps(f"psH{k}", [P, 512]) for k in range(2)]
            psY = [ps(f"psY{k}", [P, 512]) for k in range(2)]
            xl = [part(XW) for _ in range(XBUFS)]
            xT = [part(P) for _ in range(2)]
            w1c = [part(HID) for _ in range(WBUFS)]
            w2c = [part(HC * D).rearrange("p (c d) -> p c d", c=HC) for _ in range(WBUFS)]
            b1c = [part(HC) for _ in range(WBUFS)]
            act_h = [part(HC * P).rearrange("p (c n) -> p c n", c=HC) for _ in range(2)]
            ysc = [part(D) for _ in range(XBUFS)]
            T_ps, xT_ready, w_ready, h_ps, h_ready, y_ps, y_scaled, y_seen = (
                sem7(n) for n in ("T_ps7", "xT_ready7", "w_ready7", "h_ps7", "h_ready7", "y_ps7", "y_scaled7",
                                  "y_seen7"))
            x_in = [sem7(f"slots_in{b}") for b in range(XBUFS)]
            GT = 7
            back = [(t, min(GT, TILES - t)) for t in range(0, TILES, GT)]
            y_in = [sem7(f"y_in{g}") for g in range(len(back))]
            added, stored = sem7("added7"), sem7("stored7")
            yb = [region[:, k * ROWS:(k + 1) * ROWS].rearrange("p (t d) -> p t d", d=D) for k in range(TOP)]
            TURNS7 = STEPS // XBUFS - 1
            FIRST = 3

            def steps(eng, step):
                for s in range(-1, FIRST):
                    step(s, s, 0)
                with eng.Fori(0, TURNS7) as i:
                    for n in range(FIRST, FIRST + XBUFS):
                        step(i * XBUFS + n, n, i)
                for s in range(FIRST + TURNS7 * XBUFS, STEPS + 1):
                    step(s, s, 0)

            def there(s):
                return not isinstance(s, int) or 0 <= s < STEPS

            def above(eng, sem, count):
                if not isinstance(count, int) or count > 0:
                    eng.wait_ge(sem, count)

            with nc.Block() as block:
                @block.sync
                def _(sp):
                    def load(s, b):
                        no = sp.value_load(plan[0:1, 1, s:s + 1] if isinstance(s, int) else
                                           plan[0:1, 1, bass.ds(s, 1)], min_val=0, max_val=BLOCKS - 1)
                        sp.dma_start(xl[b], slot_blocks[bass.ds(no, 1), :, :].rearrange("o p w -> p (o w)")
                                     ).then_inc(x_in[b], 16)

                    for b in range(XBUFS):
                        load(b, b)
                    with sp.Fori(0, STEPS // XBUFS - 1) as i:
                        for b in range(XBUFS):
                            sp.wait_ge(y_out[b], i * 16 + 16)
                            sp.sem_inc(y_seen, 1)
                            load((i + 1) * XBUFS + b, b)
                    for b in range(XBUFS):
                        sp.wait_ge(y_out[b], 16 * (STEPS // XBUFS))
                    for g, (t0, n) in enumerate(back):
                        for k in range(TOP):
                            first = k * ROWS + t0 * P
                            sp.dma_start(yb[k][:, t0:t0 + n, :], expert_out[first:first + n * P, :].rearrange(
                                "(t p) d -> p t d", p=P)).then_inc(y_in[g], 16)
                    for g, (t0, n) in enumerate(back):
                        sp.wait_ge(added, TOP * (g + 1))
                        full = min(t0 + n, NODES // P)
                        sp.dma_start(out[t0 * P:full * P, :].rearrange("(t p) d -> p t d", p=P),
                                     xs[:, t0:full, :]).then_inc(stored, 16)
                    sp.dma_start(out[full * P:NODES, :], xs[0:NODES - full * P, full, :]).then_inc(stored, 16)
                    sp.wait_ge(stored, 16 * (len(back) + 1))

                @block.gpsimd
                def _(pool):
                    with pool.Fori(0, STEPS // XBUFS) as i:
                        for b in range(XBUFS):
                            pool.wait_ge(y_scaled, i * XBUFS + b + 1)
                            pool.sem_inc(y_seen, 1)
                            pool.indirect_dma_start(
                                out=expert_out, out_offset=bass.IndirectOffsetOnAxis(
                                    ap=xl[b][:, D:D + 1].bitcast(U32), axis=0),
                                in_=ysc[b], in_offset=None).then_inc(y_out[b], 16)

                @block.tensor
                def _(pe):
                    def step(s, n, turn):
                        if there(s + 1):
                            b = (n + 1) % XBUFS
                            pe.wait_ge(x_in[b], (turn + (n + 1) // XBUFS) * 16 + 16)
                            above(pe, xT_ready, s)
                            pe.transpose(psX[(n + 1) % 2][:, 0:P], xl[b][:, 0:D], ident[:]).then_inc(T_ps, 1)
                        if there(s):
                            pe.wait_ge(w_ready, s * 3 + 3)
                            pe.wait_ge(xT_ready, s + 1)
                            above(pe, h_ready, s - 1)
                            for c in range(HC):
                                last = pe.matmul(psH[n % 2][:, c * P:(c + 1) * P],
                                                 w1c[n % WBUFS][:, c * P:(c + 1) * P], xT[n % 2],
                                                 start=True, stop=True)
                            last.then_inc(h_ps, 1)
                        if there(s - 1):
                            m = n - 1
                            pe.wait_ge(h_ready, s)
                            above(pe, y_scaled, s - 2)
                            for c in range(HC):
                                last = pe.matmul(psY[m % 2][:, 0:D], act_h[m % 2][:, c, :], w2c[m % WBUFS][:, c, :],
                                                 start=(c == 0), stop=(c == HC - 1))
                            last.then_inc(y_ps, 1)

                    steps(pe, step)

                @block.scalar
                def _(act):
                    def step(s, n, turn):
                        if there(s):
                            above(act, y_ps, s - 1)
                            act.wait_ge(h_ps, s + 1)
                            for c in range(HC):
                                last = act.activation(act_h[n % 2][:, c, :], psH[n % 2][:, c * P:(c + 1) * P],
                                                      ACT.Gelu, bias=b1c[n % WBUFS][:, c:c + 1])
                            last.then_inc(h_ready, 1)

                    steps(act, step)

                @block.vector
                def _(dve):
                    def step(s, n, turn):
                        if there(s + 1):
                            no = dve.value_load(plan[0:1, 0, s + 1:s + 2] if isinstance(s, int) else
                                                plan[0:1, 0, bass.ds(s + 1, 1)], min_val=0, max_val=EXPERTS - 1)
                            w = (n + 1) % WBUFS
                            above(dve, y_ps, s - 1)
                            dve.tensor_copy(w1c[w].unsqueeze(1), W1_s[:, bass.ds(no, 1), :]).then_inc(w_ready, 1)
                            dve.tensor_copy(w2c[w], W2_s[:, bass.ds(no * HC, HC), :]).then_inc(w_ready, 1)
                            dve.tensor_copy(b1c[w], b1g[:, bass.ds(no * HC, HC)]).then_inc(w_ready, 1)
                            dve.wait_ge(T_ps, s + 2)
                            above(dve, h_ps, s)
                            dve.tensor_copy(xT[(n + 1) % 2], psX[(n + 1) % 2][:, 0:P]).then_inc(xT_ready, 1)
                        if there(s - 1):
                            b = (n - 1) % XBUFS
                            dve.wait_ge(y_ps, s)
                            dve.tensor_scalar(ysc[b], psY[(n - 1) % 2][:, 0:D], xl[b][:, D + 1:XW], None,
                                              ALU.mult).then_inc(y_scaled, 1)

                    steps(dve, step)
                    for g, (t0, n) in enumerate(back):
                        dve.wait_ge(y_in[g], 32)
                        for k in range(TOP):
                            if k:
                                dve.wait_ge(added, TOP * g + k)
                            dve.tensor_tensor(out=xs[:, t0:t0 + n, :], in0=xs[:, t0:t0 + n, :],
                                              in1=yb[k][:, t0:t0 + n, :], op=ALU.add).then_inc(added, 1)


def kernel(**inputs):
    import numpy as np
    import concourse.bacc as _bacc
    from concourse import mybir as _mybir
    from concourse.bass_utils import run_bass_kernel_spmd as _run

    src = {k: np.asarray(v) for k, v in inputs.items()}
    adj = src["adj"]
    adjT = np.zeros((ROWS, ROWS), adj.dtype)
    adjT[:NODES, :NODES] = adj.T
    x = np.zeros((ROWS, D), src["x"].dtype)
    x[:NODES] = src["x"]
    dg = np.zeros(ROWS, adj.dtype)
    dg[:NODES] = np.diagonal(adj)
    g = {k[len("L0_gnn_"):]: v for k, v in src.items() if k.startswith("L0_gnn_")}
    f = {k[len("L0_ffn_"):]: v for k, v in src.items() if k.startswith("L0_ffn_")}
    gru = [g[n] for n in ("edge_Wih", "edge_Whh", "node_Wih", "node_Whh")]
    bias = [g[n] for n in ("edge_bih", "edge_bhh", "node_bih", "node_bhh")]
    laid = {
        "x": x, "adjT": adjT, "diag": dg.reshape(TILES, P).T,
        "gatW": g["gat_W"].transpose(1, 0, 2), "gatWT": g["gat_W"].transpose(2, 0, 1),
        "gata": g["gat_a"].reshape(HEADS, 2, D).transpose(2, 0, 1),
        "gruw": np.stack([w.T for w in gru], axis=1),
        "grub": np.stack([b.reshape(3, D).T for b in bias], axis=1),
        "Wr": f["Wr"], "br": f["br"], "lng": f["ln_g"].T, "lnb": f["ln_b"].T,
        "W1": f["W1"].transpose(1, 0, 2), "b1": f["b1"].reshape(EXPERTS, HC, P).transpose(2, 0, 1),
        "W2": f["W2"].reshape(EXPERTS * HC, P, D).transpose(1, 0, 2), "b2": f["b2"],
    }
    nc = _bacc.Bacc("TRN2", target_bir_lowering=False, num_devices=1)
    arrays, args = {}, []
    for name, a in laid.items():
        a = np.ascontiguousarray(a)
        arrays[f"in_{name}"] = a
        args.append(nc.dram_tensor(f"in_{name}", a.shape, _mybir.dt.from_np(a.dtype), kind="ExternalInput").ap())
    args.append(nc.dram_tensor("out_0", (NODES, D), _mybir.dt.float32, kind="ExternalOutput").ap())
    gnn_moe(nc, *args)
    r = _run(nc, [arrays], core_ids=[0])
    return r.results[0]["out_0"]
```

```python
from contextlib import ExitStack

import concourse.bass as bass
import numpy as np
from concourse import mybir

F32 = mybir.dt.float32
BF16 = mybir.dt.bfloat16
U32 = mybir.dt.uint32
I32 = mybir.dt.int32
ALU = mybir.AluOpType
ACT = mybir.ActivationFunctionType
AX = mybir.AxisListType

P = 128
NODES = 3327
TILES = (NODES + P - 1) // P
ROWS = TILES * P
PAD = ROWS - 1
D = 128
HEADS = 3
ALPHA = 0.2
NEG_INF = -9000000000000000.0
EPS = 1e-05
U = 2 * HEADS
PARTS = 3
TW = D + 2 * HEADS + 2
SEG = 4
QUAD = 32
SEG_FIRST = [0, 7, 14, 20, 26]
SEG_COLS = 7 * P
SEG_CAP = P + QUAD
CHUNKS = SEG_CAP * SEG // P
SLOTS = CHUNKS * P
ROUNDS = SEG_CAP // 8
UCOLS = PARTS * U + 1
BUFS = 4
DEPTH = 6
ZBUFS = 3
SUM_COLS = P // 2
LOOPED = TILES // BUFS * BUFS
FIRST_CHUNKS = TILES - LOOPED
ZC = HEADS * SLOTS
HR = HEADS * P
GB = 416
GBLOCKS = ROWS // GB
EXPERTS = 8
HID = 512
HC = HID // P
TOP = 2
BLOCKS_E = TILES + 1
SPARE = EXPERTS
STEPS = TOP * TILES + EXPERTS
XW = D + 2
XBUFS = 12
WBUFS = 3
SCAN = 16


class Chain:

    def __init__(self, eng, sem):
        self.eng, self.sem, self.base, self.n, self.turn, self.per = eng, sem, 0, 0, None, 0

    def loop(self, turn, per):
        self.base, self.n, self.turn, self.per = self.base + self.n, 0, turn, per

    def done(self, turns):
        assert self.n == self.per, (self.n, self.per)
        self.base, self.n, self.turn = self.base + turns * self.per, 0, None

    def link(self, ins):
        self.n += 1
        ins.then_inc(self.sem, 1)
        count = self.base + self.n
        if self.turn is not None:
            count = self.turn * self.per + count
        self.eng.wait_ge(self.sem, count)


def gnn_moe(nc, x, adjT, diag, gatW, gatWT, gata, gruw, grub, Wr, br, lng, lnb, W1, b1, W2, b2, out, dbg=None):
    adj_chunks = adjT.rearrange("(c p) r -> c p r", p=P)
    adj_rows = adjT.rearrange("c (t r) -> (c t) r", r=P)
    table = nc.dram_tensor("neighbour_table", (ROWS, TW), F32, kind="Internal").ap()
    BLOCKS = EXPERTS * BLOCKS_E + SPARE
    slots = nc.dram_tensor("slots", (BLOCKS * P, XW), F32, kind="Internal").ap()
    slot_blocks = slots.rearrange("(b p) w -> b p w", p=P)
    expert_out = nc.dram_tensor("expert_out", (TOP * ROWS + 2 * SPARE * P, D), F32, kind="Internal").ap()

    with ExitStack() as ctx:
        def sb(name, shape, dt=F32):
            return ctx.enter_context(nc.sbuf_tensor(name, shape, dt))

        def sem(name):
            return ctx.enter_context(nc.semaphore(name))

        xs = sb("xs", [P, TILES, D])
        hT = sb("hT", [P, ROWS])
        tab = sb("tab", [P, TILES, TW])
        h = tab[:, :, 0:D]
        dg = sb("dg", [P, TILES])
        ident = sb("ident", [P, P])
        identb = sb("identb", [P, P], BF16)
        notid = sb("notid", [P, P])
        ones = sb("ones", [P, P])
        gatW_s = sb("gatW_s", [P, HEADS, D])
        gatWT_s = sb("gatWT_s", [P, HEADS, D])
        gata_s = sb("gata_s", [P, HEADS, 2])
        gruw_s = sb("gruw_s", [P, 4, 3 * D])
        grub_s = sb("grub_s", [P, 4, 3])
        gbias = sb("gbias", [P, 2, 2])
        Wr_s = sb("Wr_s", [P, EXPERTS])
        br_s = sb("br_s", [P, EXPERTS])
        lng_s = sb("lng_s", [P, EXPERTS])
        lnb_s = sb("lnb_s", [P, EXPERTS])
        W1_s = sb("W1_s", [P, EXPERTS, HID])
        b1_s = sb("b1_s", [P, EXPERTS, HC])
        W2_s = sb("W2_s", [P, EXPERTS * HC, D])
        b2_s = sb("b2_s", [EXPERTS, D])
        region = sb("region", [P, 4 * ROWS])
        masks = region[:, 2 * ROWS:4 * ROWS].bitcast(BF16)
        pos = [masks[:, b * ROWS:(b + 1) * ROWS] for b in range(2)]
        sgn = [masks[:, (2 + b) * ROWS:(3 + b) * ROWS] for b in range(2)]
        num = region[:, :].rearrange("p (q r) -> p q r", q=4)
        WORK = 13312
        work = sb("work", [P, WORK])
        at = [region[:, b * ROWS:(b + 1) * ROWS] for b in range(2)] + [
            work[:, (1 + b) * ROWS:(2 + b) * ROWS] for b in range(2)]
        anyw = work[:, 0:TILES * (64 + 32 + 16) // 2].bitcast(BF16)
        gts = sb("gts", [P, 1, CHUNKS, TW])
        at_in = [sem(f"at_in{b}") for b in range(BUFS)]
        stat = sb("stat", [P, 6, TILES])
        b1g = sb("b1g", [P, EXPERTS * HC])
        moments = sb("moments", [P, TILES, 6])
        meanvar = sb("meanvar", [P, TILES, 2])
        V = sb("V", [P, U])
        u32_ = sb("u_f", [P, TILES, U])
        urest = sb("u_rest", [P, TILES, U])
        uparts = sb("u_parts", [P, TILES, UCOLS], BF16)
        anyc = sb("anyc", [P, TILES, TILES])
        cidx = sb("cidx", [P, TILES, CHUNKS])
        crel = sb("crel", [P, TILES, CHUNKS])
        idx_tab = sb("idx_tab", [P, TILES, CHUNKS], U32)
        idx_adj = sb("idx_adj", [P, TILES, CHUNKS], U32)
        coliota = sb("coliota", [P, P])
        flag = sb("flag", [1, 1], I32)
        y_out = [sem(f"y_out{b}") for b in range(XBUFS)]
        plan = sb("plan", [1, 2, STEPS], I32)
        zeros = sb("zeros", [P, 512], BF16)

        done_with = []

        with ExitStack() as c2:
            def ps(name, shape, dt=F32):
                return c2.enter_context(nc.psum_tensor(name, shape, dt))

            def sem2(name):
                done_with.append(c2.enter_context(nc.semaphore(name)))
                return done_with[-1]

            psP = ps("psP", [P, TILES, UCOLS])
            psS = ps("psS", [P, TILES, UCOLS])
            undiag, pos_ready, sgn_ready, any_done, pe_used, tree = (
                sem2("undiag"), sem2("pos_ready"), sem2("sgn_ready"), sem2("any_done"), sem2("pe_used"), sem2("tree"))
            TREE = 3
            with ExitStack() as c1:
                def ps1(name, shape, dt=F32):
                    return c1.enter_context(nc.psum_tensor(name, shape, dt))

                def sem1(name):
                    done_with.append(c1.enter_context(nc.semaphore(name)))
                    return done_with[-1]

                psT = [ps1(f"psT{k}", [P, 512]) for k in range(2)]
                psU = ps1("psU", [P, TILES, U])
                psV = ps1("psV", [P, U])
                x_in, gw_in = sem1("x_in"), sem1("gw_in")
                consts, dve_c = sem1("consts"), sem1("dve_c1")
                vared, stdev, h_ready = sem1("vared"), sem1("stdev"), sem1("h_ready")
                group_T, hT_ready, V_ps, V_ready, u_ps = (
                    sem1("group_T"), sem1("hT_ready"), sem1("V_ps"), sem1("V_ready"), sem1("u_ps"))
                iotas, parts_ready = sem1("iotas1"), sem1("parts_ready")
                groups = [(t, min(4, TILES - t)) for t in range(0, TILES, 4)]

                def normalize_sync(sp):
                    sp.dma_start(xs[:], x.rearrange("(t p) d -> p t d", p=P)).then_inc(x_in, 16)
                    sp.dma_start(gatWT_s[:], gatWT).then_inc(gw_in, 16)
                    sp.dma_start(gata_s[:], gata).then_inc(gw_in, 16)
                    for b in range(BUFS):
                        sp.dma_start(at[b], adj_chunks[b, :, :]).then_inc(at_in[b], 16)

                def normalize_gpsimd(pool):
                    pool.memset(ident[:], 0.0).then_inc(iotas, 1)
                    pool.memset(identb[:], 0.0).then_inc(iotas, 1)
                    pool.memset(notid[:], 1.0).then_inc(iotas, 1)
                    pool.wait_ge(iotas, 3)
                    for tile, fill in ((ident, 1.0), (identb, 1.0), (notid, 0.0)):
                        pool.affine_select(out=tile[:], in_=tile[:], compare_op=ALU.not_equal, fill=fill, base=0,
                                           pattern=[[-1, P]], channel_multiplier=1).then_inc(consts, 1)
                    pool.memset(ones[:], 1.0).then_inc(consts, 1)
                    pool.memset(zeros[:], 0.0).then_inc(consts, 1)
                    pool.memset(tab[:, :, D:TW], 0.0).then_inc(consts, 1)
                    pool.memset(uparts[:, :, PARTS * U:UCOLS], 1.0).then_inc(consts, 1)
                    pool.iota(coliota[:], pattern=[[1, P]], base=0, channel_multiplier=0,
                              allow_small_or_imprecise_dtypes=True).then_inc(consts, 1)

                def normalize_vector(dve):
                    ch = Chain(dve, dve_c)
                    dve.wait_ge(x_in, 16)
                    for t in range(TILES):
                        last = dve.bn_stats(out=moments[:, t, :], in_=xs[:, t, :])
                    ch.link(last)
                    for t in range(TILES):
                        last = dve.bn_aggr(out=meanvar[:, t, :], in_=moments[:, t, :])
                    ch.link(last)
                    dve.tensor_scalar(stat[:, 3, :], meanvar[:, :, 1], EPS, None, ALU.add).then_inc(vared, 1)
                    dve.wait_ge(stdev, 1)
                    ch.link(dve.reciprocal(stat[:, 5, :], stat[:, 4, :]))
                    for g, (t0, n) in enumerate(groups):
                        for t in range(t0, t0 + n):
                            last = dve.tensor_scalar(tab[:, t, 0:D], xs[:, t, :], meanvar[:, t, 0:1],
                                                     stat[:, 5, t:t + 1], ALU.subtract, ALU.mult)
                        last.then_inc(h_ready, 1)
                    dve.wait_ge(V_ps, 1)
                    dve.tensor_copy(V[:], psV[:]).then_inc(V_ready, 1)
                    return ch

                def u_parts(dve, ch):
                    dve.wait_ge(u_ps, 1)
                    ch.link(dve.tensor_copy(u32_[:], psU[:]))
                    src = u32_
                    for k in range(PARTS):
                        part = uparts[:, :, k * U:(k + 1) * U]
                        ch.link(dve.tensor_copy(part, src[:]))
                        if k < PARTS - 1:
                            ch.link(dve.tensor_tensor(out=urest[:], in0=src[:], in1=part, op=ALU.subtract))
                            src = urest
                    dve.sem_inc(parts_ready, 1)

                def normalize_scalar(act):
                    act.wait_ge(vared, 1)
                    act.activation(stat[:, 4, :], stat[:, 3, :], ACT.Sqrt).then_inc(stdev, 1)
                    for g, (t0, n) in enumerate(groups):
                        act.wait_ge(group_T, g + 1)
                        act.copy(hT[:, t0 * P:(t0 + n) * P], psT[g % 2][:, 0:n * P]).then_inc(hT_ready, 1)

                def normalize_tensor(pe):
                    pe.wait_ge(gw_in, 32)
                    for i in range(HEADS):
                        last = pe.matmul(psV[:, 2 * i:2 * i + 2], gatWT_s[:, i, :], gata_s[:, i, :], start=True,
                                         stop=True)
                    last.then_inc(V_ps, 1)
                    for g, (t0, n) in enumerate(groups):
                        pe.wait_ge(h_ready, g + 1)
                        if g >= 2:
                            pe.wait_ge(hT_ready, g - 1)
                        for t in range(n):
                            last = pe.transpose(psT[g % 2][:, t * P:(t + 1) * P], tab[:, t0 + t, 0:D], ident[:])
                        last.then_inc(group_T, 1)
                    pe.wait_ge(V_ready, 1)
                    pe.wait_ge(hT_ready, len(groups))
                    for t in range(TILES):
                        last = pe.matmul(psU[:, t, :], hT[:, t * P:(t + 1) * P], V[:], start=True, stop=True)
                    last.then_inc(u_ps, 1)

                with nc.Block() as block:
                    def over_chunks(eng, step):
                        with eng.Fori(0, LOOPED // BUFS) as i:
                            for n in range(FIRST_CHUNKS, FIRST_CHUNKS + BUFS):
                                step(i * BUFS + n, n % BUFS)

                    def first_chunks(step):
                        for c in range(FIRST_CHUNKS):
                            step(c, c)

                    @block.sync
                    def _(sp):
                        def load(c, b):
                            sp.wait_ge(pos_ready, c + 1)
                            sp.wait_ge(sgn_ready, c + 1)
                            src = adj_chunks[c + BUFS:c + BUFS + 1, :, :] if isinstance(c, int) else \
                                adj_chunks[bass.ds(c + BUFS, 1), :, :]
                            sp.dma_start(at[b], src.rearrange("o p r -> p (o r)")).then_inc(at_in[b], 16)

                        normalize_sync(sp)
                        with sp.Fori(0, LOOPED // BUFS - 1) as i:
                            for b in range(BUFS):
                                load(i * BUFS + b, b)
                        for c in range(LOOPED - BUFS, TILES - BUFS):
                            load(c, c % BUFS)

                    @block.gpsimd
                    def _(pool):
                        def step(c, b):
                            turn = c // BUFS if isinstance(c, int) else None
                            if turn is None:
                                pool.wait_ge(at_in[b], (c - b) * (16 // BUFS) + 16)
                            else:
                                pool.wait_ge(at_in[b], 16 * turn + 16)
                            dblock = at[b][:, bass.ds(c * P, P)]
                            pool.tensor_tensor(out=dblock, in0=dblock, in1=notid[:], op=ALU.mult).then_inc(undiag, 1)

                        normalize_gpsimd(pool)
                        pool.wait_ge(consts, 8)
                        first_chunks(step)
                        over_chunks(pool, step)

                    @block.vector
                    def _(dve):
                        def step(c, b):
                            dve.wait_ge(undiag, c + 1)
                            dve.wait_ge(pe_used, c + 1)
                            dve.tensor_scalar(pos[b % 2], at[b], 0.0, None, ALU.is_gt).then_inc(pos_ready, 1)
                            dve.wait_ge(pos_ready, c + 1)
                            src, w, o = pos[b % 2].rearrange("p (t r) -> p t r", r=P), P, 0
                            for k in range(TREE):
                                w //= 2
                                dst = anyw[:, o:o + TILES * w].rearrange("p (t r) -> p t r", r=w)
                                o += TILES * w
                                dve.tensor_tensor(out=dst, in0=src[:, :, 0:w], in1=src[:, :, w:2 * w],
                                                  op=ALU.max).then_inc(tree, 1)
                                dve.wait_ge(tree, c * TREE + k + 1)
                                src = dst
                            dve.tensor_reduce(out=anyc[:, bass.ds(c, 1), :].rearrange("p o t -> p (o t)"), in_=src,
                                              axis=AX.X, op=ALU.max).then_inc(any_done, 1)

                        ch = normalize_vector(dve)
                        first_chunks(step)
                        u_parts(dve, ch)
                        over_chunks(dve, step)

                    @block.scalar
                    def _(act):
                        def step(c, b):
                            act.wait_ge(undiag, c + 1)
                            act.wait_ge(pe_used, c + 1)
                            act.activation(sgn[b % 2], at[b], ACT.Sign).then_inc(sgn_ready, 1)

                        normalize_scalar(act)
                        first_chunks(step)
                        over_chunks(act, step)

                    @block.tensor
                    def _(pe):
                        pe.wait_ge(consts, 8)
                        for bank in (psP, psS):
                            pe.matmul(bank[:].rearrange("p t u -> p (t u)"), zeros[:, 0:P], zeros[:, 0:TILES * UCOLS],
                                      start=True, stop=False, skip_group_check=True)
                        pe.sem_inc(pe_used, 2)

                        def step(c, b):
                            parts = uparts[:, bass.ds(c, 1), :].rearrange("p o u -> p (o u)")
                            for bank, mask, ready in ((psP, pos, pos_ready), (psS, sgn, sgn_ready)):
                                pe.wait_ge(ready, c + 1)
                                for t in range(TILES):
                                    last = pe.matmul(bank[:, t, :], mask[b % 2][:, t * P:(t + 1) * P], parts,
                                                     start=False, stop=False, skip_group_check=True)
                            last.then_inc(pe_used, 1)

                        normalize_tensor(pe)
                        pe.wait_ge(parts_ready, 1)
                        first_chunks(step)
                        over_chunks(pe, step)

            psK = ps("psK", [P, 2 * 512])
            psI = ps("psI", [P, SEG_CAP])
            psF = ps("psF", [1, 1])
            psB = ps("psB", [P, EXPERTS * HC])
            pneg = work[:, 0:3 * TILES * U].rearrange("p (k t u) -> p k t u", k=3, t=TILES)
            counts = work[:, 470:470 + TILES]
            counts2 = work[:, 496:496 + 1]
            anyb = work[:, 512:512 + TILES * QUAD // 2].bitcast(BF16).rearrange("p (c q) -> p c q", q=QUAD)
            keys = work[:, 1024:1024 + SEG_COLS]
            keyiota = work[:, 2048:2048 + SEG_COLS]
            top = work[:, 3072:3072 + SEG_CAP]
            lists = work[:, 3328:3328 + SEG_CAP]
            padz = work[:, 3584:3584 + SEG_CAP]
            left = work[:, 3840:3848]
            segb = work[:, 3848:3850]
            leftf = work[:, 3850:3851]
            tileiota = work[:, 3900:3900 + TILES * CHUNKS].rearrange("p (t k) -> p t k", k=CHUNKS)
            scaled = work[:, 4100:4100 + TILES * CHUNKS].rearrange("p (t k) -> p t k", k=CHUNKS)
            b1_ps, up_in, w_in = sem2("b1_ps"), sem2("up_in"), sem2("w_in")
            made, dve_c, any_t, keys_ps, lists_ready, lists_ps, e_ready, stored, over, over_ps = (
                sem2("made"), sem2("dve_c3"), sem2("any_t"), sem2("keys_ps"), sem2("lists_ready"), sem2("lists_ps"),
                sem2("e_ready"), sem2("stored"), sem2("over"), sem2("over_ps"))
            with nc.Block() as block:
                @block.sync
                def _(sp):
                    def bring(pairs, done):
                        for dst, src in pairs:
                            sp.dma_start(dst[:], src).then_inc(done, 16)

                    bring(((W1_s, W1), (lng_s, lng), (lnb_s, lnb), (b1_s, b1)), up_in)
                    sp.wait_ge(e_ready, 1)
                    sp.dma_start(table.rearrange("(t p) w -> p t w", p=P), tab[:]).then_inc(stored, 16)
                    bring(((dg, diag), (gatW_s, gatW), (gruw_s, gruw), (grub_s, grub), (Wr_s, Wr), (W2_s, W2),
                           (b2_s, b2)), w_in)
                    sp.dma_start(br_s[:], br.partition_broadcast(P)).then_inc(w_in, 16)
                    sp.wait_ge(stored, 16)
                    sp.wait_ge(w_in, 16 * 8)

                @block.gpsimd
                def _(pool):
                    pool.iota(keyiota, pattern=[[1, SEG_COLS]], base=1, channel_multiplier=0,
                              allow_small_or_imprecise_dtypes=True).then_inc(made, 1)
                    pool.iota(tileiota, pattern=[[1, TILES], [0, CHUNKS]], base=0, channel_multiplier=0,
                              allow_small_or_imprecise_dtypes=True).then_inc(made, 1)
                    pool.wait_ge(b1_ps, 1)
                    for e in range(EXPERTS):
                        pool.tensor_scalar(W1_s[:, e, :], W1_s[:, e, :], lng_s[:, e:e + 1], None,
                                           ALU.mult).then_inc(made, 1)

                @block.vector
                def _(dve):
                    ch = Chain(dve, dve_c)
                    dve.memset(anyb, 0.0)
                    for s in range(SEG):
                        q = slice(s * QUAD, (s + 1) * QUAD)
                        dve.memset(segb[q, 0:1], float(SEG_FIRST[s] * P - 1))
                        dve.memset(segb[q, 1:2], float(PAD + 1 - SEG_FIRST[s] * P))
                    ch.link(dve.memset(keys[64:P, 6 * P:7 * P], 0.0))
                    dve.tensor_scalar(anyb[:, :, 0:TILES], anyc[:], 0.0, None, ALU.is_gt).then_inc(any_t, 1)
                    by_part = "p t (k u) -> p t u k"
                    for k, bank in enumerate((psP, psS)):
                        ch.link(dve.tensor_reduce(out=pneg[:, k], in_=bank[:, :, 0:PARTS * U].rearrange(
                            by_part, k=PARTS), axis=AX.X, op=ALU.add))
                    ch.link(dve.tensor_copy(counts.unsqueeze(2), psP[:, :, PARTS * U:UCOLS]))
                    ch.link(dve.tensor_tensor(out=counts.unsqueeze(2), in0=counts.unsqueeze(2),
                                              in1=psS[:, :, PARTS * U:UCOLS], op=ALU.subtract))
                    ch.link(dve.tensor_reduce(out=counts2, in_=counts, axis=AX.X, op=ALU.max))
                    ch.link(dve.tensor_tensor(out=pneg[:, 2], in0=pneg[:, 0], in1=pneg[:, 1], op=ALU.subtract))
                    for dst, a, b in ((0, 0, 2), (HEADS, 2, 0)):
                        e = tab[:, :, D + dst:D + dst + HEADS]
                        ch.link(dve.tensor_tensor(out=e, in0=pneg[:, a, :, 0:U:2], in1=pneg[:, b, :, 1:U:2],
                                                  op=ALU.add))
                    e = tab[:, :, D:D + 2 * HEADS]
                    dve.scalar_tensor_tensor(out=e, in0=e, scalar=ALPHA, in1=e, op0=ALU.mult,
                                             op1=ALU.max).then_inc(e_ready, 1)
                    dve.wait_ge(keys_ps, 1)
                    dve.wait_ge(made, 2)
                    dve.tensor_tensor(out=keys[0:64, :], in0=psK[0:64, 0:SEG_COLS], in1=keyiota[0:64, :], op=ALU.mult)
                    ch.link(dve.tensor_tensor(out=keys[64:P, 0:6 * P], in0=psK[64:P, 0:6 * P],
                                              in1=keyiota[64:P, 0:6 * P], op=ALU.mult))
                    for k in range(ROUNDS):
                        eight = top[:, 8 * k:8 * k + 8]
                        ch.link(dve.max(out=eight, in_=keys))
                        ch.link(dve.match_replace(out=keys, in_to_replace=eight, in_values=keys, imm_value=0.0))
                    ch.link(dve.max(out=left, in_=keys))
                    ch.link(dve.tensor_tensor(out=leftf, in0=left[:, 0:1], in1=counts2, op=ALU.max))
                    dve.tensor_scalar(leftf, leftf, 0.0, None, ALU.is_gt).then_inc(over, 1)
                    ch.link(dve.tensor_scalar(padz, top, 0.0, segb[:, 1:2], ALU.is_equal, ALU.mult))
                    dve.scalar_tensor_tensor(out=lists, in0=top, scalar=segb[:, 0:1], in1=padz, op0=ALU.add,
                                             op1=ALU.add).then_inc(lists_ready, 1)
                    dve.wait_ge(b1_ps, 1)
                    dve.tensor_tensor(out=b1g[:], in0=psB[:], in1=b1_s[:].rearrange("p e c -> p (e c)"), op=ALU.add)
                    dve.wait_ge(over_ps, 1)
                    dve.tensor_copy(flag[:], psF[:])
                    dve.wait_ge(lists_ps, 1)
                    ch.link(dve.tensor_copy(cidx[:], psI[:].rearrange("p (k r) -> p r k", r=QUAD)[:, 0:TILES, :]))
                    dve.tensor_copy(idx_tab[:], cidx[:])
                    dve.scalar_tensor_tensor(out=crel[:], in0=tileiota, scalar=-float(P), in1=cidx[:], op0=ALU.mult,
                                             op1=ALU.add)
                    ch.link(dve.tensor_scalar(scaled, cidx[:], float(TILES), None, ALU.mult))
                    dve.tensor_tensor(out=idx_adj[:], in0=scaled, in1=tileiota, op=ALU.add)

                @block.tensor
                def _(pe):
                    pe.wait_ge(any_t, 1)
                    for s in range(SEG):
                        for c in range(SEG_FIRST[s], SEG_FIRST[s + 1]):
                            j = (c - SEG_FIRST[s]) * P
                            last = pe.matmul(psK[s * QUAD:(s + 1) * QUAD, j:j + P], anyb[:, c, :], identb[:],
                                             start=True, stop=True)
                    last.then_inc(keys_ps, 1)
                    pe.wait_ge(up_in, 64)
                    for e in range(EXPERTS):
                        for c in range(HC):
                            last = pe.matmul(psB[:, e * HC + c:e * HC + c + 1], W1_s[:, e, c * P:(c + 1) * P],
                                             lnb_s[:, e:e + 1], start=True, stop=True)
                    last.then_inc(b1_ps, 1)
                    pe.wait_ge(over, 1)
                    pe.matmul(psF[:], leftf, ones[:, 0:1], start=True, stop=True).then_inc(over_ps, 1)
                    pe.wait_ge(lists_ready, 1)
                    pe.transpose(psI[:, 0:P], lists[:, 0:P], ident[:])
                    for s in range(SEG):
                        q = slice(s * QUAD, (s + 1) * QUAD)
                        last = pe.matmul(psI[q, P:SEG_CAP], lists[q, P:SEG_CAP], ident[q, q], start=True, stop=True)
                    last.then_inc(lists_ps, 1)

        with ExitStack() as c4:
            def ps(name, shape, dt=F32):
                return c4.enter_context(nc.psum_tensor(name, shape, dt))

            def sem4(name):
                return c4.enter_context(nc.semaphore(name))

            o = 0

            def carve(*shape):
                nonlocal o
                n = 1
                for s in shape:
                    n *= s
                v = work[:, o:o + n]
                o += n
                return v

            ga = [carve(SLOTS).rearrange("p (k r) -> p k r", k=CHUNKS) for _ in range(DEPTH)]
            z = [carve(ZC).rearrange("p (k i r) -> p k i r", k=CHUNKS, i=HEADS) for _ in range(ZBUFS)]
            offs = carve(SLOTS)
            tree = carve(HR * 2)
            rdenb = carve(HR)
            rden = carve(HEADS)
            negm = carve(HEADS)
            assert o <= WORK, o
            tabf = tab[:].rearrange("p t w -> p (t w)")
            gt = [tabf[:, b * CHUNKS * TW:(b + 1) * CHUNKS * TW].rearrange("p (k w) -> p k w", k=CHUNKS)
                  for b in range(DEPTH - 1)] + [gts[:, 0]]
            crel_s = sb("crel_s", [P, DEPTH, CHUNKS])
            offdiag = [carve(SLOTS // 2).bitcast(BF16) for _ in range(3)]
            stage = sb("stage", [P, DEPTH, 2, CHUNKS], U32)
            zT = ps("zT", [P, 512])
            mB = ps("mB", [P, 512])
            psD = ps("psD", [P, 512])
            rB = ps("rB", [P, 512])
            psN = [ps(f"psN{k}", [P, 512]) for k in range(2)]
            psM = [ps(f"psM{k}", [P, 512]) for k in range(2)]
            (staged, idx_seen, offdiag_ready, az_ready, offs_ready, z_ready, tree_c, top_ready, topT_ready, negm_ready,
             mB_ready, s_ready, exp_ready, den_ready, mul_ready, num_ready, rden_ready, rB_ready,
             rdenb_ready, evac_heads, evac_sum) = (
                 sem4(n) for n in (
                     "staged", "idx_seen", "offdiag_ready", "az_ready", "offs_ready", "z_ready", "tree_c", "top_ready",
                     "topT_ready", "negm_ready", "mB_ready", "s_ready", "exp_ready", "den_ready",
                     "mul_ready", "num_ready", "rden_ready", "rB_ready",
                     "rdenb_ready", "evac_heads", "evac_sum"))
            gathered = [sem4(f"gathered{b}") for b in range(DEPTH)]
            PER_GATHER = 16 * 2 * CHUNKS

            class Tile:

                def __init__(self, t, buf, turn):
                    self.t, self.b, self.turn, self.n = t, buf % DEPTH, turn + buf // DEPTH, buf

                def exists(self):
                    return not isinstance(self.t, int) or 0 <= self.t < TILES

                def plus(self, d):
                    return Tile(self.t + d, self.n + d, self.turn - self.n // DEPTH)

            HEAD_TILES = 2
            TURNS = (TILES - HEAD_TILES - 1) // DEPTH

            def pipeline(eng, step, drain):
                for t in range(HEAD_TILES):
                    step(Tile(t, t, 0))
                with eng.Fori(0, TURNS) as i:
                    for b in range(HEAD_TILES, HEAD_TILES + DEPTH):
                        step(Tile(i * DEPTH + b, b, i))
                for t in range(HEAD_TILES + TURNS * DEPTH, TILES + drain):
                    step(Tile(t, t, 0))

            def sparse_pool(pool):
                def step(x):
                    t, b = x.t, x.b
                    pool.wait_ge(num_ready, t + 1)
                    pool.wait_ge(staged, 3 * t + 3)
                    pool.sem_inc(idx_seen, 1)
                    for k in range(CHUNKS):
                        pool.indirect_dma_start(
                            out=ga[b][:, k, :], out_offset=None, in_=adj_rows,
                            in_offset=bass.IndirectOffsetOnAxis(ap=stage[:, b, 1, k:k + 1], axis=0),
                        ).then_inc(gathered[b], 16)
                        pool.indirect_dma_start(
                            out=gt[b][:, k, :], out_offset=None, in_=table,
                            in_offset=bass.IndirectOffsetOnAxis(ap=stage[:, b, 0, k:k + 1], axis=0),
                        ).then_inc(gathered[b], 16)

                pipeline(pool, step, 0)

            def sparse_vector(dve):
                def fill(x):
                    dve.wait_ge(gathered[x.b], x.turn * PER_GATHER + PER_GATHER)
                    ga_f = ga[x.b].rearrange("p k r -> p (k r)")
                    dve.wait_ge(offdiag_ready, x.t + 1)
                    dve.scalar_tensor_tensor(out=ga_f, in0=offdiag[x.b % 3], scalar=0.0, in1=ga_f, op0=ALU.not_equal,
                                             op1=ALU.mult).then_inc(az_ready, 1)
                    dve.wait_ge(az_ready, x.t + DEPTH + 1)
                    dve.tensor_scalar(offs, ga[x.b].rearrange("p k r -> p (k r)"), 0.0, NEG_INF, ALU.is_equal,
                                      ALU.mult).then_inc(offs_ready, 1)

                def top(x):
                    dve.wait_ge(z_ready, x.t + 1)
                    zz = z[x.b % ZBUFS].rearrange("p k i r -> p (k i r)")
                    pairs = zz[:, 0:4 * HR].rearrange("p (two n) -> p two n", two=2)
                    dve.tensor_tensor(out=tree, in0=pairs[:, 0], in1=pairs[:, 1], op=ALU.max).then_inc(tree_c, 1)
                    dve.wait_ge(tree_c, 2 * x.t + 1)
                    dve.tensor_tensor(out=tree[:, 0:HR], in0=tree[:, 0:HR], in1=tree[:, HR:2 * HR],
                                      op=ALU.max).then_inc(tree_c, 1)
                    dve.wait_ge(tree_c, 2 * x.t + 2)
                    dve.tensor_tensor(out=tree[:, 0:HR], in0=tree[:, 0:HR], in1=zz[:, 4 * HR:5 * HR],
                                      op=ALU.max).then_inc(top_ready, 1)

                def highest(x):
                    dve.wait_ge(mB_ready, x.t + 1)
                    dve.wait_ge(topT_ready, x.t + 1)
                    dve.tensor_reduce(out=negm, in_=zT[:, 0:HR].rearrange("p (i s) -> p i s", i=HEADS), axis=AX.X,
                                      op=ALU.max, negate=True).then_inc(negm_ready, 1)

                def below(x):
                    dve.wait_ge(mB_ready, x.t + 2)
                    flat = z[x.b % ZBUFS].rearrange("p k i r -> p k (i r)")
                    dve.tensor_tensor(out=flat, in0=flat, in1=mB[:, 0:HR].unsqueeze(1).to_broadcast(
                        [P, CHUNKS, HR]), op=ALU.add).then_inc(s_ready, 1)

                def times_adj(x):
                    dve.wait_ge(den_ready, x.t + 1)
                    dve.tensor_tensor(out=z[x.b % ZBUFS], in0=z[x.b % ZBUFS],
                                      in1=ga[x.b].unsqueeze(2).to_broadcast([P, CHUNKS, HEADS, P]),
                                      op=ALU.mult).then_inc(mul_ready, 1)

                def inverse(x):
                    dve.wait_ge(den_ready, x.t + 1)
                    dve.wait_ge(rB_ready, x.t + 1)
                    dve.reciprocal(rden, psD[:, 0:HEADS * SUM_COLS:SUM_COLS]).then_inc(rden_ready, 1)

                def normalize(x):
                    dve.wait_ge(rdenb_ready, x.t + 2)
                    dve.wait_ge(num_ready, x.t + DEPTH + 1)
                    dve.tensor_tensor(out=num[:, 0:HEADS, bass.ds(x.t * P, P)],
                                      in0=psN[x.b % 2][:, 0:HR].rearrange("p (i r) -> p i r", i=HEADS),
                                      in1=rdenb.rearrange("p (i r) -> p i r", i=HEADS),
                                      op=ALU.mult).then_inc(evac_heads, 1)

                dve.sem_inc(az_ready, DEPTH)
                dve.sem_inc(rden_ready, 1)
                dve.sem_inc(evac_heads, 2)
                fill(Tile(0, 0, 0))

                def step(x):
                    for f, d in ((top, 0), (fill, 1), (highest, 0), (inverse, -1), (normalize, -2), (times_adj, -1),
                                 (below, 0)):
                        if x.plus(d).exists():
                            f(x.plus(d))

                pipeline(dve, step, 2)

            def sparse_scalar(act):
                def fill(x):
                    act.wait_ge(offs_ready, x.t + 1)
                    for k in range(CHUNKS):
                        for j in range(HEADS):
                            last = act.activation(z[x.b % ZBUFS][:, k, j, :], offs[:, k * P:(k + 1) * P], ACT.Identity,
                                                  bias=gt[x.b][:, k, D + j:D + j + 1])
                    last.then_inc(z_ready, 1)

                def place_indices(x):
                    tile = bass.ds(x.t, 1)
                    for dst, src in ((stage[:, x.b, 0, :], idx_tab), (stage[:, x.b, 1, :], idx_adj),
                                     (crel_s[:, x.b, :], crel)):
                        act.copy(dst, src[:, tile, :].rearrange("p o k -> p (o k)")).then_inc(staged, 1)

                def from_diag(x):
                    act.wait_ge(staged, 3 * x.t + 3)
                    act.wait_ge(az_ready, x.t + DEPTH - 2)
                    for k in range(CHUNKS):
                        last = act.activation(offdiag[x.b % 3][:, k * P:(k + 1) * P], coliota[:], ACT.Identity,
                                              scale=-1.0, bias=crel_s[:, x.b, k:k + 1])
                    last.then_inc(offdiag_ready, 1)

                def exponential(x):
                    act.wait_ge(s_ready, x.t + 1)
                    act.activation(z[x.b % ZBUFS], z[x.b % ZBUFS], ACT.Exp).then_inc(exp_ready, 1)

                def support(x):
                    act.wait_ge(num_ready, x.t + DEPTH + 1)
                    act.copy(num[:, HEADS, bass.ds(x.t * P, P)], psM[x.b % 2][:, 0:P]).then_inc(evac_sum, 1)

                def inverse(x):
                    act.wait_ge(rB_ready, x.t + 2)
                    act.wait_ge(evac_heads, x.t + 2)
                    act.copy(rdenb, rB[:, 0:HR]).then_inc(rdenb_ready, 1)

                act.sem_inc(evac_sum, 2)
                act.sem_inc(rdenb_ready, 1)
                for dst, src in ((stage[:, :, 0, :], idx_tab), (stage[:, :, 1, :], idx_adj), (crel_s[:], crel)):
                    act.copy(dst, src[:, 0:DEPTH, :]).then_inc(staged, 1)
                act.wait_ge(staged, 3)
                act.sem_inc(staged, 3 * DEPTH - 3)
                from_diag(Tile(0, 0, 0))
                from_diag(Tile(1, 1, 0))
                from_diag(Tile(2, 2, 0))
                fill(Tile(0, 0, 0))

                def step(x):
                    for f, d in ((support, -2), (fill, 1), (inverse, -1), (exponential, 0), (from_diag, 3),
                                 (place_indices, DEPTH)):
                        if x.plus(d).exists():
                            f(x.plus(d))

                pipeline(act, step, 2)

            def sparse_tensor(pe):
                pe.sem_inc(num_ready, DEPTH)

                pe.sem_inc(rB_ready, 1)
                pe.sem_inc(mB_ready, 1)

                def spread_columns(out, column):
                    for j in range(HEADS):
                        last = pe.matmul(out[:, j * P:(j + 1) * P], column[:, j:j + 1].to_broadcast([P, P]), ident[:],
                                         start=True, stop=True)
                    return last

                def sums(x):
                    pe.wait_ge(exp_ready, x.t + 1)
                    pe.wait_ge(rden_ready, x.t + 1)
                    for j in range(HEADS):
                        for k in range(CHUNKS):
                            last = pe.matmul(psD[:, j * SUM_COLS:(j + 1) * SUM_COLS], z[x.b % ZBUFS][:, k, j, :],
                                             ones[:, 0:SUM_COLS], start=(k == 0),
                                             stop=(k == CHUNKS - 1))
                    last.then_inc(den_ready, 1)

                def spread_inverse(x):
                    pe.wait_ge(rden_ready, x.t + 2)
                    pe.wait_ge(rdenb_ready, x.t + 1)
                    spread_columns(rB, rden).then_inc(rB_ready, 1)

                def transposed(x):
                    pe.wait_ge(top_ready, x.t + 1)
                    for j in range(HEADS):
                        last = pe.transpose(zT[:, j * P:(j + 1) * P], tree[:, j * P:(j + 1) * P], ident[:])
                    last.then_inc(topT_ready, 1)

                def spread(x):
                    pe.wait_ge(negm_ready, x.t + 1)
                    spread_columns(mB, negm).then_inc(mB_ready, 1)

                def products(x):
                    pe.wait_ge(mul_ready, x.t + 1)
                    pe.wait_ge(evac_heads, x.t + 1)
                    for k in range(CHUNKS):
                        last = pe.matmul(psN[x.b % 2][:, 0:HR], gt[x.b][:, k, 0:D],
                                         z[x.b % ZBUFS][:, k].rearrange("p i r -> p (i r)"),
                                         start=(k == 0), stop=(k == CHUNKS - 1))
                    last.then_inc(num_ready, 1)

                def support_products(x):
                    pe.wait_ge(az_ready, x.t + DEPTH + 1)
                    pe.wait_ge(evac_sum, x.t + 1)
                    for k in range(CHUNKS):
                        pe.matmul(psM[x.b % 2][:, 0:P], gt[x.b][:, k, 0:D], ga[x.b][:, k, :],
                                  start=(k == 0), stop=(k == CHUNKS - 1))

                def step(x):
                    for f, d in ((transposed, 0), (sums, -1), (spread, 0), (spread_inverse, -1),
                                 (support_products, 0), (products, -1)):
                        if x.plus(d).exists():
                            f(x.plus(d))

                pipeline(pe, step, 1)

            o = 0
            rglob = carve(ROWS)
            da, dz, dE, dB = carve(P), carve(HR), carve(HR), carve(4 * P)
            dt_ = carve(TW)
            doffs, dmsk, dsc = carve(P), carve(P), carve(6 * HEADS).rearrange("p (s i) -> p s i", i=HEADS)
            diota = carve(TILES)
            eT = [mB]

            HIGHEST, SUM, PRODUCT = range(3)
            PASSES = (HIGHEST, SUM, PRODUCT)
            LINKS = (6, 6, 7)
            dn = ("d_in", "d_z", "d_zT", "d_exp", "d_e", "d_eT", "d_mul", "d_num", "d_link")
            ds_ = {p: {n: sem4(f"{n}{p}") for n in dn} for p in PASSES}
            d_start, d_rden, d_tile, d_open, d_iota, d_evac, d_free = (sem4(n) for n in (
                "d_start", "d_rden", "d_tile", "d_open", "d_iota", "d_evac", "d_free"))
            d_pass = [sem4(f"d_pass{p}") for p in PASSES]

            def dense_sync(sp):
                with sp.Fori(0, TILES) as t:
                    for p in PASSES:
                        s = ds_[p]
                        with sp.Fori(0, TILES) as c:
                            sp.wait_ge(d_free, (t * len(PASSES) + p) * TILES + c + 1)
                            sp.dma_start(da, adj_chunks[bass.ds(c, 1), :, bass.ds(t * P, P)].rearrange(
                                "o p r -> p (o r)")).then_inc(s["d_in"], 16)
                            sp.dma_start(dt_, table.rearrange("(c p) w -> c p w", p=P)[bass.ds(c, 1), :, :].rearrange(
                                "o p w -> p (o w)")).then_inc(s["d_in"], 16)

            def dense_pool(pool):
                pool.iota(rglob, pattern=[[1, ROWS]], base=0, channel_multiplier=0,
                          allow_small_or_imprecise_dtypes=True).then_inc(d_iota, 1)
                pool.iota(diota, pattern=[[P, TILES]], base=0, channel_multiplier=1,
                          allow_small_or_imprecise_dtypes=True).then_inc(d_iota, 1)

            def dense_vector(dve):
                negc, negall, denc, denall, rdall = (dsc[:, k, :] for k in range(5))
                az = dB[:, HEADS * P:4 * P]
                dve.sem_inc(d_free, 1)
                dve.wait_ge(d_iota, 2)
                with dve.Fori(0, TILES) as t:
                    dve.wait_ge(d_evac, t + 1)
                    dve.memset(negall, 3.0e38)
                    dve.memset(denall, 0.0).then_inc(d_start, 1)
                    dve.wait_ge(d_start, t + 1)
                    dve.sem_inc(d_open, 1)
                    for p in PASSES:
                        s = ds_[p]
                        with dve.Fori(0, TILES) as c:
                            n = t * TILES + c
                            count = [0]

                            def link(ins):
                                count[0] += 1
                                ins.then_inc(s["d_link"], 1)
                                dve.wait_ge(s["d_link"], n * LINKS[p] + count[0])

                            dve.wait_ge(s["d_in"], n * 32 + 32)
                            link(dve.scalar_tensor_tensor(out=az, in0=rglob[:, bass.ds(t * P, P)],
                                                          scalar=diota[:, bass.ds(c, 1)], in1=da,
                                                          op0=ALU.not_equal, op1=ALU.mult))
                            link(dve.tensor_scalar(doffs, az, 0.0, NEG_INF, ALU.is_equal, ALU.mult))
                            for sign, e0 in ((ALU.is_lt, HEADS), (ALU.is_gt, 0)):
                                link(dve.tensor_scalar(dmsk, az, 0.0, None, sign))
                                for j in range(HEADS):
                                    src = doffs if e0 else dz[:, j * P:(j + 1) * P]
                                    last = dve.scalar_tensor_tensor(
                                        out=dz[:, j * P:(j + 1) * P], in0=dmsk, scalar=dt_[:, D + e0 + j:D + e0 + j + 1],
                                        in1=src, op0=ALU.mult, op1=ALU.add)
                                if e0:
                                    link(last)
                                else:
                                    last.then_inc(s["d_z"], 1)
                            dve.wait_ge(s["d_zT"], n + 1)
                            if p == HIGHEST:
                                link(dve.tensor_reduce(out=negc, in_=zT[:, 0:HEADS * P].rearrange(
                                    "p (i s) -> p i s", i=HEADS), axis=AX.X, op=ALU.max, negate=True))
                                dve.tensor_tensor(out=negall, in0=negall, in1=negc, op=ALU.min).then_inc(d_free, 1)
                            elif p == SUM:
                                dve.wait_ge(s["d_exp"], n + 1)
                                link(dve.tensor_copy(rdall, denall))
                                dve.tensor_tensor(out=denall, in0=rdall, in1=denc, op=ALU.add).then_inc(d_free, 1)
                            else:
                                dve.wait_ge(s["d_exp"], n + 1)
                                for j in range(HEADS):
                                    last = dve.tensor_scalar(dE[:, j * P:(j + 1) * P], dE[:, j * P:(j + 1) * P],
                                                             rdall[:, j:j + 1], None, ALU.mult)
                                link(last)
                                dve.sem_inc(s["d_e"], 1)
                                dve.wait_ge(s["d_eT"], n + 1)
                                link(dve.tensor_tensor(
                                    out=dB[:, 0:HEADS * P].rearrange("p (i r) -> p i r", i=HEADS),
                                    in0=eT[0][:, 0:HEADS * P].rearrange("p (i r) -> p i r", i=HEADS),
                                    in1=az.unsqueeze(1).to_broadcast([P, HEADS, P]), op=ALU.mult))
                                dve.sem_inc(s["d_mul"], 1)
                                dve.wait_ge(s["d_num"], n + 1)
                                dve.sem_inc(d_free, 1)
                            assert count[0] == LINKS[p], count
                        dve.wait_ge(d_free, (t * len(PASSES) + p) * TILES + TILES + 1)
                        if p == SUM:
                            dve.reciprocal(rdall, denall).then_inc(d_rden, 1)
                            dve.wait_ge(d_rden, t + 1)
                        dve.sem_inc(d_pass[p], 1)
                    dve.sem_inc(d_tile, 1)

            def dense_scalar(act):
                act.sem_inc(d_evac, 1)
                with act.Fori(0, TILES) as t:
                    act.wait_ge(d_pass[HIGHEST], t + 1)
                    for p in (SUM, PRODUCT):
                        s = ds_[p]
                        with act.Fori(0, TILES) as c:
                            n = t * TILES + c
                            act.wait_ge(s["d_zT"], n + 1)
                            for j in range(HEADS):
                                last = act.activation(dE[:, j * P:(j + 1) * P], zT[:, j * P:(j + 1) * P], ACT.Exp,
                                                      bias=dsc[:, 1, j:j + 1], accum_out=dsc[:, 2, j:j + 1])
                            last.then_inc(s["d_exp"], 1)
                    act.wait_ge(d_tile, t + 1)
                    act.copy(num[:, :, bass.ds(t * P, P)], psN[0][:].rearrange("p (q r) -> p q r", q=4)
                             ).then_inc(d_evac, 1)

            def dense_tensor(pe):
                with pe.Fori(0, TILES) as t:
                    pe.wait_ge(d_evac, t + 1)
                    pe.matmul(psN[0][:], zeros[:, 0:P], zeros[:], start=True, stop=False, skip_group_check=True)
                    for p in PASSES:
                        s = ds_[p]
                        with pe.Fori(0, TILES) as c:
                            n = t * TILES + c
                            pe.wait_ge(s["d_z"], n + 1)
                            for j in range(HEADS):
                                last = pe.transpose(zT[:, j * P:(j + 1) * P], dz[:, j * P:(j + 1) * P], ident[:])
                            last.then_inc(s["d_zT"], 1)
                            if p == PRODUCT:
                                pe.wait_ge(s["d_e"], n + 1)
                                for j in range(HEADS):
                                    last = pe.transpose(eT[0][:, j * P:(j + 1) * P], dE[:, j * P:(j + 1) * P], ident[:])
                                last.then_inc(s["d_eT"], 1)
                                pe.wait_ge(s["d_mul"], n + 1)
                                pe.matmul(psN[0][:], dt_[:, 0:D], dB, start=False, stop=False,
                                          skip_group_check=True).then_inc(s["d_num"], 1)

            with nc.Block() as block:
                def either(eng, dense, sparse):
                    crowded = eng.value_load(flag[0:1, 0:1], min_val=0, max_val=P)
                    with eng.If(crowded > 0):
                        if dense:
                            dense(eng)
                        else:
                            eng.nop()
                    with eng.Else():
                        if sparse:
                            sparse(eng)
                        else:
                            eng.nop()

                @block.sync
                def _(sp):
                    either(sp, dense_sync, None)

                @block.gpsimd
                def _(pool):
                    either(pool, dense_pool, sparse_pool)

                @block.vector
                def _(dve):
                    either(dve, dense_vector, sparse_vector)

                @block.scalar
                def _(act):
                    either(act, dense_scalar, sparse_scalar)

                @block.tensor
                def _(pe):
                    either(pe, dense_tensor, sparse_tensor)

        with ExitStack() as c5:
            def ps(name, shape, dt=F32):
                return c5.enter_context(nc.psum_tensor(name, shape, dt))

            def sem5(name):
                return c5.enter_context(nc.semaphore(name))

            gates = [[ps(f"gate{c}{g}", [P, 512]) for g in range(4)] for c in range(2)]
            buf = [work[:, k * GB:(k + 1) * GB] for k in range(12)]
            es = buf[0]
            rg, zg, ng, tg = buf[1:3], buf[3:5], buf[5:7], buf[7:9]
            sumT = num[:, HEADS, :]
            es_ps, es_ready, gate_ps, rz_ready, t_ready, n_ready, rz_ps = (
                sem5("es_ps"), sem5("es_ready"), sem5("gate_ps"), sem5("rz_ready"), sem5("t_ready"), sem5("n_ready"),
                sem5("rz_ps"))
            cell_done, dve_c, bias_c = sem5("cell_done"), sem5("dve_c5"), sem5("bias_c")
            with nc.Block() as block:
                @block.gpsimd
                def _(pool):
                    for used in done_with:
                        pool.sem_clear(used)

                @block.tensor
                def _(pe):
                    pe.sem_inc(gate_ps, 1)
                    with pe.Fori(0, GBLOCKS) as i:
                        cols = bass.ds(i * GB, GB)

                        def heads(cols):
                            for j in range(HEADS):
                                last = pe.matmul(gates[1][0][:, 0:GB], gatW_s[:, j, :], num[:, j, cols],
                                                 start=(j == 0), stop=(j == HEADS - 1))
                            last.then_inc(es_ps, 1)

                        pe.wait_ge(rz_ready, 2 * i + 1)
                        heads(cols)
                        for c in range(2):
                            pe.wait_ge(t_ready, 2 * i + c + 1)
                            if c:
                                pe.wait_ge(es_ready, i + 1)
                            inp = es if c else num[:, HEADS, cols]
                            wi, wh = gruw_s[:, 2 * c, :], gruw_s[:, 2 * c + 1, :]
                            for g in range(2):
                                pe.matmul(gates[c][g][:, 0:GB], wi[:, g * D:(g + 1) * D], inp, start=True, stop=False)
                                last = pe.matmul(gates[c][g][:, 0:GB], wh[:, g * D:(g + 1) * D], hT[:, cols],
                                                 start=False, stop=True)
                            last.then_inc(rz_ps, 1)
                            pe.matmul(gates[c][3][:, 0:GB], wh[:, 2 * D:3 * D], hT[:, cols], start=True, stop=True)
                            pe.matmul(gates[c][2][:, 0:GB], wi[:, 2 * D:3 * D], inp, start=True,
                                      stop=True).then_inc(gate_ps, 1)

                @block.scalar
                def _(act):
                    act.sem_inc(rz_ready, 1)
                    act.wait_ge(bias_c, 1)
                    with act.Fori(0, GBLOCKS) as i:
                        act.wait_ge(gate_ps, 2 * i + 1)
                        act.wait_ge(es_ps, i + 1)
                        act.mul(es, gates[1][0][:, 0:GB], 1.0 / HEADS).then_inc(es_ready, 1)
                        for c in range(2):
                            act.wait_ge(rz_ps, 2 * i + c + 1)
                            act.wait_ge(cell_done, 2 * i + c + 1)
                            act.activation(rg[c], gates[c][0][:, 0:GB], ACT.Sigmoid, bias=gbias[:, c, 0:1])
                            act.activation(zg[c], gates[c][1][:, 0:GB], ACT.Sigmoid,
                                           bias=gbias[:, c, 1:2]).then_inc(rz_ready, 1)
                            act.wait_ge(t_ready, 2 * i + c + 3)
                            act.activation(ng[c], tg[c], ACT.Tanh, bias=grub_s[:, 2 * c, 2:3]).then_inc(n_ready, 1)

                @block.vector
                def _(dve):
                    dve.tensor_tensor(out=gbias[:], in0=grub_s[:, 0:4:2, 0:2], in1=grub_s[:, 1:4:2, 0:2],
                                      op=ALU.add).then_inc(bias_c, 1)
                    dve.sem_inc(cell_done, 2)
                    dve.sem_inc(t_ready, 2)
                    ch = Chain(dve, dve_c)
                    with dve.Fori(0, GBLOCKS) as i:
                        ch.loop(i, 2 * 3 + 2)
                        cols = bass.ds(i * GB, GB)
                        for c in range(2):
                            dve.wait_ge(rz_ready, 2 * i + c + 2)
                            dve.wait_ge(gate_ps, 2 * i + c + 2)
                            ch.link(dve.scalar_tensor_tensor(out=tg[c], in0=gates[c][3][:, 0:GB],
                                                             scalar=grub_s[:, 2 * c + 1, 2:3], in1=rg[c], op0=ALU.add,
                                                             op1=ALU.mult))
                            dve.tensor_tensor(out=tg[c], in0=gates[c][2][:, 0:GB], in1=tg[c],
                                              op=ALU.add).then_inc(t_ready, 1)
                            dve.wait_ge(n_ready, 2 * i + c + 1)
                            ch.link(dve.tensor_tensor(out=rg[c], in0=hT[:, cols], in1=ng[c], op=ALU.subtract))
                            ch.link(dve.tensor_tensor(out=rg[c], in0=rg[c], in1=zg[c], op=ALU.mult))
                            if c == 0:
                                ch.link(dve.tensor_tensor(out=buf[9], in0=rg[c], in1=ng[c], op=ALU.add))
                                dve.sem_inc(cell_done, 1)
                            else:
                                ch.link(dve.tensor_tensor(out=rg[c], in0=rg[c], in1=ng[c], op=ALU.add))
                                dve.tensor_tensor(out=sumT[:, cols], in0=rg[c], in1=buf[9],
                                                  op=ALU.add).then_inc(cell_done, 1)
                        ch.done(GBLOCKS)

        xt = region[:, 0:ROWS].rearrange("p (t d) -> p t d", t=TILES)
        sent = [tab[:, :, 0:XW], region[:, ROWS:ROWS + TILES * XW].rearrange("p (t w) -> p t w", w=XW)]
        xn = sent[0][:, :, 0:D]
        filling = hT[:, 0:2 * SPARE * XW].rearrange("p (j w) -> p j w", w=XW)
        xtT = region[:, 3 * ROWS:4 * ROWS]
        small = work[:, ROWS:]
        logits = small[:, 0:TILES * EXPERTS].rearrange("p (t e) -> p t e", e=EXPERTS)
        best = small[:, 256:256 + TILES * 8].rearrange("p (t e) -> p t e", e=8)
        besti = small[:, 512:512 + TILES * 8].bitcast(U32).rearrange("p (t e) -> p t e", e=8)
        bestf = small[:, 768:768 + TILES * 2].rearrange("p (t e) -> p t e", e=2)
        w12 = small[:, 832:832 + 4 * TILES].rearrange("p (k t) -> p k t", k=4)
        eiota = small[:, 960:960 + TILES * EXPERTS].rearrange("p (t e) -> p t e", e=EXPERTS)
        gtf = gts[:].rearrange("p b k w -> p (b k w)")
        wt = gtf[:, 0:TILES * EXPERTS]
        wtv = wt.rearrange("p (t e) -> p t e", e=EXPERTS)
        wT8 = small[0:EXPERTS, 1472:1472 + ROWS]
        so = 1472 + ROWS

        def small_part(*shape):
            nonlocal so
            n = int(np.prod(shape))
            v = small[:, so:so + n]
            so += n
            assert ROWS + so <= WORK
            names = "abcd"[:len(shape)]
            return v.rearrange(f"p ({' '.join(names)}) -> p {' '.join(names)}",
                               **dict(zip(names, shape))) if len(shape) > 1 else v

        chosen = small_part(TOP, TILES, EXPERTS)
        chosen2 = small_part(TOP, TILES, EXPERTS)
        either_chosen = small_part(TILES, EXPERTS)
        earlier = small_part(P)
        scan = [small_part(SCAN + TILES, EXPERTS) for _ in range(2)]
        place = small_part(TILES, EXPERTS)
        slot_f = small_part(TOP, TILES)
        slot_i = small_part(TOP * TILES).bitcast(U32)
        first_slot = small_part(EXPERTS)
        fill_first = small_part(EXPERTS)
        fill_f = small_part(EXPERTS)
        fill_i = small_part(EXPERTS).bitcast(U32)
        block_first = small_part(EXPERTS, BLOCKS_E)
        block_used = small_part(EXPERTS, BLOCKS_E)
        ends = [small_part(4 + EXPERTS) for _ in range(2)]
        unused = small_part(EXPERTS)
        next_slot = [small_part(EXPERTS) for _ in range(3)]
        total = small_part(EXPERTS)
        step_no = small_part(STEPS, EXPERTS)
        past = small_part(STEPS, EXPERTS)
        past_unused = small_part(STEPS, EXPERTS)
        step_f = small_part(2, STEPS)
        plan_end = so
        with ExitStack() as c6:
            def ps(name, shape, dt=F32):
                return c6.enter_context(nc.psum_tensor(name, shape, dt))

            def sem6(name):
                return c6.enter_context(nc.semaphore(name))

            psT = [ps(f"psR{k}", [P, 512]) for k in range(2)]
            psL = ps("psL", [P, TILES, EXPERTS])
            psQ = ps("psQ", [P, 512])
            TE = TILES * EXPERTS
            psC = psQ[:, 0:2 * TE].rearrange("p (k t e) -> p k t e", k=2, e=EXPERTS)
            psW = [ps(f"psW{k}", [P, 512]) for k in range(2)]
            psZ = [ps(f"psZ{k}", [P, 512]) for k in range(2)]
            ROUTED = [(0, 8), (8, 9), (17, TILES - 17)]
            groups = [(t, min(4, t1 + m - t)) for t1, m in ROUTED for t in range(t1, t1 + m, 4)]
            NG = len(groups)
            of_part = [[g for g, (t, _) in enumerate(groups) if t1 <= t < t1 + m] for t1, m in ROUTED]
            (sum_T, x_done, dve_c, vared, stdev, xt_ready, xn_ready, tr, tr_copied, log_ps, weighed, dif, wt_ready,
             wT_ps, wT_ready, bz_ps, eio, xn_copied, chosen_ready, place_ps, slots_ready, fill_ready,
             sent_done, spare_ready, spare_sent) = (sem6(n) for n in (
                 "sum_T", "x_done", "dve_c6", "vared6", "stdev6", "xt_ready", "xn_ready", "tr6", "tr_copied",
                 "log_ps", "weighed", "dif", "wt_ready", "wT_ps", "wT_ready", "bz_ps", "eio",
                 "xn_copied", "chosen_ready", "place_ps", "slots_ready", "fill_ready", "sent_done",
                 "spare_ready", "spare_sent"))
            with nc.Block() as block:
                @block.sync
                def _(sp):
                    sp.wait_ge(spare_ready, 3)
                    sp.dma_start(slot_blocks[EXPERTS * BLOCKS_E:BLOCKS, :, :].rearrange("b p w -> p b w"),
                                 filling[:, SPARE:2 * SPARE, :]).then_inc(spare_sent, 16)
                    sp.wait_ge(fill_ready, 1)
                    for e in range(EXPERTS):
                        first = sp.value_load(fill_i[0:1, e:e + 1].bitcast(I32), min_val=0,
                                              max_val=(EXPERTS * BLOCKS_E - 1) * P)
                        sp.dma_start(slots[bass.ds(first, P), :], filling[:, e, :]).then_inc(spare_sent, 16)
                    sp.wait_ge(spare_sent, 16 * (EXPERTS + 1))

                @block.gpsimd
                def _(pool):
                    def iota(out, pattern, base, channel, sem):
                        pool.iota(out, pattern=pattern, base=base, channel_multiplier=channel,
                                  allow_small_or_imprecise_dtypes=True).then_inc(sem, 1)

                    iota(eiota, [[0, TILES], [1, EXPERTS]], 0, 0, eio)
                    iota(first_slot, [[BLOCKS_E * P, EXPERTS]], 0, 0, eio)
                    iota(fill_first, [[BLOCKS_E * P, EXPERTS]], 0, 1, eio)
                    iota(block_first, [[0, EXPERTS], [P, BLOCKS_E]], 0, 0, eio)
                    iota(step_no, [[1, STEPS], [0, EXPERTS]], 0, 0, eio)
                    for v in scan:
                        pool.memset(v[:, 0:SCAN, :], 0.0).then_inc(eio, 1)
                    for v in ends:
                        pool.memset(v[:, 0:4], 0.0).then_inc(eio, 1)
                    pool.wait_ge(eio, 9)
                    pool.tensor_scalar(earlier, coliota[:], fill_first[:, 0:1], None, ALU.is_gt).then_inc(eio, 1)
                    pool.memset(filling[:, :, 0:D], 0.0).then_inc(spare_ready, 1)
                    pool.memset(filling[:, :, D + 1:XW], 0.0).then_inc(spare_ready, 1)
                    iota(filling[:, :, D:D + 1].bitcast(I32), [[P, 2 * SPARE], [0, 1]], TOP * ROWS, 1, spare_ready)
                    for k in range(TOP):
                        iota(sent[k][:, :, D:D + 1].bitcast(I32), [[1, TILES], [0, 1]], k * ROWS, TILES, eio)
                    for q, (t0, m) in enumerate(ROUTED):
                        pool.wait_ge(xn_copied, q + 1)
                        pool.wait_ge(slots_ready, q + 1)
                        for t in range(t0, t0 + m):
                            for k in range(TOP):
                                pool.indirect_dma_start(
                                    out=slots, out_offset=bass.IndirectOffsetOnAxis(
                                        ap=slot_i[:, k * TILES + t:k * TILES + t + 1], axis=0),
                                    in_=sent[k][:, t, :], in_offset=None).then_inc(sent_done, 16)
                    pool.wait_ge(sent_done, 16 * TOP * TILES)

                @block.tensor
                def _(pe):
                    def node_major(gs):
                        for g in gs:
                            t0, n = groups[g]
                            if g >= 2:
                                pe.wait_ge(x_done, g - 1)
                            for t in range(n):
                                last = pe.transpose(psT[g % 2][:, t * P:(t + 1) * P],
                                                    sumT[:, (t0 + t) * P:(t0 + t + 1) * P], ident[:])
                            last.then_inc(sum_T, 1)

                    def router(q):
                        for g in of_part[q]:
                            t0, n = groups[g]
                            pe.wait_ge(xt_ready, g + 1)
                            if g >= 2:
                                pe.wait_ge(tr_copied, g - 1)
                            for t in range(n):
                                last = pe.transpose(psW[g % 2][:, t * P:(t + 1) * P], xt[:, t0 + t, :], ident[:])
                            last.then_inc(tr, 1)
                        for g in of_part[q]:
                            t0, n = groups[g]
                            pe.wait_ge(tr_copied, g + 1)
                            for t in range(t0, t0 + n):
                                last = pe.matmul(psL[:, t, :], xtT[:, t * P:(t + 1) * P], Wr_s[:], start=True,
                                                 stop=True)
                        last.then_inc(log_ps, 1)

                    def places(q):
                        t0, m = ROUTED[q]
                        pe.wait_ge(chosen_ready, q + 1)
                        for k, w in enumerate((earlier, ones[:])):
                            o = k * TE + t0 * EXPERTS
                            last = pe.matmul(psQ[:, o:o + m * EXPERTS], w, either_chosen[:, t0:t0 + m, :].rearrange(
                                "p t e -> p (t e)"), start=True, stop=True)
                        last.then_inc(place_ps, 1)

                    node_major(of_part[0])
                    for q in range(len(ROUTED)):
                        router(q)
                        ahead = of_part[q + 1] if q + 1 < len(ROUTED) else []
                        node_major(ahead[0:2])
                        places(q)
                        node_major(ahead[2:])
                    pe.wait_ge(wt_ready, len(ROUTED))
                    for g, (t0, n) in enumerate(groups):
                        if g >= 2:
                            pe.wait_ge(wT_ready, g - 1)
                        for t in range(n):
                            last = pe.transpose(psW[g % 2][0:EXPERTS, t * P:(t + 1) * P], wtv[:, t0 + t, :], ident[:])
                        last.then_inc(wT_ps, 1)
                    for g, (t0, n) in enumerate(groups):
                        pe.wait_ge(wT_ready, g + 1)
                        if g >= 2:
                            pe.wait_ge(x_done, NG + g - 1)
                        for t in range(n):
                            last = pe.matmul(psZ[g % 2][:, t * P:(t + 1) * P], wT8[:, (t0 + t) * P:(t0 + t + 1) * P],
                                             b2_s[:], start=True, stop=True)
                        last.then_inc(bz_ps, 1)

                @block.scalar
                def _(act):
                    for q, (t0, m) in enumerate(ROUTED):
                        part = slice(t0, t0 + m)
                        act.wait_ge(vared, 2 * q + 1)
                        act.activation(stat[:, 4, part], stat[:, 3, part], ACT.Sqrt).then_inc(stdev, 1)
                        for g in of_part[q]:
                            t, n = groups[g]
                            act.wait_ge(tr, g + 1)
                            act.copy(xtT[:, t * P:(t + n) * P], psW[g % 2][:, 0:n * P]).then_inc(tr_copied, 1)
                        act.wait_ge(vared, 2 * q + 2)
                        act.activation(stat[:, 1, part], stat[:, 0, part], ACT.Sqrt).then_inc(stdev, 1)
                        act.wait_ge(xn_ready, q + 1)
                        act.copy(sent[1][:, part, 0:D], sent[0][:, part, 0:D]).then_inc(xn_copied, 1)
                        act.wait_ge(dif, q + 1)
                        for k in range(TOP):
                            act.activation(sent[k][:, part, D + 1], w12[:, 0, part], ACT.Sigmoid,
                                           scale=(-1.0, 1.0)[k]).then_inc(weighed, 1)
                    for g, (t0, n) in enumerate(groups):
                        act.wait_ge(wT_ps, g + 1)
                        act.copy(wT8[:, t0 * P:(t0 + n) * P], psW[g % 2][0:EXPERTS, 0:n * P]).then_inc(wT_ready, 1)

                @block.vector
                def _(dve):
                    ch = Chain(dve, dve_c)
                    carried = first_slot
                    for q, (t0, m) in enumerate(ROUTED):
                        part = slice(t0, t0 + m)
                        wide = [P, m, EXPERTS]
                        for g in of_part[q]:
                            t1, n = groups[g]
                            dve.wait_ge(sum_T, g + 1)
                            for t in range(n):
                                last = dve.scalar_tensor_tensor(
                                    out=xs[:, t1 + t, :], in0=psT[g % 2][:, t * P:(t + 1) * P],
                                    scalar=dg[:, t1 + t:t1 + t + 1], in1=xs[:, t1 + t, :], op0=ALU.mult, op1=ALU.add)
                            last.then_inc(x_done, 1)
                            dve.wait_ge(x_done, g + 1)
                            for t in range(t1, t1 + n):
                                last = dve.bn_stats(out=moments[:, t, :], in_=xs[:, t, :])
                            ch.link(last)
                            for t in range(t1, t1 + n):
                                last = dve.bn_aggr(out=meanvar[:, t, :], in_=moments[:, t, :])
                        ch.link(last)
                        dve.tensor_scalar(stat[:, 3, part], meanvar[:, part, 1], EPS, None, ALU.add).then_inc(vared, 1)
                        dve.wait_ge(stdev, 2 * q + 1)
                        ch.link(dve.reciprocal(stat[:, 5, part], stat[:, 4, part]))
                        for g in of_part[q]:
                            t1, n = groups[g]
                            for t in range(t1, t1 + n):
                                last = dve.tensor_scalar(xt[:, t, :], xs[:, t, :], meanvar[:, t, 0:1],
                                                         stat[:, 5, t:t + 1], ALU.subtract, ALU.mult)
                            last.then_inc(xt_ready, 1)
                        dve.wait_ge(xt_ready, of_part[q][-1] + 1)
                        for t in range(t0, t0 + m):
                            last = dve.bn_stats(out=moments[:, t, :], in_=xt[:, t, :])
                        ch.link(last)
                        for t in range(t0, t0 + m):
                            last = dve.bn_aggr(out=meanvar[:, t, :], in_=moments[:, t, :])
                        ch.link(last)
                        dve.tensor_scalar(stat[:, 0, part], meanvar[:, part, 1], EPS, None, ALU.add).then_inc(vared, 1)
                        dve.wait_ge(stdev, 2 * q + 2)
                        ch.link(dve.reciprocal(stat[:, 2, part], stat[:, 1, part]))
                        for t in range(t0, t0 + m):
                            last = dve.tensor_scalar(sent[0][:, t, 0:D], xt[:, t, :], meanvar[:, t, 0:1],
                                                     stat[:, 2, t:t + 1], ALU.subtract, ALU.mult)
                        last.then_inc(xn_ready, 1)
                        dve.wait_ge(eio, 12)
                        dve.wait_ge(log_ps, q + 1)
                        ch.link(dve.tensor_tensor(out=logits[:, part, :], in0=psL[:, part, :],
                                                  in1=br_s[:].unsqueeze(1).to_broadcast(wide), op=ALU.add))
                        for t in range(t0, t0 + m):
                            last = dve.max(out=best[:, t, :], in_=logits[:, t, :])
                        ch.link(last)
                        dve.tensor_tensor(out=w12[:, 0, part].unsqueeze(2), in0=best[:, part, 1:2],
                                          in1=best[:, part, 0:1], op=ALU.subtract).then_inc(dif, 1)
                        for t in range(t0, t0 + m):
                            last = dve.max_index(out=besti[:, t, :], in_max=best[:, t, :], in_values=logits[:, t, :])
                        ch.link(last)
                        ch.link(dve.tensor_copy(bestf[:, part, :], besti[:, part, 0:2]))
                        for k in range(TOP):
                            last = dve.tensor_tensor(out=chosen[:, k, part, :], in0=eiota[:, part, :],
                                                     in1=bestf[:, part, k:k + 1].to_broadcast(wide), op=ALU.is_equal)
                        ch.link(last)
                        dve.tensor_tensor(out=either_chosen[:, part, :], in0=chosen[:, 0, part, :],
                                          in1=chosen[:, 1, part, :], op=ALU.add).then_inc(chosen_ready, 1)
                        dve.wait_ge(weighed, TOP * q + TOP)
                        for k in range(TOP):
                            last = dve.tensor_tensor(out=chosen2[:, k, part, :], in0=chosen[:, k, part, :],
                                                     in1=sent[k][:, part, D + 1:XW].to_broadcast(wide), op=ALU.mult)
                        ch.link(last)
                        dve.tensor_tensor(out=wtv[:, part, :], in0=chosen2[:, 0, part, :],
                                          in1=chosen2[:, 1, part, :], op=ALU.add).then_inc(wt_ready, 1)
                        dve.wait_ge(place_ps, q + 1)
                        dve.wait_ge(wt_ready, q + 1)
                        src, dst = scan
                        ch.link(dve.tensor_copy(src[:, SCAN:SCAN + m, :], psC[:, 1, part, :]))
                        for d in (1, 2, 4, 8):
                            ch.link(dve.tensor_tensor(out=dst[:, SCAN:SCAN + m, :], in0=src[:, SCAN:SCAN + m, :],
                                                      in1=src[:, SCAN - d:SCAN - d + m, :], op=ALU.add))
                            src, dst = dst, src
                        ch.link(dve.tensor_tensor(out=place[:, part, :], in0=psC[:, 0, part, :],
                                                  in1=src[:, SCAN - 1:SCAN - 1 + m, :], op=ALU.add))
                        ch.link(dve.tensor_tensor(out=place[:, part, :], in0=place[:, part, :],
                                                  in1=carried.unsqueeze(1).to_broadcast(wide), op=ALU.add))
                        for k in range(TOP):
                            last = dve.tensor_tensor(out=chosen2[:, k, part, :], in0=chosen[:, k, part, :],
                                                     in1=place[:, part, :], op=ALU.mult)
                        ch.link(last)
                        ch.link(dve.tensor_reduce(out=slot_f[:, :, part], in_=chosen2[:, :, part, :], axis=AX.X,
                                                  op=ALU.add))
                        dve.tensor_copy(slot_i.rearrange("p (k t) -> p k t", k=TOP)[:, :, part],
                                        slot_f[:, :, part]).then_inc(slots_ready, 1)
                        ch.link(dve.tensor_tensor(out=next_slot[q], in0=src[:, SCAN + m - 1, :], in1=carried,
                                                  op=ALU.add))
                        carried = next_slot[q]
                    ch.link(dve.tensor_tensor(out=total, in0=carried, in1=first_slot, op=ALU.subtract))
                    ch.link(dve.tensor_tensor(out=fill_f, in0=fill_first, in1=total, op=ALU.add))
                    dve.tensor_copy(fill_i, fill_f).then_inc(fill_ready, 1)
                    ch.link(dve.tensor_tensor(out=block_used, in0=block_first, in1=total.unsqueeze(2).to_broadcast(
                        [P, EXPERTS, BLOCKS_E]), op=ALU.is_lt))
                    ch.link(dve.tensor_reduce(out=ends[0][:, 4:], in_=block_used, axis=AX.X, op=ALU.add))
                    ch.link(dve.tensor_scalar(unused, ends[0][:, 4:], -1.0, float(BLOCKS_E), ALU.mult, ALU.add))
                    src, dst = ends
                    for d in (1, 2, 4):
                        ch.link(dve.tensor_tensor(out=dst[:, 4:], in0=src[:, 4:], in1=src[:, 4 - d:4 - d + EXPERTS],
                                                  op=ALU.add))
                        src, dst = dst, src
                    ch.link(dve.tensor_tensor(out=past, in0=step_no, in1=src[:, 4:].unsqueeze(1).to_broadcast(
                        [P, STEPS, EXPERTS]), op=ALU.is_ge))
                    ch.link(dve.tensor_tensor(out=past_unused, in0=past, in1=unused.unsqueeze(1).to_broadcast(
                        [P, STEPS, EXPERTS]), op=ALU.mult))
                    ch.link(dve.tensor_reduce(out=step_f[:, 0, :], in_=past, axis=AX.X, op=ALU.add))
                    ch.link(dve.tensor_reduce(out=step_f[:, 1, :], in_=past_unused, axis=AX.X, op=ALU.add))
                    dve.tensor_scalar(plan[0:1, 0, :], step_f[0:1, 0, :], float(EXPERTS - 1), None, ALU.min)
                    dve.tensor_tensor(out=plan[0:1, 1, :], in0=step_f[0:1, 1, :], in1=step_no[0:1, :, 0], op=ALU.add)
                    for g, (t0, n) in enumerate(groups):
                        dve.wait_ge(bz_ps, g + 1)
                        dve.tensor_tensor(out=xs[:, t0:t0 + n, :], in0=psZ[g % 2][:, 0:n * P].rearrange(
                            "p (t d) -> p t d", t=n), in1=xs[:, t0:t0 + n, :], op=ALU.add).then_inc(x_done, 1)

        with ExitStack() as c7:
            def ps(name, shape, dt=F32):
                return c7.enter_context(nc.psum_tensor(name, shape, dt))

            def sem7(name):
                return c7.enter_context(nc.semaphore(name))

            o = 0

            def part(n):
                nonlocal o
                o += n
                assert o <= WORK
                return work[:, o - n:o]

            psX = [ps(f"psX{k}", [P, 512]) for k in range(2)]
            psH = [ps(f"psH{k}", [P, 512]) for k in range(2)]
            psY = [ps(f"psY{k}", [P, 512]) for k in range(2)]
            xl = [part(XW) for _ in range(XBUFS)]
            xT = [part(P) for _ in range(2)]
            w1c = [part(HID) for _ in range(WBUFS)]
            w2c = [part(HC * D).rearrange("p (c d) -> p c d", c=HC) for _ in range(WBUFS)]
            b1c = [part(HC) for _ in range(WBUFS)]
            act_h = [part(HC * P).rearrange("p (c n) -> p c n", c=HC) for _ in range(2)]
            ysc = [part(D) for _ in range(XBUFS)]
            T_ps, xT_ready, w_ready, h_ps, h_ready, y_ps, y_scaled, y_seen = (
                sem7(n) for n in ("T_ps7", "xT_ready7", "w_ready7", "h_ps7", "h_ready7", "y_ps7", "y_scaled7",
                                  "y_seen7"))
            x_in = [sem7(f"slots_in{b}") for b in range(XBUFS)]
            GT = 7
            back = [(t, min(GT, TILES - t)) for t in range(0, TILES, GT)]
            y_in = [sem7(f"y_in{g}") for g in range(len(back))]
            added, stored = sem7("added7"), sem7("stored7")
            yb = [region[:, k * ROWS:(k + 1) * ROWS].rearrange("p (t d) -> p t d", d=D) for k in range(TOP)]
            assert STEPS % XBUFS == 0
            TURNS7 = STEPS // XBUFS - 1
            FIRST = 3

            def steps(eng, step):
                for s in range(-1, FIRST):
                    step(s, s, 0)
                with eng.Fori(0, TURNS7) as i:
                    for n in range(FIRST, FIRST + XBUFS):
                        step(i * XBUFS + n, n, i)
                for s in range(FIRST + TURNS7 * XBUFS, STEPS + 1):
                    step(s, s, 0)

            def there(s):
                return not isinstance(s, int) or 0 <= s < STEPS

            def above(eng, sem, count):
                if not isinstance(count, int) or count > 0:
                    eng.wait_ge(sem, count)

            with nc.Block() as block:
                @block.sync
                def _(sp):
                    def load(s, b):
                        no = sp.value_load(plan[0:1, 1, s:s + 1] if isinstance(s, int) else
                                           plan[0:1, 1, bass.ds(s, 1)], min_val=0, max_val=BLOCKS - 1)
                        sp.dma_start(xl[b], slot_blocks[bass.ds(no, 1), :, :].rearrange("o p w -> p (o w)")
                                     ).then_inc(x_in[b], 16)

                    for b in range(XBUFS):
                        load(b, b)
                    with sp.Fori(0, STEPS // XBUFS - 1) as i:
                        for b in range(XBUFS):
                            sp.wait_ge(y_out[b], i * 16 + 16)
                            sp.sem_inc(y_seen, 1)
                            load((i + 1) * XBUFS + b, b)
                    for b in range(XBUFS):
                        sp.wait_ge(y_out[b], 16 * (STEPS // XBUFS))
                    for g, (t0, n) in enumerate(back):
                        for k in range(TOP):
                            sp.dma_start(yb[k][:, t0:t0 + n, :], expert_out[k * ROWS:(k + 1) * ROWS, :].rearrange(
                                "(p t) d -> p t d", t=TILES)[:, t0:t0 + n, :]).then_inc(y_in[g], 16)
                    for g, (t0, n) in enumerate(back):
                        sp.wait_ge(added, TOP * (g + 1))
                        full = min(t0 + n, NODES // P)
                        sp.dma_start(out[t0 * P:full * P, :].rearrange("(t p) d -> p t d", p=P),
                                     xs[:, t0:full, :]).then_inc(stored, 16)
                    sp.dma_start(out[full * P:NODES, :], xs[0:NODES - full * P, full, :]).then_inc(stored, 16)
                    sp.wait_ge(stored, 16 * (len(back) + 1))

                @block.gpsimd
                def _(pool):
                    with pool.Fori(0, STEPS // XBUFS) as i:
                        for b in range(XBUFS):
                            pool.wait_ge(y_scaled, i * XBUFS + b + 1)
                            pool.sem_inc(y_seen, 1)
                            pool.indirect_dma_start(
                                out=expert_out, out_offset=bass.IndirectOffsetOnAxis(
                                    ap=xl[b][:, D:D + 1].bitcast(U32), axis=0),
                                in_=ysc[b], in_offset=None).then_inc(y_out[b], 16)

                @block.tensor
                def _(pe):
                    def step(s, n, turn):
                        if there(s + 1):
                            b = (n + 1) % XBUFS
                            pe.wait_ge(x_in[b], (turn + (n + 1) // XBUFS) * 16 + 16)
                            above(pe, xT_ready, s)
                            pe.transpose(psX[(n + 1) % 2][:, 0:P], xl[b][:, 0:D], ident[:]).then_inc(T_ps, 1)
                        if there(s):
                            pe.wait_ge(w_ready, s * 3 + 3)
                            pe.wait_ge(xT_ready, s + 1)
                            above(pe, h_ready, s - 1)
                            for c in range(HC):
                                last = pe.matmul(psH[n % 2][:, c * P:(c + 1) * P],
                                                 w1c[n % WBUFS][:, c * P:(c + 1) * P], xT[n % 2],
                                                 start=True, stop=True)
                            last.then_inc(h_ps, 1)
                        if there(s - 1):
                            m = n - 1
                            pe.wait_ge(h_ready, s)
                            above(pe, y_scaled, s - 2)
                            for c in range(HC):
                                last = pe.matmul(psY[m % 2][:, 0:D], act_h[m % 2][:, c, :], w2c[m % WBUFS][:, c, :],
                                                 start=(c == 0), stop=(c == HC - 1))
                            last.then_inc(y_ps, 1)

                    steps(pe, step)

                @block.scalar
                def _(act):
                    def step(s, n, turn):
                        if there(s):
                            above(act, y_ps, s - 1)
                            act.wait_ge(h_ps, s + 1)
                            for c in range(HC):
                                last = act.activation(act_h[n % 2][:, c, :], psH[n % 2][:, c * P:(c + 1) * P],
                                                      ACT.Gelu, bias=b1c[n % WBUFS][:, c:c + 1])
                            last.then_inc(h_ready, 1)

                    steps(act, step)

                @block.vector
                def _(dve):
                    def step(s, n, turn):
                        if there(s + 1):
                            no = dve.value_load(plan[0:1, 0, s + 1:s + 2] if isinstance(s, int) else
                                                plan[0:1, 0, bass.ds(s + 1, 1)], min_val=0, max_val=EXPERTS - 1)
                            w = (n + 1) % WBUFS
                            above(dve, y_ps, s - 1)
                            dve.tensor_copy(w1c[w].unsqueeze(1), W1_s[:, bass.ds(no, 1), :]).then_inc(w_ready, 1)
                            dve.tensor_copy(w2c[w], W2_s[:, bass.ds(no * HC, HC), :]).then_inc(w_ready, 1)
                            dve.tensor_copy(b1c[w], b1g[:, bass.ds(no * HC, HC)]).then_inc(w_ready, 1)
                            dve.wait_ge(T_ps, s + 2)
                            above(dve, h_ps, s)
                            dve.tensor_copy(xT[(n + 1) % 2], psX[(n + 1) % 2][:, 0:P]).then_inc(xT_ready, 1)
                        if there(s - 1):
                            b = (n - 1) % XBUFS
                            dve.wait_ge(y_ps, s)
                            dve.tensor_scalar(ysc[b], psY[(n - 1) % 2][:, 0:D], xl[b][:, D + 1:XW], None,
                                              ALU.mult).then_inc(y_scaled, 1)

                    steps(dve, step)
                    for g, (t0, n) in enumerate(back):
                        dve.wait_ge(y_in[g], 32)
                        for k in range(TOP):
                            if k:
                                dve.wait_ge(added, TOP * g + k)
                            dve.tensor_tensor(out=xs[:, t0:t0 + n, :], in0=xs[:, t0:t0 + n, :],
                                              in1=yb[k][:, t0:t0 + n, :], op=ALU.add).then_inc(added, 1)


def kernel(**inputs):
    import numpy as np
    import concourse.bacc as _bacc
    from concourse import mybir as _mybir
    from concourse.bass_utils import run_bass_kernel_spmd as _run

    src = {k: np.asarray(v) for k, v in inputs.items()}
    adj = src["adj"]
    adjT = np.zeros((ROWS, ROWS), adj.dtype)
    adjT[:NODES, :NODES] = adj.T
    x = np.zeros((ROWS, D), src["x"].dtype)
    x[:NODES] = src["x"]
    dg = np.zeros(ROWS, adj.dtype)
    dg[:NODES] = np.diagonal(adj)
    g = {k[len("L0_gnn_"):]: v for k, v in src.items() if k.startswith("L0_gnn_")}
    f = {k[len("L0_ffn_"):]: v for k, v in src.items() if k.startswith("L0_ffn_")}
    gru = [g[n] for n in ("edge_Wih", "edge_Whh", "node_Wih", "node_Whh")]
    bias = [g[n] for n in ("edge_bih", "edge_bhh", "node_bih", "node_bhh")]
    laid = {
        "x": x, "adjT": adjT, "diag": dg.reshape(TILES, P).T,
        "gatW": g["gat_W"].transpose(1, 0, 2), "gatWT": g["gat_W"].transpose(2, 0, 1),
        "gata": g["gat_a"].reshape(HEADS, 2, D).transpose(2, 0, 1),
        "gruw": np.stack([w.T for w in gru], axis=1),
        "grub": np.stack([b.reshape(3, D).T for b in bias], axis=1),
        "Wr": f["Wr"], "br": f["br"], "lng": f["ln_g"].T, "lnb": f["ln_b"].T,
        "W1": f["W1"].transpose(1, 0, 2), "b1": f["b1"].reshape(EXPERTS, HC, P).transpose(2, 0, 1),
        "W2": f["W2"].reshape(EXPERTS * HC, P, D).transpose(1, 0, 2), "b2": f["b2"],
    }
    nc = _bacc.Bacc("TRN2", target_bir_lowering=False, num_devices=1)
    arrays, args = {}, []
    for name, a in laid.items():
        a = np.ascontiguousarray(a)
        arrays[f"in_{name}"] = a
        args.append(nc.dram_tensor(f"in_{name}", a.shape, _mybir.dt.from_np(a.dtype), kind="ExternalInput").ap())
    args.append(nc.dram_tensor("out_0", (NODES, D), _mybir.dt.float32, kind="ExternalOutput").ap())
    gnn_moe(nc, *args)
    r = _run(nc, [arrays], core_ids=[0])
    return r.results[0]["out_0"]
```
